# Optimizing a Trainium2 kernel written in Bass

```python
import numpy as np
import jax
import jax.numpy as jnp

def _softmax(x, axis=-1):
    return jax.nn.softmax(x, axis=axis)

def _gelu(x):
    return jax.nn.gelu(x, approximate=True)

def _silu(x):
    return jax.nn.silu(x)

def _sigmoid(x):
    return jax.nn.sigmoid(x)

def _layernorm(x, axis=-1, eps=1e-05):
    m = jnp.mean(x, axis=axis, keepdims=True)
    v = jnp.var(x, axis=axis, keepdims=True)
    return (x - m) / jnp.sqrt(v + eps)

def _scatter_add(tgt, idx, src, axis=0):
    return tgt.at[idx].add(src)

def _segment_sum(src, seg, n):
    return jax.ops.segment_sum(src, seg, n)
kernel_name = 'mk_flamingo_gated_d1_seqx_r4_ed549a'

def setup_inputs(seed: int=0):
    np.random.seed(seed)
    _w = jnp.asarray

    def _rec_inputs():
        import jax
        import jax.numpy as jnp
        _rk = jax.random.key(seed)
        x = 6.313e-05 + 0.9998 * jax.random.normal(jax.random.fold_in(_rk, 1), (4, 512, 256), jnp.float32)
        _lenS = 512 - jax.random.randint(jax.random.fold_in(_rk, 7), (4,), 0, max(1, 512 // 4) + 1, jnp.int32)
        _lenS2 = 512 - jax.random.randint(jax.random.fold_in(_rk, 8), (4,), 0, max(1, 512 // 4) + 1, jnp.int32)
        _ctx_1024P = jax.random.normal(jax.random.fold_in(_rk, 11), (4, 16, 256), jnp.float32)
        _ctx_1024c = jax.random.dirichlet(jax.random.fold_in(_rk, 511), 0.3 * jnp.ones((16,), jnp.float32), (4, 512))
        _ctx_1024t = jnp.einsum('bsk,bkd->bsd', _ctx_1024c, _ctx_1024P)
        _ctx_1024t = _ctx_1024t * jax.lax.rsqrt(jnp.mean(jnp.square(_ctx_1024t)) + 1e-12) * 0.953939
        ctx_1024 = -0.000214406 + 1.00034 * (_ctx_1024t + 0.3 * jax.random.normal(jax.random.fold_in(_rk, 611), (4, 512, 256), jnp.float32))
        _g = jax.random.normal(jax.random.fold_in(_rk, 9001), (2, 1), jnp.float32)
        _g = jnp.sign(_g) * jnp.maximum(jnp.abs(_g), 1.0) + (_g == 0) * 1.0
        g_xattn = _g[0]
        g_ffn = _g[1]
        return (x, ctx_1024, g_xattn, g_ffn)
    x, ctx_1024, g_xattn, g_ffn = _rec_inputs()

    def _L0_xattn_setup():
        import jax, jax.numpy as jnp
        import numpy as np
        from jax import lax
        BIG = jnp.float32(1e+30)

        def _pairwise_euclidean(a, b):
            aa = jnp.sum(a * a, axis=-1)[:, None]
            bb = jnp.sum(b * b, axis=-1)[None, :]
            ab = a @ b.T
            return jnp.sqrt(jnp.maximum(aa + bb - 2.0 * ab, 0.0))

        def _dtw_cost(D):
            row0 = jnp.cumsum(D[0])

            def row_step(prev_row, d_row):
                first = d_row[0] + prev_row[0]

                def col_step(left, inp):
                    d_ij, up, diag = inp
                    r = d_ij + jnp.minimum(jnp.minimum(up, left), diag)
                    return (r, r)
                _, rest = lax.scan(col_step, first, (d_row[1:], prev_row[1:], prev_row[:-1]))
                row = jnp.concatenate([first[None], rest])
                return (row, row)
            _, rows = lax.scan(row_step, row0, D[1:])
            return jnp.concatenate([row0[None], rows], axis=0)

        def _backtrack(R, T1, T2):
            L = T1 + T2 - 1

            def step(carry, _):
                i, j, done = carry
                valid = jnp.logical_not(done)
                cd = jnp.where((i > 0) & (j > 0), R[jnp.maximum(i - 1, 0), jnp.maximum(j - 1, 0)], BIG)
                cu = jnp.where(i > 0, R[jnp.maximum(i - 1, 0), j], BIG)
                cl = jnp.where(j > 0, R[i, jnp.maximum(j - 1, 0)], BIG)
                choice = jnp.argmin(jnp.stack([cd, cu, cl]))
                ni = jnp.where(choice <= 1, i - 1, i)
                nj = jnp.where((choice == 0) | (choice == 2), j - 1, j)
                at_origin = (i == 0) & (j == 0)
                ni = jnp.where(at_origin, 0, ni)
                nj = jnp.where(at_origin, 0, nj)
                return ((ni, nj, done | at_origin), (i, j, valid))
            init = (jnp.int32(T1 - 1), jnp.int32(T2 - 1), jnp.bool_(False))
            _, (i_idx, j_idx, valid) = lax.scan(step, init, None, length=L)
            return (i_idx, j_idx, valid)

        def _align_one(small, large):
            T_small, d = small.shape
            T_large = large.shape[0]
            D = _pairwise_euclidean(small, large)
            R = _dtw_cost(D)
            i_idx, j_idx, valid = _backtrack(R, T_small, T_large)
            contrib = small[i_idx] * valid[:, None].astype(small.dtype)
            expanded = jnp.zeros((T_large, d), dtype=small.dtype).at[j_idx].add(contrib)
            return expanded
        key = jax.random.key(seed)
        k1, k2 = jax.random.split(key)
        teacher = jax.random.normal(k1, (16, 100, 256), dtype=jnp.float32)
        student = jax.random.normal(k2, (16, 150, 256), dtype=jnp.float32)
        return {'teacher_features': teacher, 'student_features': student}
    _L0_xattn_all = _L0_xattn_setup()
    _L0_xattn_in = {k: v for k, v in _L0_xattn_all.items() if k in ()}
    del _L0_xattn_all

    def _L0_ffn_setup():
        import jax, jax.numpy as jnp
        import numpy as np
        import math
        E = 16
        TOP_K = 2
        D = 256
        F = 1024
        SH = 512
        key = jax.random.key(seed)
        ks = jax.random.split(key, 10)
        s = lambda k, shape, fan: jax.random.normal(k, shape, jnp.float32) / np.sqrt(fan)
        return {'x': jax.random.normal(ks[0], (32, 64, D), jnp.float32), 'gate_w': s(ks[1], (E, D), D), 'up_w': s(ks[2], (E, F, D), D), 'up_b': s(ks[3], (E, F), D), 'gw': s(ks[4], (E, F, D), D), 'gb': s(ks[5], (E, F), D), 'down_w': s(ks[6], (E, D, F), F), 'down_b': s(ks[7], (E, D), F), 'sh_gate_w': s(ks[8], (SH, D), D), 'sh_up_w': s(ks[9], (SH, D), D), 'sh_down_w': s(jax.random.fold_in(key, 11), (D, SH), SH)}
    _L0_ffn_all = _L0_ffn_setup()
    _L0_ffn_in = {k: v for k, v in _L0_ffn_all.items() if k in ('gate_w', 'up_w', 'up_b', 'gw', 'gb', 'down_w', 'down_b', 'sh_gate_w', 'sh_up_w', 'sh_down_w')}
    del _L0_ffn_all
    return {'x': x, 'ctx_1024': ctx_1024, 'g_xattn': g_xattn, 'g_ffn': g_ffn, 'L0_ffn_gate_w': _L0_ffn_in['gate_w'], 'L0_ffn_up_w': _L0_ffn_in['up_w'], 'L0_ffn_up_b': _L0_ffn_in['up_b'], 'L0_ffn_gw': _L0_ffn_in['gw'], 'L0_ffn_gb': _L0_ffn_in['gb'], 'L0_ffn_down_w': _L0_ffn_in['down_w'], 'L0_ffn_down_b': _L0_ffn_in['down_b'], 'L0_ffn_sh_gate_w': _L0_ffn_in['sh_gate_w'], 'L0_ffn_sh_up_w': _L0_ffn_in['sh_up_w'], 'L0_ffn_sh_down_w': _L0_ffn_in['sh_down_w']}

def reference(x, ctx_1024, g_xattn, g_ffn, L0_ffn_gate_w, L0_ffn_up_w, L0_ffn_up_b, L0_ffn_gw, L0_ffn_gb, L0_ffn_down_w, L0_ffn_down_b, L0_ffn_sh_gate_w, L0_ffn_sh_up_w, L0_ffn_sh_down_w):
    import jax
    import jax.numpy as jnp

    def _L0_xattn_ref(teacher_features, student_features):
        import jax, jax.numpy as jnp
        import numpy as np
        from jax import lax
        BIG = jnp.float32(1e+30)

        def _pairwise_euclidean(a, b):
            aa = jnp.sum(a * a, axis=-1)[:, None]
            bb = jnp.sum(b * b, axis=-1)[None, :]
            ab = a @ b.T
            return jnp.sqrt(jnp.maximum(aa + bb - 2.0 * ab, 0.0))

        def _dtw_cost(D):
            row0 = jnp.cumsum(D[0])

            def row_step(prev_row, d_row):
                first = d_row[0] + prev_row[0]

                def col_step(left, inp):
                    d_ij, up, diag = inp
                    r = d_ij + jnp.minimum(jnp.minimum(up, left), diag)
                    return (r, r)
                _, rest = lax.scan(col_step, first, (d_row[1:], prev_row[1:], prev_row[:-1]))
                row = jnp.concatenate([first[None], rest])
                return (row, row)
            _, rows = lax.scan(row_step, row0, D[1:])
            return jnp.concatenate([row0[None], rows], axis=0)

        def _backtrack(R, T1, T2):
            L = T1 + T2 - 1

            def step(carry, _):
                i, j, done = carry
                valid = jnp.logical_not(done)
                cd = jnp.where((i > 0) & (j > 0), R[jnp.maximum(i - 1, 0), jnp.maximum(j - 1, 0)], BIG)
                cu = jnp.where(i > 0, R[jnp.maximum(i - 1, 0), j], BIG)
                cl = jnp.where(j > 0, R[i, jnp.maximum(j - 1, 0)], BIG)
                choice = jnp.argmin(jnp.stack([cd, cu, cl]))
                ni = jnp.where(choice <= 1, i - 1, i)
                nj = jnp.where((choice == 0) | (choice == 2), j - 1, j)
                at_origin = (i == 0) & (j == 0)
                ni = jnp.where(at_origin, 0, ni)
                nj = jnp.where(at_origin, 0, nj)
                return ((ni, nj, done | at_origin), (i, j, valid))
            init = (jnp.int32(T1 - 1), jnp.int32(T2 - 1), jnp.bool_(False))
            _, (i_idx, j_idx, valid) = lax.scan(step, init, None, length=L)
            return (i_idx, j_idx, valid)

        def _align_one(small, large):
            T_small, d = small.shape
            T_large = large.shape[0]
            D = _pairwise_euclidean(small, large)
            R = _dtw_cost(D)
            i_idx, j_idx, valid = _backtrack(R, T_small, T_large)
            contrib = small[i_idx] * valid[:, None].astype(small.dtype)
            expanded = jnp.zeros((T_large, d), dtype=small.dtype).at[j_idx].add(contrib)
            return expanded
        return jax.vmap(_align_one)(teacher_features, student_features)

    def _L0_ffn_ref(x, gate_w, up_w, up_b, gw, gb, down_w, down_b, sh_gate_w, sh_up_w, sh_down_w):
        import jax, jax.numpy as jnp
        import numpy as np
        import math
        E = 16
        TOP_K = 2
        D = 256
        F = 1024
        SH = 512
        B, S, Dm = x.shape
        h = x.reshape(-1, Dm)
        T = h.shape[0]
        scores = jax.nn.sigmoid(h @ gate_w.T)
        cap = math.ceil(T / E * TOP_K)
        topk_score, topk_ids = jax.lax.top_k(scores.T, cap)
        xin = h[topk_ids]
        up = jnp.einsum('ecd,efd->ecf', xin, up_w) + up_b[:, None, :]
        g = jnp.einsum('ecd,efd->ecf', xin, gw) + gb[:, None, :]
        eo = jax.nn.silu(g) * up
        eo = jnp.einsum('ecf,edf->ecd', eo, down_w) + down_b[:, None, :]
        flat = (eo * topk_score[..., None]).reshape(-1, Dm)
        out = jnp.zeros_like(h).at[topk_ids.reshape(-1)].add(flat)
        out = out.reshape(B, S, Dm)
        shared = jax.nn.silu(jnp.einsum('bsd,fd->bsf', x, sh_gate_w)) * jnp.einsum('bsd,fd->bsf', x, sh_up_w)
        shared = jnp.einsum('bsf,df->bsd', shared, sh_down_w)
        return out + shared
    x = x + jnp.tanh(g_xattn[0]) * _L0_xattn_ref(ctx_1024, _layernorm(x, axis=-1))
    x = x + jnp.tanh(g_ffn[0]) * _L0_ffn_ref(_layernorm(x, axis=-1), L0_ffn_gate_w, L0_ffn_up_w, L0_ffn_up_b, L0_ffn_gw, L0_ffn_gb, L0_ffn_down_w, L0_ffn_down_b, L0_ffn_sh_gate_w, L0_ffn_sh_up_w, L0_ffn_sh_down_w)
    return x

_drawn_inputs = setup_inputs


def setup_inputs(seed=0):
    import zlib

    import numpy as np

    out = dict(_drawn_inputs(seed))
    spreads = {}
    factors = {}
    for name, (base, spread) in spreads.items():
        noise = np.random.default_rng([zlib.crc32(name.encode()), seed]).standard_normal(out[name].shape)
        drawn = base * np.exp(spread * noise) if base else spread * noise
        out[name] = jnp.asarray(drawn.astype(out[name].dtype))
    for name, factor in factors.items():
        out[name] = (out[name] * factor).astype(out[name].dtype)
    return out
```

```python
import concourse.bass as bass
from concourse import mybir
from contextlib import ExitStack

F32 = mybir.dt.float32
BF16 = mybir.dt.bfloat16
I32 = mybir.dt.int32
ALU = mybir.AluOpType
ACT = mybir.ActivationFunctionType

P = 128
B, S, D = 4, 512, 256
ST = S // P
NT = B * ST
KC = D // P
NK = 32
W = S // NK
CELL = W + 1
PAD = 32
STEPS = S + NK
HALF = 16
LOOPS = STEPS // (2 * HALF)
DROWS = PAD + S + NK
MROW = 2 * W + 4
BIG = 1e30
EPS = 1e-5
TINY = 1e-18

E_, CAP, F = 16, 256, 1024
FT = F // P
SH = 512
SF = SH // P
NTOK = B * S
HROW = D + E_
SEG = 8
SEGT = NTOK // SEG


def prepare_distances(nc, h):
    ctx = ExitStack()
    with ctx:
        sb = lambda name, shape, dt=F32: ctx.enter_context(nc.sbuf_tensor(name, shape, dt))
        sem = lambda name: ctx.enter_context(nc.semaphore(name))
        X = h["X"]
        C = h["C"]
        ident = h["ident"]
        XN = sb("XN", [P, NT, D])
        CT = sb("CT", [P, KC, B, S])
        XT = sb("XT", [P, KC, B, S])
        XSQ = sb("XSQ", [P, KC, B, S])
        junk = sb("junkA", [P, D])
        bnst = sb("bnst", [P, NT, 6])
        mv = sb("mv", [P, NT, 2])
        sd = sb("sd", [P, 4, NT])
        aa = sb("aa", [P, NT])
        bbrow = sb("bbrow", [1, B, S])
        ones = sb("onesA", [P, P])
        d2 = sb("d2", [P, B, S])
        root = sb("root", [P, B, S])
        half_inv = sb("half_inv", [P, B, S])
        dt_ = [sb(f"dt{i}", [P, P, CELL]) for i in range(2)]
        bcol = sb("bcol", [P, 1])
        pidx = sb("pidx", [P, 2], I32)
        zpad = sb("zpad", [P, PAD * CELL])
        lnhalf = sb("lnhalf", [P, 1])
        bank = [ctx.enter_context(nc.psum_tensor(f"pA{i}", [P, 512], F32)) for i in range(8)]

        x_in, c_in, ident_ready, ones_ready = sem("x_in"), sem("c_in"), sem("ident_ready"), sem("ones_readyA")
        c_T, c_Te, x_T, x_Te = sem("c_T"), sem("c_Te"), sem("x_T"), sem("x_Te")
        xn_ready, var_ready, root_ready = sem("xn_ready"), sem("var_ready"), sem("sd_ready")
        aa_ready, sq_ready, bb_done, bb_ready = sem("aa_ready"), sem("sq_ready"), sem("bb_done"), sem("bb_ready")
        d_done, d_evac, inv_ready, newton = sem("d_done"), sem("d_evac"), sem("inv_ready"), sem("newton")
        w_T, w_evA, w_evD, d_out0, d_out1 = sem("w_T"), sem("w_evA"), sem("w_evD"), sem("d_out0"), sem("d_out1")
        zero_ready, pad_out = sem("zero_ready"), sem("pad_out")
        vch, ach, pch = sem("vchA"), sem("achA"), sem("pchA")
        bcol_ready, pidx_ready = sem("bcol_ready"), sem("pidx_ready")
        d_out = [d_out0, d_out1]
        block = ctx.enter_context(nc.Block())

        dd = h["dd"]

        @block.sync
        def _(sp):
            sp.dma_start(C[:, :, :], h["ctx"].rearrange("b (t p) d -> p (b t) d", p=P)).then_inc(c_in, 16)
            sp.wait_ge(zero_ready, 1)
            sp.dma_start(dd[:, 0:PAD, :], zpad[:, :].rearrange("p (r c) -> p r c", c=CELL)).then_inc(pad_out, 16)
            sp.dma_start(dd[:, PAD + S:DROWS, :], zpad[:, :].rearrange("p (r c) -> p r c", c=CELL)).then_inc(pad_out, 16)
            for it in range(ST):
                sp.wait_ge(w_evA, 2 * (it + 1))
                sp.wait_ge(w_evD, 2 * (it + 1))
                sp.dma_start(dd[:, PAD + it * P:PAD + (it + 1) * P, :], dt_[it % 2][:, :, :]).then_inc(d_out[it % 2], 16)
            sp.wait_ge(d_out0, 32)
            sp.wait_ge(d_out1, 32)
            sp.wait_ge(pad_out, 32)

        @block.gpsimd
        def _(pool):
            nc.gpsimd.memset(ident[:, :], 0.0).then_inc(pch, 1)
            pool.wait_ge(pch, 1)
            nc.gpsimd.affine_select(out=ident[:, :], in_=ident[:, :], compare_op=ALU.not_equal, fill=1.0, base=0,
                                    pattern=[[-1, P]], channel_multiplier=1).then_inc(ident_ready, 1)
            nc.gpsimd.memset(ones[:, :], 1.0).then_inc(ones_ready, 1)
            nc.gpsimd.memset(zpad[:, :], 0.0).then_inc(zero_ready, 1)
            nc.gpsimd.iota(pidx[:, 0:1], pattern=[[0, 1]], base=0, channel_multiplier=1).then_inc(pidx_ready, 1)

        @block.scalar
        def _(act):
            act.dma_start(X[:, :, :], h["x"].rearrange("b (t p) d -> p (b t) d", p=P)).then_inc(x_in, 16)
            act.wait_ge(c_in, 16)
            for i in range(NT):
                nc.scalar.activation(junk[:, :], C[:, i, :], ACT.Square, accum_out=aa[:, i:i + 1]).then_inc(ach, 1)
                act.wait_ge(ach, i + 1)
            act.wait_ge(var_ready, 1)
            nc.scalar.activation(sd[:, 1, :], sd[:, 0, :], ACT.Sqrt).then_inc(root_ready, 1)
            for g in range(KC * B):
                act.wait_ge(c_T, g + 1)
                nc.scalar.activation(CT[:, g % KC, g // KC, :], bank[g % 4][:, :], ACT.Copy, scale=-2.0).then_inc(c_Te, 1)
            for g in range(KC * B):
                act.wait_ge(x_Te, g + 1)
                nc.scalar.activation(XSQ[:, g % KC, g // KC, :], XT[:, g % KC, g // KC, :], ACT.Square).then_inc(sq_ready, 1)
            for it in range(ST):
                act.wait_ge(d_evac, 4 * (it + 1))
                nc.scalar.activation(half_inv[:, :, :], d2[:, :, :], ACT.Ln).then_inc(ach, 1)
                act.wait_ge(ach, NT + 2 * it + 1)
                nc.scalar.activation(half_inv[:, :, :], half_inv[:, :, :], ACT.Exp, scale=-0.5, bias=lnhalf[:, :]).then_inc(ach, 1)
                nc.scalar.activation(root[:, :, :], d2[:, :, :], ACT.Sqrt).then_inc(inv_ready, 1)
                for g in (0, 2):
                    act.wait_ge(w_T, 4 * it + g + 1)
                    if g == 0 and it >= 2:
                        act.wait_ge(d_out[it % 2], 16)
                    nc.scalar.activation(dt_[it % 2][:, :, 1 + 4 * g:5 + 4 * g].rearrange("p i w -> p w i"),
                                         bank[g][:, :].rearrange("p (w i) -> p w i", w=4), ACT.Copy).then_inc(w_evA, 1)

        @block.vector
        def _(dve):
            n = [0]

            def link(ins):
                n[0] += 1
                ins.then_inc(vch, 1)
                dve.wait_ge(vch, n[0])

            nc.vector.memset(lnhalf[:, :], -0.6931471805599453)
            dve.wait_ge(pidx_ready, 1)
            link(nc.vector.tensor_scalar(out=pidx[:, 1:2], in0=pidx[:, 0:1], scalar1=NK - 1, scalar2=None, op0=ALU.bitwise_and))
            link(nc.vector.tensor_scalar(out=bcol[:, 0:1], in0=pidx[:, 1:2], scalar1=0.0, scalar2=BIG, op0=ALU.is_equal, op1=ALU.mult))
            link(nc.vector.tensor_scalar(out=h["first_block"][:, :], in0=pidx[:, 1:2], scalar1=0.0, scalar2=None, op0=ALU.is_equal))
            link(nc.vector.tensor_scalar(out=h["last_block"][:, :], in0=pidx[:, 1:2], scalar1=float(NK - 1), scalar2=None, op0=ALU.is_equal))
            dve.wait_ge(x_in, 16)
            for i in range(NT):
                last = nc.vector.bn_stats(bnst[:, i, :], X[:, i, :])
            link(last)
            for i in range(NT):
                last = nc.vector.bn_aggr(mv[:, i, :], bnst[:, i, :])
            link(last)
            nc.vector.tensor_scalar(out=sd[:, 0, :], in0=mv[:, :, 1], scalar1=EPS, scalar2=None, op0=ALU.add).then_inc(var_ready, 1)
            dve.wait_ge(root_ready, 1)
            dve.wait_ge(var_ready, 1)
            link(nc.vector.reciprocal(sd[:, 2, :], sd[:, 1, :]))
            link(nc.vector.tensor_tensor(out=sd[:, 3, :], in0=sd[:, 0, :], in1=sd[:, 2, :], op=ALU.mult))
            link(nc.vector.tensor_tensor(out=sd[:, 2, :], in0=sd[:, 3, :], in1=sd[:, 1, :], op=ALU.add))
            link(nc.vector.tensor_scalar(out=sd[:, 3, :], in0=sd[:, 2, :], scalar1=0.5, scalar2=None, op0=ALU.mult))
            link(nc.vector.reciprocal(sd[:, 2, :], sd[:, 3, :]))
            for i in range(NT):
                nc.vector.tensor_scalar(out=XN[:, i, :], in0=X[:, i, :], scalar1=mv[:, i, 0:1], scalar2=sd[:, 2, i:i + 1],
                                        op0=ALU.subtract, op1=ALU.mult).then_inc(xn_ready, 1)
            for g in range(KC * B):
                dve.wait_ge(x_T, g + 1)
                nc.vector.tensor_copy(XT[:, g % KC, g // KC, :], bank[4 + g % 4][:, :]).then_inc(x_Te, 1)
            for b in range(B):
                dve.wait_ge(bb_done, b + 1)
                nc.vector.tensor_copy(bbrow[0:1, b, :], bank[b][0:1, :]).then_inc(bb_ready, 1)
            for it in range(ST):
                if it:
                    dve.wait_ge(w_T, 4 * it)
                for b in range(B):
                    dve.wait_ge(d_done, 4 * it + b + 1)
                    nc.vector.tensor_scalar(out=d2[:, b, :], in0=bank[4 + b][:, :], scalar1=aa[:, b * ST + it:b * ST + it + 1],
                                            scalar2=TINY, op0=ALU.add, op1=ALU.max).then_inc(d_evac, 1)
                dve.wait_ge(inv_ready, it + 1)
                dve.wait_ge(d_evac, 4 * (it + 1))
                link(nc.vector.tensor_tensor(out=XSQ[:, 0, :, :], in0=root[:, :, :], in1=root[:, :, :], op=ALU.mult))
                link(nc.vector.tensor_tensor(out=XSQ[:, 1, :, :], in0=d2[:, :, :], in1=XSQ[:, 0, :, :], op=ALU.subtract))
                link(nc.vector.tensor_tensor(out=XSQ[:, 0, :, :], in0=XSQ[:, 1, :, :], in1=half_inv[:, :, :], op=ALU.mult))
                nc.vector.tensor_tensor(out=root[:, :, :], in0=root[:, :, :], in1=XSQ[:, 0, :, :], op=ALU.add).then_inc(newton, 1)
                if it >= 2:
                    dve.wait_ge(d_out[it % 2], 16)
                nc.vector.tensor_copy(dt_[it % 2][:, :, 0], bcol[:, 0:1].to_broadcast([P, P]))
                for g in (1, 3):
                    dve.wait_ge(w_T, 4 * it + g + 1)
                    last = nc.vector.tensor_copy(dt_[it % 2][:, :, 1 + 4 * g:5 + 4 * g].rearrange("p i w -> p w i"),
                                                 bank[g][:, :].rearrange("p (w i) -> p w i", w=4))
                    last.then_inc(w_evD, 1)

        @block.tensor
        def _(pe):
            pe.wait_ge(ident_ready, 1)
            pe.wait_ge(c_in, 16)
            for g in range(KC * B):
                if g >= 4:
                    pe.wait_ge(c_Te, g - 3)
                for t in range(ST):
                    last = nc.tensor.transpose(bank[g % 4][:, t * P:(t + 1) * P],
                                               C[:, (g // KC) * ST + t, (g % KC) * P:(g % KC + 1) * P], ident[:, :])
                last.then_inc(c_T, 1)
            for g in range(KC * B):
                pe.wait_ge(xn_ready, (g // KC + 1) * ST)
                if g >= 4:
                    pe.wait_ge(x_Te, g - 3)
                for t in range(ST):
                    last = nc.tensor.transpose(bank[4 + g % 4][:, t * P:(t + 1) * P],
                                               XN[:, (g // KC) * ST + t, (g % KC) * P:(g % KC + 1) * P], ident[:, :])
                last.then_inc(x_T, 1)
            pe.wait_ge(ones_ready, 1)
            pe.wait_ge(c_Te, KC * B)
            for b in range(B):
                pe.wait_ge(sq_ready, KC * (b + 1))
                for kc in range(KC):
                    last = nc.tensor.matmul(bank[b][0:1, :], ones[:, 0:1], XSQ[:, kc, b, :], start=(kc == 0), stop=(kc == KC - 1))
                last.then_inc(bb_done, 1)
            pe.wait_ge(bb_ready, B)
            pe.wait_ge(x_Te, KC * B)
            for it in range(ST):
                for b in range(B):
                    if it:
                        pe.wait_ge(d_evac, 4 * (it - 1) + b + 1)
                    for kc in range(KC):
                        nc.tensor.matmul(bank[4 + b][:, :], CT[:, kc, b, it * P:(it + 1) * P], XT[:, kc, b, :],
                                         start=(kc == 0), stop=False)
                    nc.tensor.matmul(bank[4 + b][:, :], ones[0:1, :], bbrow[0:1, b, :], start=False, stop=True).then_inc(d_done, 1)
                pe.wait_ge(newton, it + 1)
                if it:
                    pe.wait_ge(w_evA, 2 * it)
                    pe.wait_ge(w_evD, 2 * it)
                rv = root[:, :, :].rearrange("p b (k w) -> p (b k) w", w=W)
                for w in range(W):
                    last = nc.tensor.transpose(bank[w // 4][:, (w % 4) * P:(w % 4 + 1) * P], rv[:, :, w], ident[:, :])
                    if w % 4 == 3:
                        last.then_inc(w_T, 1)


def accumulate_costs(nc, h):
    ctx = ExitStack()
    with ctx:
        sb = lambda name, shape, dt=F32: ctx.enter_context(nc.sbuf_tensor(name, shape, dt))
        sem = lambda name: ctx.enter_context(nc.semaphore(name))
        RING = 2 * HALF
        GR = 4
        dist = [sb(f"dist{i}", [P, HALF * CELL]) for i in range(2)]
        rows = sb("rowsB", [P, RING + 1, CELL])
        upper = sb("upper", [P, RING, CELL])
        left0 = sb("left0", [P, 1])
        isup = sb("isup", [P, GR, W])
        mring = sb("mring", [P, RING, 3, W], BF16)
        marks = h["marks"]
        tch, last_kept = sem("tchB"), sem("last_kept")
        dist_in = [sem(f"dist_in{i}") for i in range(2)]
        rows_ready = [sem(f"rows_ready{i}") for i in range(2)]
        marks_ready = [sem(f"marks_ready{i}") for i in range(2)]
        marks_kept = [sem(f"marks_kept{i}") for i in range(2)]
        dd = h["dd"]
        skew = bass.AP(dd.tensor, dd.offset, [[NK * DROWS * CELL, B], [(DROWS - 1) * CELL, NK], [1, DROWS * CELL]])
        block = ctx.enter_context(nc.Block())

        @block.sync
        def _(sp):
            with sp.Fori(0, LOOPS) as it:
                for hf in range(2):
                    sp.wait_ge(rows_ready[hf], it + 1)
                    sp.dma_start(dist[hf][:, :], skew[:, :, bass.ds((it * RING + (PAD + hf * HALF)) * CELL, HALF * CELL)])\
                        .then_inc(dist_in[hf], 16)

        @block.gpsimd
        def _(pool):
            nc.gpsimd.memset(marks[:, STEPS:, :, :], 0.0).then_inc(last_kept, 1)

        def mark(g, part):
            lo = g * GR
            diag, up = rows[:, lo:lo + GR, 0:W], rows[:, lo:lo + GR, 1:CELL]
            left, m = rows[:, lo + 1:lo + 1 + GR, 0:W], mring[:, lo:lo + GR, :, :]
            if part == 0:
                nc.vector.tensor_tensor(out=isup[:, :, :], in0=up, in1=diag, op=ALU.is_lt)
            if part == 1:
                nc.vector.tensor_tensor(out=m[:, :, 2, :], in0=left, in1=upper[:, lo:lo + GR, 1:CELL], op=ALU.is_lt)
            if part == 2:
                nc.vector.tensor_tensor(out=m[:, :, 1, :], in0=isup[:, :, :], in1=m[:, :, 2, :], op=ALU.is_gt)
            if part == 3:
                nc.vector.scalar_tensor_tensor(out=m[:, :, 0, :], in0=isup[:, :, :], scalar=0.5, in1=m[:, :, 2, :],
                                               op0=ALU.is_lt, op1=ALU.is_gt)

        @block.vector
        def _(dve):
            nc.vector.memset(rows[:, :, :], BIG)
            nc.vector.memset(upper[:, :, :], BIG).then_inc(tch, 1)
            dve.wait_ge(tch, 1)
            nc.vector.tensor_scalar(out=rows[:, RING, 0:1], in0=h["first_block"][:, :], scalar1=-BIG, scalar2=BIG,
                                    op0=ALU.mult, op1=ALU.add).then_inc(tch, 1)
            dve.wait_ge(tch, 2)
            dve.sem_inc(rows_ready[0], 1)
            from_left = [(p - 1) % NK for p in range(NK)]
            with dve.Fori(0, LOOPS) as it:
                dve.sem_clear(tch)
                for u in range(RING):
                    hf = u // HALF
                    cur, prev = rows[:, u + 1, :], rows[:, u if u else RING, :]
                    g = (u // GR - 1) % (RING // GR)
                    shuffle = nc.vector.stream_shuffle(left0[:, :], prev[:, W:CELL], from_left)
                    if u % HALF == 0:
                        shuffle.then_inc(rows_ready[1 - hf], 1)
                    if u % HALF == 2 * GR:
                        shuffle.then_inc(marks_ready[1 - hf], 1)
                    nc.vector.tensor_tensor(out=upper[:, u, 1:CELL], in0=prev[:, 0:W], in1=prev[:, 1:CELL], op=ALU.min).then_inc(tch, 1)
                    if u % HALF == GR:
                        dve.wait_ge(marks_kept[hf], it + 1)
                    if u % GR in (0, 2):
                        mark(g, (0, None, 3)[u % GR])
                    if u % HALF == 0:
                        dve.wait_ge(dist_in[hf], it * 16 + 16)
                    dve.wait_ge(tch, 2 * u + 1)
                    nc.vector.tensor_tensor_scan(out=cur, data0=upper[:, u, :], data1=dist[hf][:, (u % HALF) * CELL:(u % HALF + 1) * CELL],
                                                 initial=left0[:, :], op0=ALU.min, op1=ALU.add).then_inc(tch, 1)
                    if u % GR < 2:
                        mark(g, 1 + u % GR)
                    if u == 2:
                        nc.vector.tensor_copy(rows[:, 0, :], rows[:, RING, :])
                    dve.wait_ge(tch, 2 * u + 2)
            for part in range(4):
                mark(RING // GR - 1, part)
                nc.vector.tensor_copy(left0[:, :], rows[:, 0, 0:1]).then_inc(tch, 1)
                dve.wait_ge(tch, 2 * RING + part + 1)
            nc.vector.tensor_copy(left0[:, :], rows[:, 0, 0:1]).then_inc(marks_ready[1], 1)

        @block.scalar
        def _(act):
            for hf in range(2):
                act.sem_inc(marks_kept[hf], 1)
            with act.Fori(0, LOOPS) as it:
                for hf in range(2):
                    act.wait_ge(marks_ready[hf], it + 1 + hf)
                    nc.scalar.activation(marks[:, bass.ds(it * RING + hf * HALF, HALF), :, :].rearrange("p r m w -> p (r m w)"),
                                         mring[:, hf * HALF:(hf + 1) * HALF, :, :].rearrange("p r m w -> p (r m w)"), ACT.Copy)\
                        .then_inc(marks_kept[hf], 1)


def trace_path(nc, h):
    ctx = ExitStack()
    with ctx:
        sb = lambda name, shape, dt=F32: ctx.enter_context(nc.sbuf_tensor(name, shape, dt))
        sem = lambda name: ctx.enter_context(nc.semaphore(name))
        marks = h["marks"]
        SLOT = HALF + 2
        gives = [sb(f"gives{i}", [P, SLOT, MROW], BF16) for i in range(2)]
        lefts = [sb(f"lefts{i}", [P, SLOT, MROW], BF16) for i in range(2)]
        on = sb("on", [P, 2 * HALF, MROW], BF16)
        given = sb("given", [P, MROW])
        kz = sb("kz", [P, 2])
        tch, ini = sem("tchC"), sem("iniC")
        slot_ready = [sem(f"slot_ready{i}") for i in range(2)]
        half_done = [sem(f"half_done{i}") for i in range(2)]
        om_out = [sem(f"om_out{i}") for i in range(2)]
        om = h["om"]
        skew = bass.AP(om.tensor, om.offset, [[NK * DROWS * MROW, B], [(DROWS - 1) * MROW, NK], [1, DROWS * MROW]])
        block = ctx.enter_context(nc.Block())

        def pairs(row, first, gap, n):
            return bass.AP(row.tensor, row.offset + first, [list(row.ap[0]), [2, n], [gap, 2]])

        def back(row):
            return bass.AP(row.tensor, row.offset + 2 * W + 1, [list(row.ap[0]), [-1, 2 * W]])

        @block.vector
        def _(dve):
            n = [0]

            def link(ins):
                n[0] += 1
                ins.then_inc(ini, 1)
                dve.wait_ge(ini, n[0])

            nc.vector.tensor_scalar(out=kz[:, 0:1], in0=h["first_block"][:, :], scalar1=1.0, scalar2=None, op0=ALU.mult)
            link(nc.vector.tensor_scalar(out=kz[:, 1:2], in0=h["first_block"][:, :], scalar1=-1.0, scalar2=1.0, op0=ALU.mult, op1=ALU.add))
            for m, (s, op) in enumerate(((1, ALU.mult), (0, ALU.max), (1, ALU.mult))):
                link(nc.vector.tensor_scalar(out=marks[:, 0:STEPS, m, 0], in0=marks[:, 0:STEPS, m, 0], scalar1=kz[:, s:s + 1],
                                             scalar2=None, op0=op))
            link(nc.vector.memset(marks[:, STEPS - 1, :, :], 0.0))
            link(nc.vector.memset(marks[:, STEPS - 1:STEPS + 1, 1, W - 1:W], 1.0))
            for i in range(2):
                nc.vector.memset(gives[i][:, :, :], 0.0)
                last = nc.vector.memset(lefts[i][:, :, :], 1.0)
            nc.vector.memset(given[:, :], 0.0)
            link(last)
            link(nc.vector.memset(on[:, :, :], 0.0))
            link(nc.vector.tensor_copy(on[:, 0, 2 * W:2 * W + 1], h["last_block"][:, :]))
            last_init = n[0]
            h["init_count"] = last_init
            from_right = [(p + 1) % NK for p in range(NK)]
            dve.sem_inc(half_done[1], 1)
            with dve.Fori(0, LOOPS) as it:
                dve.sem_clear(tch)
                k = 0
                for u in reversed(range(2 * HALF)):
                    hf, r = u // HALF, u % HALF
                    cur, prev = on[:, u, :], on[:, (u + 1) % (2 * HALF), :]
                    if r == HALF - 1:
                        dve.wait_ge(slot_ready[hf], 3 * it + 3)
                        dve.wait_ge(om_out[hf], 16 * it + 16)
                        nc.vector.tensor_copy(kz[:, 0:1], kz[:, 1:2])
                        nc.vector.stream_shuffle(gives[hf][:, 1:HALF + 1, 2 * W], gives[hf][:, 2:HALF + 2, 0], from_right)
                        nc.vector.stream_shuffle(lefts[hf][:, 0:HALF, 2 * W + 1], lefts[hf][:, 1:HALF + 1, 1], from_right).then_inc(tch, 1)
                        k += 1
                        dve.wait_ge(tch, k)
                    shuffle = nc.vector.stream_shuffle(cur[:, 2 * W + 2:2 * W + 3], prev[:, 2:3], from_right)
                    if r == HALF - 1:
                        shuffle.then_inc(half_done[1 - hf], 1)
                    here = bass.AP(prev.tensor, prev.offset + 2, [list(prev.ap[0]), [2, W + 1], [0, 2]])
                    nc.vector.tensor_tensor(out=pairs(given[:, :], 0, 3, W + 1), in0=pairs(gives[hf][:, r + 1, :], 0, 3, W + 1), in1=here,
                                            op=ALU.mult).then_inc(tch, 1)
                    k += 1
                    dve.wait_ge(tch, k)
                    nc.vector.tensor_tensor_scan(out=back(cur), data0=back(lefts[hf][:, r, :]), data1=back(given[:, :]),
                                                 initial=cur[:, 2 * W + 2:2 * W + 3], op0=ALU.mult, op1=ALU.add).then_inc(tch, 1)
                    k += 1
                    dve.wait_ge(tch, k)
            nc.vector.memset(given[:, :], 0.0).then_inc(half_done[0], 1)

        @block.scalar
        def _(act):
            act.wait_ge(ini, 9)
            with act.Fori(0, LOOPS) as it:
                for hf in (1, 0):
                    act.wait_ge(half_done[hf], it + 1)
                    mk = marks[:, bass.ds((it * -(2 * HALF)) + ((LOOPS - 1) * 2 * HALF + hf * HALF), SLOT), :, :]
                    nc.scalar.activation(gives[hf][:, :, 0:2 * W:2], mk[:, :, 0, :], ACT.Copy).then_inc(slot_ready[hf], 1)
                    nc.scalar.activation(gives[hf][:, :, 3:2 * W + 3:2], mk[:, :, 1, :], ACT.Copy).then_inc(slot_ready[hf], 1)
                    nc.scalar.activation(lefts[hf][:, :, 1:2 * W + 1:2], mk[:, :, 2, :], ACT.Copy).then_inc(slot_ready[hf], 1)

        @block.sync
        def _(sp):
            for hf in range(2):
                sp.sem_inc(om_out[hf], 16)
            with sp.Fori(0, LOOPS) as it:
                for hf in (1, 0):
                    sp.wait_ge(half_done[hf], it + 2)
                    sp.dma_start(skew[:, :, bass.ds(it * -(2 * HALF * MROW) + (PAD + (LOOPS - 1) * 2 * HALF + hf * HALF) * MROW, HALF * MROW)],
                                 on[:, hf * HALF:(hf + 1) * HALF, :].rearrange("p r c -> p (r c)")).then_inc(om_out[hf], 16)
            for hf in range(2):
                sp.wait_ge(om_out[hf], 16 * LOOPS + 16)


def align(nc, h):
    ctx = ExitStack()
    with ctx:
        sb = lambda name, shape, dt=F32: ctx.enter_context(nc.sbuf_tensor(name, shape, dt))
        sem = lambda name: ctx.enter_context(nc.semaphore(name))
        X, C = h["X"], h["C"]
        rows = [sb(f"rows{i}", [P, P, MROW], BF16) for i in range(2)]
        path = sb("path", [P, ST, B * S])
        identb = h["identb"]
        g = sb("gD", [P, 2])
        tg = h["tg"]
        tp = [ctx.enter_context(nc.psum_tensor(f"pD{i}", [P, 8 * P], BF16)) for i in range(4)]
        acc = [ctx.enter_context(nc.psum_tensor(f"aD{i}", [P, 2 * D], F32)) for i in range(4)]
        rows_in = [sem(f"rows_in{i}") for i in range(2)]
        ib, t_done, evA, evD, g_in, tg_ready = sem("ib"), sem("t_doneD"), sem("evAD"), sem("evDD"), sem("g_in"), sem("tg_ready")
        sums, x1_ready = sem("sums"), sem("x1_ready")
        block = ctx.enter_context(nc.Block())

        @block.sync
        def _(sp):
            sp.dma_start(g[:, 0:1], bass.AP(h["g_xattn"].tensor, h["g_xattn"].offset, [[0, P], [1, 1]])).then_inc(g_in, 16)
            sp.dma_start(g[:, 1:2], bass.AP(h["g_ffn"].tensor, h["g_ffn"].offset, [[0, P], [1, 1]])).then_inc(g_in, 16)
            for it in range(ST):
                if it >= 2:
                    sp.wait_ge(t_done, 2 * (it - 1))
                sp.dma_start(rows[it % 2][:, :, :], h["om"][:, PAD + it * P:PAD + (it + 1) * P, :]).then_inc(rows_in[it % 2], 16)

        @block.tensor
        def _(pe):
            pe.wait_ge(ib, 1)
            for it in range(ST):
                pe.wait_ge(rows_in[it % 2], 16 * (it // 2 + 1))
                for half in range(2):
                    n = 2 * it + half
                    if n >= 4:
                        pe.wait_ge((evA, evD)[half], n // 2 - 1)
                    for w in range(8):
                        last = nc.tensor.transpose(tp[n % 4][:, w * P:(w + 1) * P], rows[it % 2][:, :, 2 * (8 * half + w) + 2], identb[:, :])
                    last.then_inc(t_done, 1)
            pe.wait_ge(evA, ST)
            pe.wait_ge(evD, ST)
            for b in range(B):
                for jp in range(2):
                    n = 2 * b + jp
                    if n >= 4:
                        pe.wait_ge(x1_ready, 2 * (n - 3))
                    for j in range(2):
                        jt = 2 * jp + j
                        for it in range(ST):
                            last = nc.tensor.matmul(acc[n % 4][:, j * D:(j + 1) * D], path[:, it, b * S + jt * P:b * S + (jt + 1) * P],
                                                    C[:, b * ST + it, :], start=(it == 0), stop=(it == ST - 1))
                    last.then_inc(sums, 1)

        def evacuate(eng, n):
            it, half = n // 2, n % 2
            dst = path[:, it, :].rearrange("p (k w) -> p w k", w=W)[:, 8 * half:8 * half + 8, :]
            return eng(dst, tp[n % 4][:, :].rearrange("p (w k) -> p w k", w=8))

        @block.scalar
        def _(act):
            act.wait_ge(g_in, 32)
            nc.scalar.activation(tg[:, :], g[:, :], ACT.Tanh).then_inc(tg_ready, 1)
            for it in range(ST):
                act.wait_ge(t_done, 2 * it + 1)
                evacuate(lambda o, i: nc.scalar.activation(o, i, ACT.Copy), 2 * it).then_inc(evA, 1)

        @block.vector
        def _(dve):
            nc.vector.tensor_copy(identb[:, :], h["ident"][:, :]).then_inc(ib, 1)
            for it in range(ST):
                dve.wait_ge(t_done, 2 * it + 2)
                evacuate(nc.vector.tensor_copy, 2 * it + 1).then_inc(evD, 1)
            dve.wait_ge(tg_ready, 1)
            for n in range(2 * B):
                dve.wait_ge(sums, n + 1)
                for j in range(2):
                    nc.vector.scalar_tensor_tensor(out=X[:, 2 * n + j, :], in0=acc[n % 4][:, j * D:(j + 1) * D], scalar=tg[:, 0:1],
                                                   in1=X[:, 2 * n + j, :], op0=ALU.mult, op1=ALU.add).then_inc(x1_ready, 1)


def route(nc, h):
    ctx = ExitStack()
    with ctx:
        sb = lambda name, shape, dt=F32: ctx.enter_context(nc.sbuf_tensor(name, shape, dt))
        sem = lambda name: ctx.enter_context(nc.semaphore(name))
        X, ident, ids = h["X"], h["ident"], h["ids"]
        H = sb("H", [P, NT, D])
        HT = sb("HT", [P, KC, NTOK])
        bnst = sb("bnstR", [P, NT, 6])
        mv = sb("mvR", [P, NT, 2])
        sd = sb("sdR", [P, 4, NT])
        gw = sb("gwR", [E_, D])
        gz = sb("gz", [P, KC, SEG, P])
        swn = sb("swn", [P, 2, SF, D])
        sdn = sb("sdn", [P, KC, SH])
        swT = sb("swT", [P, 2, KC, SH])
        sdT = sb("sdT", [P, SF, D])
        sil = sb("sil", [P, 2, 512])
        hid = sb("hid", [P, 2, SF, 512])
        sout = sb("sout", [P, 2, 2 * D])
        score = sb("score", [P, SEGT])
        scT = sb("scT", [P, 2, P])
        junk = sb("junkR", [P, SEGT])
        T = sb("T", [P, 8])
        bit = sb("bit", [P, 1], I32)
        cnt = sb("cnt", [P, 2])
        off = sb("off", [P, 4])
        gt, eq = sb("gt", [P, SEGT]), sb("eq", [P, SEGT])
        gtc, eqc = sb("gtc", [P, SEGT]), sb("eqc", [P, SEGT])
        zero = sb("zeroR", [P, SEGT])
        pos = sb("pos", [P, SEGT])
        posi = sb("posi", [P, 3, 2 * P], I32)
        posf = sb("posf", [P, 2, 2 * P])
        iot = sb("iot", [P, P], I32)
        iof = sb("iof", [P, 16])
        v0 = sb("v0", [P, 16])
        v1 = sb("v1", [P, 1])
        pm = sb("pm", [P, 4, P])
        oa = sb("oa", [P, 2 * P, 16], BF16)
        ob = sb("ob", [P, 2, 2 * P, 16], BF16)
        idv = sb("idv", [P, 2, P])
        idl = sb("idl", [P, 2, 16])
        lsp = sb("lsp", [P, 4, P])
        bank = [ctx.enter_context(nc.psum_tensor(f"pR{i}", [P, 512], F32)) for i in range(8)]

        w_in, gw_in, sdn_in = sem("w_inR"), sem("gw_inR"), sem("sdn_inR")
        varr, rootr, h_ready = sem("varR"), sem("rootR"), sem("h_readyR")
        h_T, h_Te, g_T, g_Te = sem("h_TR"), sem("h_TeR"), sem("g_TR"), sem("g_TeR")
        s_done, s_ready, c_ready, t_done = sem("s_doneR"), sem("s_readyR"), sem("c_readyR"), sem("t_doneR")
        masks, pos_ready, pos_T, oh_ready, idl_done = sem("masksR"), sem("pos_readyR"), sem("pos_TR"), sem("oh_readyR"), sem("idl_doneR")
        scT_done, scT_ready, lsp_ready, ids_done, off_done = sem("scT_doneR"), sem("scT_readyR"), sem("lsp_readyR"), sem("ids_doneR"), sem("off_doneR")
        sw_T, sw_Te, gu_done, sil_ready, hid_ready, dn_done, so_ready = [sem(n) for n in (
            "sw_TR", "sw_TeR", "gu_doneR", "sil_readyR", "hid_readyR", "dn_doneR", "so_readyR")]
        so_out = [sem(f"so_outR{i}") for i in range(2)]
        hx_out = sem("hx_outR")
        vch, ach, pch, sch = sem("vchR"), sem("achR"), sem("pchR"), sem("schR")
        hx, accum = h["hx"], h["accum"]
        ROUNDS = 30
        block = ctx.enter_context(nc.Block())

        @block.sync
        def _(sp):
            sp.dma_start(gw[:, :], h["gate_w"]).then_inc(gw_in, 16)
            sp.dma_start(swn[:, 0, :, :], h["sh_gate_w"].rearrange("(t p) d -> p t d", p=P)).then_inc(w_in, 16)
            sp.dma_start(swn[:, 1, :, :], h["sh_up_w"].rearrange("(t p) d -> p t d", p=P)).then_inc(w_in, 16)
            sp.dma_start(sdn[:, :, :], h["sh_down_w"].rearrange("(t p) f -> p t f", p=P)).then_inc(w_in, 16)
            sp.wait_ge(h_ready, NT)
            sp.dma_start(hx[:, 0:D].rearrange("(t p) d -> p t d", p=P), H[:, :, :]).then_inc(hx_out, 16)
            sp.wait_ge(scT_ready, 1)
            hv = hx[:, D:HROW].rearrange("(s f p) e -> p f s e", f=2, p=P)
            for f in range(2):
                sp.dma_start(hv[:, f, :, :], scT[:, f, :].rearrange("p (s e) -> p s e", e=E_)).then_inc(hx_out, 16)
            av = accum.rearrange("(t p) d -> p t d", p=P)
            for n in range(2 * B):
                sp.wait_ge(so_ready, n + 1)
                sp.dma_start(av[:, 2 * n:2 * n + 2, :], sout[:, n % 2, :].rearrange("p (t d) -> p t d", t=2)).then_inc(so_out[n % 2], 16)
            sp.wait_ge(hx_out, 48)
            for i in range(2):
                sp.wait_ge(so_out[i], 16 * B)

        @block.gpsimd
        def _(pool):
            nc.gpsimd.iota(iot[:, :], pattern=[[1, P]], base=0, channel_multiplier=0).then_inc(pch, 1)
            nc.gpsimd.iota(posi[:, 2, 0:1], pattern=[[0, 1]], base=0, channel_multiplier=1).then_inc(pch, 1)
            nc.gpsimd.memset(gz[:, :, :, :], 0.0).then_inc(pch, 1)
            nc.gpsimd.memset(zero[:, :], 0.0).then_inc(pch, 1)
            nc.gpsimd.iota(bit[:, :], pattern=[[0, 1]], base=1 << ROUNDS, channel_multiplier=0).then_inc(pch, 1)
            nc.gpsimd.memset(T[:, :], 0.0).then_inc(pch, 1)

        @block.scalar
        def _(act):
            a = [0]
            act.wait_ge(varr, 1)
            nc.scalar.activation(sd[:, 1, :], sd[:, 0, :], ACT.Sqrt).then_inc(rootr, 1)
            act.wait_ge(pch, 6)
            act.wait_ge(g_T, 1)
            for s in range(SEG):
                last = nc.scalar.activation(gz[:, :, s, E_ * s:E_ * (s + 1)], bank[7][:, 0:KC * E_].rearrange("p (k e) -> p k e", k=KC), ACT.Copy)
            last.then_inc(g_Te, 1)
            for g in range(0, KC * B, 2):
                act.wait_ge(h_T, g + 1)
                nc.scalar.activation(HT[:, g % KC, (g // KC) * 512:(g // KC + 1) * 512], bank[g % 4][:, :], ACT.Copy).then_inc(h_Te, 1)
            act.wait_ge(s_done, 1)
            nc.scalar.activation(score[:, :], bank[6][:, 0:SEGT], ACT.Sigmoid).then_inc(s_ready, 1)
            act.wait_ge(scT_done, 1)
            nc.scalar.activation(scT[:, :, :].rearrange("p a b -> p (a b)"), bank[5][:, 0:2 * P], ACT.Copy).then_inc(scT_ready, 1)
            for g in range(6):
                act.wait_ge(sw_T, g + 1)
                dst = swT[:, g // 2, g % 2, :] if g < 4 else sdT[:, 2 * (g - 4):2 * (g - 4) + 2, :].rearrange("p f d -> p (f d)")
                nc.scalar.activation(dst, bank[g % 2][:, :], ACT.Copy).then_inc(sw_Te, 1)
            for tg in range(B):
                for ft in range(SF):
                    n = tg * SF + ft
                    act.wait_ge(gu_done, n + 1)
                    if n >= 2:
                        act.wait_ge(hid_ready, n - 1)
                    nc.scalar.activation(sil[:, n % 2, :], bank[n % 2][:, :], ACT.Silu).then_inc(sil_ready, 1)
                for jp in range(2):
                    n = tg * 2 + jp
                    act.wait_ge(dn_done, n + 1)
                    if n >= 2:
                        act.wait_ge(so_out[n % 2], 16 * (n // 2))
                    nc.scalar.activation(sout[:, n % 2, :], bank[4 if n % 2 == 0 else 7][:, :], ACT.Copy).then_inc(so_ready, 1)

        @block.vector
        def _(dve):
            n = [0]

            def link(ins):
                n[0] += 1
                ins.then_inc(vch, 1)
                dve.wait_ge(vch, n[0])

            for i in range(NT):
                last = nc.vector.bn_stats(bnst[:, i, :], X[:, i, :])
            link(last)
            for i in range(NT):
                last = nc.vector.bn_aggr(mv[:, i, :], bnst[:, i, :])
            link(last)
            nc.vector.tensor_scalar(out=sd[:, 0, :], in0=mv[:, :, 1], scalar1=EPS, scalar2=None, op0=ALU.add).then_inc(varr, 1)
            dve.wait_ge(rootr, 1)
            dve.wait_ge(varr, 1)
            link(nc.vector.reciprocal(sd[:, 2, :], sd[:, 1, :]))
            link(nc.vector.tensor_tensor(out=sd[:, 3, :], in0=sd[:, 0, :], in1=sd[:, 2, :], op=ALU.mult))
            link(nc.vector.tensor_tensor(out=sd[:, 2, :], in0=sd[:, 3, :], in1=sd[:, 1, :], op=ALU.add))
            link(nc.vector.tensor_scalar(out=sd[:, 3, :], in0=sd[:, 2, :], scalar1=0.5, scalar2=None, op0=ALU.mult))
            link(nc.vector.reciprocal(sd[:, 2, :], sd[:, 3, :]))
            for i in range(NT):
                nc.vector.tensor_scalar(out=H[:, i, :], in0=X[:, i, :], scalar1=mv[:, i, 0:1], scalar2=sd[:, 2, i:i + 1],
                                        op0=ALU.subtract, op1=ALU.mult).then_inc(h_ready, 1)
            for g in range(1, KC * B, 2):
                dve.wait_ge(h_T, g + 1)
                nc.vector.tensor_copy(HT[:, g % KC, (g // KC) * 512:(g // KC + 1) * 512], bank[g % 4][:, :]).then_inc(c_ready, 1)

            dve.wait_ge(pch, 6)
            link(nc.vector.tensor_copy(v1[:, :], posi[:, 2, 0:1]))
            link(nc.vector.tensor_scalar(out=posi[:, 0, 0:P], in0=iot[:, :], scalar1=15, scalar2=None, op0=ALU.bitwise_and))
            link(nc.vector.tensor_scalar(out=posi[:, 1, 0:P], in0=iot[:, :], scalar1=4, scalar2=None, op0=ALU.logical_shift_right))
            link(nc.vector.tensor_scalar(out=posi[:, 2, 1:2], in0=posi[:, 2, 0:1], scalar1=15, scalar2=None, op0=ALU.bitwise_and))
            link(nc.vector.tensor_scalar(out=posi[:, 2, 2:3], in0=posi[:, 2, 0:1], scalar1=4, scalar2=None, op0=ALU.logical_shift_right))
            link(nc.vector.tensor_copy(T[:, 4:6], posi[:, 2, 1:3]))
            link(nc.vector.tensor_copy(pm[:, 2:4, :], posi[:, 0:2, 0:P]))
            link(nc.vector.tensor_copy(iof[:, :], pm[:, 2, 0:16]))
            link(nc.vector.tensor_scalar(out=pm[:, 0, :], in0=pm[:, 2, :], scalar1=T[:, 4:5], scalar2=None, op0=ALU.is_equal))
            link(nc.vector.scalar_tensor_tensor(out=pm[:, 1, :], in0=pm[:, 3, :], scalar=T[:, 5:6], in1=pm[:, 0, :],
                                                op0=ALU.is_gt, op1=ALU.mult))
            nc.vector.tensor_scalar(out=pm[:, 3, :], in0=pm[:, 3, :], scalar1=T[:, 5:6], scalar2=None, op0=ALU.is_equal).then_inc(masks, 1)

            dve.wait_ge(masks, 1)
            dve.wait_ge(s_ready, 1)
            Ti, Ci = T[:, 0:1].bitcast(I32), T[:, 1:2].bitcast(I32)
            with dve.Fori(0, ROUNDS) as r:
                dve.sem_clear(sch)
                nc.vector.tensor_scalar(out=bit[:, :], in0=bit[:, :], scalar1=1, scalar2=None, op0=ALU.logical_shift_right).then_inc(sch, 1)
                dve.wait_ge(sch, 1)
                nc.vector.tensor_tensor(out=Ci, in0=Ti, in1=bit[:, :], op=ALU.bitwise_or).then_inc(sch, 1)
                dve.wait_ge(sch, 2)
                nc.vector.tensor_scalar(out=junk[:, :], in0=score[:, :], scalar1=T[:, 1:2], scalar2=0.0, op0=ALU.is_ge, op1=ALU.add,
                                        accum_out=cnt[:, 0:1]).then_inc(t_done, 1)
                dve.wait_ge(off_done, r + 1)
                nc.vector.scalar_tensor_tensor(out=T[:, 2:3], in0=bank[6][:, 256:257], scalar=float(CAP), in1=T[:, 1:2],
                                               op0=ALU.is_ge, op1=ALU.mult).then_inc(sch, 1)
                dve.wait_ge(sch, 3)
                nc.vector.tensor_tensor(out=T[:, 0:1], in0=T[:, 0:1], in1=T[:, 2:3], op=ALU.max).then_inc(sch, 1)
                dve.wait_ge(sch, 4)
            nc.vector.tensor_scalar(out=gt[:, :], in0=score[:, :], scalar1=T[:, 0:1], scalar2=0.0, op0=ALU.is_gt, op1=ALU.add,
                                    accum_out=cnt[:, 0:1])
            nc.vector.tensor_scalar(out=eq[:, :], in0=score[:, :], scalar1=T[:, 0:1], scalar2=0.0, op0=ALU.is_equal, op1=ALU.add,
                                    accum_out=cnt[:, 1:2]).then_inc(t_done, 1)
            dve.wait_ge(t_done, ROUNDS + 1)
            nc.vector.tensor_tensor_scan(out=gtc[:, :], data0=gt[:, :], data1=zero[:, :], initial=0.0, op0=ALU.add, op1=ALU.add)
            link(nc.vector.tensor_tensor_scan(out=eqc[:, :], data0=eq[:, :], data1=zero[:, :], initial=0.0, op0=ALU.add, op1=ALU.add))
            dve.wait_ge(off_done, ROUNDS + 1)
            link(nc.vector.tensor_copy(off[:, :], bank[6][:, 264:268]))
            link(nc.vector.tensor_tensor(out=off[:, 1:2], in0=off[:, 1:2], in1=off[:, 2:3], op=ALU.add))
            link(nc.vector.tensor_scalar(out=off[:, 0:2], in0=off[:, 0:2], scalar1=-4097.0, scalar2=None, op0=ALU.add))
            link(nc.vector.scalar_tensor_tensor(out=gtc[:, :], in0=gtc[:, :], scalar=off[:, 0:1], in1=gt[:, :], op0=ALU.add, op1=ALU.mult))
            link(nc.vector.scalar_tensor_tensor(out=eqc[:, :], in0=eqc[:, :], scalar=off[:, 1:2], in1=eq[:, :], op0=ALU.add, op1=ALU.mult))
            nc.vector.scalar_tensor_tensor(out=pos[:, :], in0=gtc[:, :], scalar=4096.0, in1=eqc[:, :], op0=ALU.add, op1=ALU.add)\
                .then_inc(pos_ready, 1)
            dve.wait_ge(pos_T, 1)
            link(nc.vector.tensor_copy(posi[:, 0, :], bank[4][:, 0:2 * P]))
            nc.vector.tensor_scalar(out=posi[:, 1, :], in0=posi[:, 0, :], scalar1=4, scalar2=None, op0=ALU.logical_shift_right)
            link(nc.vector.tensor_scalar(out=posi[:, 2, :], in0=posi[:, 0, :], scalar1=15, scalar2=None, op0=ALU.bitwise_and))
            link(nc.vector.tensor_copy(posf[:, :, :], posi[:, 1:3, :]))
            link(nc.vector.tensor_scalar(out=v0[:, 0:8], in0=iof[:, 0:8], scalar1=2.0, scalar2=None, op0=ALU.mult))
            link(nc.vector.tensor_scalar(out=v0[:, 8:16], in0=v0[:, 0:8], scalar1=1.0, scalar2=None, op0=ALU.add))
            ia = bass.AP(iof[:, :].tensor, iof[:, :].offset, [list(iof[:, :].ap[0]), [0, 2 * P], [1, 16]])
            pa = lambda i: posf[:, i, :].unsqueeze(2).to_broadcast([P, 2 * P, 16])
            nc.vector.tensor_tensor(out=oa[:, :, :], in0=pa(0), in1=ia, op=ALU.is_equal)
            link(nc.vector.tensor_tensor(out=ob[:, 1, :, :], in0=pa(1), in1=ia, op=ALU.is_equal))
            v0b = bass.AP(v0[:, :].tensor, v0[:, :].offset, [list(v0[:, :].ap[0]), [1, 16], [0, E_ * 16]])
            nc.vector.tensor_tensor(out=ob[:, 0, :, :].rearrange("p (c e) b -> p c (e b)", c=16),
                                    in0=ob[:, 1, :, :].rearrange("p (c e) b -> p c (e b)", c=16), in1=v0b, op=ALU.mult).then_inc(oh_ready, 1)
            dve.wait_ge(oh_ready, 1)
            nc.vector.tensor_scalar(out=ob[:, 1, :, :], in0=ob[:, 1, :, :], scalar1=v1[:, 0:1], scalar2=None, op0=ALU.mult).then_inc(oh_ready, 1)
            dve.wait_ge(idl_done, 2)
            for g in range(2):
                link(nc.vector.tensor_copy(idv[:, 0, :], bank[2 + g][:, P:2 * P]))
                link(nc.vector.scalar_tensor_tensor(out=idv[:, 1, :], in0=bank[2 + g][:, 0:P], scalar=float(P), in1=idv[:, 0, :],
                                                    op0=ALU.mult, op1=ALU.add))
                link(nc.vector.tensor_tensor(out=idv[:, 0, :].rearrange("p (e b) -> p e b", e=8),
                                             in0=idv[:, 1, :].rearrange("p (e b) -> p e b", e=8),
                                             in1=pm[:, 3, 0:P].rearrange("p (e b) -> p e b", e=8), op=ALU.mult))
                link(nc.vector.tensor_reduce(out=idl[:, g, :], in_=idv[:, 0, :].rearrange("p (e b) -> p b e", e=8),
                                             axis=mybir.AxisListType.X, op=ALU.add))
                for f in range(2):
                    last = nc.vector.tensor_tensor(out=lsp[:, 2 * g + f, :].rearrange("p (b a) -> p b a", a=16),
                                                   in0=idl[:, g, 8 * f:8 * f + 8].unsqueeze(2).to_broadcast([P, 8, 16]),
                                                   in1=pm[:, 0, :].rearrange("p (b a) -> p b a", a=16), op=ALU.mult)
                link(last)
            nc.vector.tensor_copy(v1[:, :], v0[:, 0:1]).then_inc(lsp_ready, 1)
            dve.wait_ge(ids_done, 1)
            nc.vector.tensor_copy(ids[:, :], bank[1][:, 0:2 * E_]).then_inc(c_ready, 1)
            for m in range(B * SF):
                dve.wait_ge(sil_ready, m + 1)
                if m >= 2 * SF and m % SF == 0:
                    dve.wait_ge(dn_done, 2 * (m // SF - 1))
                nc.vector.tensor_tensor(out=hid[:, (m // SF) % 2, m % SF, :], in0=sil[:, m % 2, :], in1=bank[2 + m % 2][:, :],
                                        op=ALU.mult).then_inc(hid_ready, 1)

        @block.tensor
        def _(pe):
            pe.wait_ge(gw_in, 16)
            for kc in range(KC):
                last = nc.tensor.transpose(bank[7][:, kc * E_:(kc + 1) * E_], gw[:, kc * P:(kc + 1) * P], ident[0:E_, 0:E_])
            last.then_inc(g_T, 1)
            for g in range(KC * B):
                pe.wait_ge(h_ready, (g // KC + 1) * ST)
                if g >= 4:
                    pe.wait_ge((h_Te, c_ready)[g % 2], (g - 4) // 2 + 1)
                for t in range(ST):
                    last = nc.tensor.transpose(bank[g % 4][:, t * P:(t + 1) * P],
                                               H[:, (g // KC) * ST + t, (g % KC) * P:(g % KC + 1) * P], ident[:, :])
                last.then_inc(h_T, 1)
            pe.wait_ge(g_Te, 1)
            pe.wait_ge(h_Te, B)
            pe.wait_ge(c_ready, B)
            for s in range(SEG):
                for kc in range(KC):
                    last = nc.tensor.matmul(bank[6][:, 0:SEGT], gz[:, kc, s, :], HT[:, kc, s * SEGT:(s + 1) * SEGT],
                                            start=(s == 0 and kc == 0), stop=(s == SEG - 1 and kc == KC - 1))
            last.then_inc(s_done, 1)
            pe.wait_ge(masks, 1)
            pe.wait_ge(s_ready, 1)
            for f in range(2):
                last = nc.tensor.transpose(bank[5][:, f * P:(f + 1) * P], score[:, f * P:(f + 1) * P], ident[:, :])
            last.then_inc(scT_done, 1)
            with pe.Fori(0, ROUNDS) as r:
                pe.wait_ge(t_done, r + 1)
                nc.tensor.matmul(bank[6][:, 256:257], pm[:, 0, :], cnt[:, 0:1], start=True, stop=True).then_inc(off_done, 1)
            pe.wait_ge(t_done, ROUNDS + 1)
            nc.tensor.matmul(bank[6][:, 264:266], pm[:, 1, :], cnt[:, :], start=True, stop=True)
            nc.tensor.matmul(bank[6][:, 266:268], pm[:, 0, :], cnt[:, :], start=True, stop=True).then_inc(off_done, 1)
            pe.wait_ge(pos_ready, 1)
            for f in range(2):
                last = nc.tensor.transpose(bank[4][:, f * P:(f + 1) * P], pos[:, f * P:(f + 1) * P], ident[:, :])
            last.then_inc(pos_T, 1)
            pe.wait_ge(oh_ready, 2)
            for g in range(2):
                for c in range(16):
                    lhs = oa[:, c * E_ + 8 * g:c * E_ + 8 * g + 8, :].rearrange("p e a -> p (e a)")
                    rhs = ob[:, :, c * E_ + 8 * g:c * E_ + 8 * g + 8, :].rearrange("p v e b -> p v (e b)")
                    last = nc.tensor.matmul(bank[2 + g][:, 0:2 * P], lhs, rhs, start=(c == 0), stop=(c == 15))
                last.then_inc(idl_done, 1)
            pe.wait_ge(lsp_ready, 1)
            for f in range(2):
                for g in range(2):
                    last = nc.tensor.matmul(bank[1][:, E_ * f + 8 * g:E_ * f + 8 * g + 8], lsp[:, 2 * g + f, :],
                                            pm[:, 3, :].rearrange("p (e a) -> p e a", a=16)[:, :, 0], start=True, stop=True)
            last.then_inc(ids_done, 1)
            pe.wait_ge(w_in, 48)
            pe.wait_ge(c_ready, B + 1)
            for g in range(6):
                if g >= 2:
                    pe.wait_ge(sw_Te, g - 1)
                for t in range(4):
                    if g < 4:
                        src = swn[:, g // 2, t, (g % 2) * P:(g % 2 + 1) * P]
                    else:
                        src = sdn[:, t % 2, (2 * (g - 4) + t // 2) * P:(2 * (g - 4) + t // 2 + 1) * P]
                    last = nc.tensor.transpose(bank[g % 2][:, t * P:(t + 1) * P], src, ident[:, :])
                last.then_inc(sw_T, 1)
            pe.wait_ge(sw_Te, 6)
            for tg in range(B):
                for ft in range(SF):
                    m = tg * SF + ft
                    if m >= 2:
                        pe.wait_ge(sil_ready, m - 1)
                        pe.wait_ge(hid_ready, m - 1)
                    for v in range(2):
                        for kc in range(KC):
                            last = nc.tensor.matmul(bank[2 * v + m % 2][:, :], swT[:, v, kc, ft * P:(ft + 1) * P],
                                                    HT[:, kc, tg * 512:(tg + 1) * 512], start=(kc == 0), stop=(kc == KC - 1))
                    last.then_inc(gu_done, 1)
                pe.wait_ge(hid_ready, (tg + 1) * SF)
                for jp in range(2):
                    m = 2 * tg + jp
                    if m >= 2:
                        pe.wait_ge(so_ready, m - 1)
                    for j in range(2):
                        for ft in range(SF):
                            last = nc.tensor.matmul(bank[4 if m % 2 == 0 else 7][:, j * D:(j + 1) * D],
                                                    hid[:, tg % 2, ft, (2 * jp + j) * P:(2 * jp + j + 1) * P], sdT[:, ft, :],
                                                    start=(ft == 0), stop=(ft == SF - 1))
                    last.then_inc(dn_done, 1)


def run_experts(nc, h):
    ctx = ExitStack()
    with ctx:
        sb = lambda name, shape, dt=F32: ctx.enter_context(nc.sbuf_tensor(name, shape, dt))
        sem = lambda name: ctx.enter_context(nc.semaphore(name))
        two = lambda name: [sem(f"{name}{i}") for i in range(2)]
        ident, ids = h["ident"], h["ids"]
        wn = [sb(f"wn{i}", [P, 2 * FT * D + KC * F]) for i in range(2)]
        wt = [sb(f"wt{i}", [P, 3, KC * F]) for i in range(2)]
        xg = [sb(f"xg{i}", [P, 2, HROW]) for i in range(2)]
        xgT = [sb(f"xgT{i}", [P, KC, CAP]) for i in range(2)]
        bn = sb("bn", [P, 2, P])
        bT = sb("bT", [P, 2, E_ * FT])
        db = [sb(f"db{i}", [P, D]) for i in range(2)]
        sil = sb("silE", [P, 2, CAP])
        hid = sb("hidE", [P, FT, CAP])
        so = sb("so", [P, 2, 2, D])
        tmp = sb("tmpE", [P, 2, D])
        tr = [ctx.enter_context(nc.psum_tensor(f"tr{i}", [P, 512], F32)) for i in range(3)]
        gps = [ctx.enter_context(nc.psum_tensor(f"gps{i}", [P, CAP], F32)) for i in range(2)]
        ups = [ctx.enter_context(nc.psum_tensor(f"ups{i}", [P, CAP], F32)) for i in range(2)]
        ops = ctx.enter_context(nc.psum_tensor("ops", [P, 2, D], F32))
        w_in, x_in, scattered = two("w_inE"), two("x_inE"), two("scattered")
        bn_in, b_T, b_Te = sem("bn_inE"), sem("b_TE"), sem("b_TeE")
        tr_done, tr_free = [sem(f"tr_done{i}") for i in range(3)], [sem(f"tr_free{i}") for i in range(3)]
        ou, so_free = two("output_usedE"), two("so_freeE")
        g_done, u_done, s_rdy, h_rdy, o_done, o_rdy, t_rdy = [sem(n) for n in ("g_doneE", "u_doneE", "s_rdyE", "h_rdyE", "o_doneE", "o_rdyE", "t_rdyE")]
        block = ctx.enter_context(nc.Block())
        NG = 13
        uses = [5, 4, 4]
        WU, WG, WD = 0, FT * D, 2 * FT * D
        hx, accum = h["hx"], h["accum"]
        up_w = h["up_w"].rearrange("e (t p) d -> p e t d", p=P)
        gw = h["gw"].rearrange("e (t p) d -> p e t d", p=P)
        dw = h["down_w"].rearrange("e (t p) f -> p e t f", p=P)
        dbv = bass.AP(h["down_b"].tensor, h["down_b"].offset, [[0, P], [D, E_], [1, D]])
        PAIRS = E_ // 2

        def one(e):
            return bass.ds(e, 1) if not isinstance(e, int) else slice(e, e + 1)

        @block.sync
        def _(sp):
            sp.dma_start(bn[:, 0, :], h["up_b"].rearrange("e (t p) -> (e t) p", p=P)).then_inc(bn_in, 16)
            sp.dma_start(bn[:, 1, :], h["gb"].rearrange("e (t p) -> (e t) p", p=P)).then_inc(bn_in, 16)

            def load(n, k):
                    e = n * 2 + k
                    sp.dma_start(wn[k][:, WU:WG].rearrange("p (o t d) -> p o t d", o=1, t=FT), up_w[:, one(e), :, :]).then_inc(w_in[k], 16)
                    sp.dma_start(wn[k][:, WG:WD].rearrange("p (o t d) -> p o t d", o=1, t=FT), gw[:, one(e), :, :]).then_inc(w_in[k], 16)
                    sp.dma_start(wn[k][:, WD:].rearrange("p (o t f) -> p o t f", o=1, t=KC), dw[:, one(e), :, :]).then_inc(w_in[k], 16)
                    sp.dma_start(db[k][:, :].rearrange("p (o d) -> p o d", o=1), dbv[:, one(e), :]).then_inc(w_in[k], 16)

            for k in range(2):
                load(0, k)
            with sp.Fori(1, PAIRS) as n:
                for k in range(2):
                    sp.wait_ge(tr_done[2], n * 8 + (4 * k - 4))
                    sp.wait_ge(ou[k], n)
                    load(n, k)

        @block.gpsimd
        def _(pool):
            def gather(e):
                k = e % 2
                if e >= 2:
                    pool.wait_ge(ou[k], e // 2)
                for f in range(2):
                    nc.gpsimd.indirect_dma_start(out=xg[k][:, f, :], out_offset=None, in_=hx[:, :],
                                                 in_offset=bass.IndirectOffsetOnAxis(ap=ids[:, E_ * f + e:E_ * f + e + 1], axis=0),
                                                 bounds_check=NTOK - 1).then_inc(x_in[k], 16)

            for k in range(2):
                pool.sem_inc(so_free[k], 1)
            gather(0)
            for e in range(E_):
                k = e % 2
                if e + 1 < E_:
                    gather(e + 1)
                if e:
                    pool.wait_ge(scattered[1 - k], 32 * ((e + 1) // 2))
                    pool.sem_inc(so_free[1 - k], 1)
                pool.wait_ge(o_rdy, 2 * (e + 1))
                for f in range(2):
                    nc.gpsimd.indirect_dma_start(out=accum[:, :],
                                                 out_offset=bass.IndirectOffsetOnAxis(ap=ids[:, E_ * f + e:E_ * f + e + 1], axis=0),
                                                 in_=so[:, k, f, :], in_offset=None, bounds_check=NTOK - 1,
                                                 compute_op=ALU.add).then_inc(scattered[k], 16)
            for k in range(2):
                pool.wait_ge(scattered[k], 32 * PAIRS)

        def sources(q, k):
            if q < 8:
                m, kc, hf = q // 4, (q % 4) // 2, q % 2
                base = (WU, WG)[m]
                return [wn[k][:, base + (4 * hf + t) * D + kc * P:base + (4 * hf + t) * D + (kc + 1) * P] for t in range(4)]
            if q < 12:
                return [wn[k][:, WD + (t % 2) * F + (2 * (q - 8) + t // 2) * P:WD + (t % 2) * F + (2 * (q - 8) + t // 2 + 1) * P] for t in range(4)]
            return [xg[k][:, t % 2, (t // 2) * P:(t // 2 + 1) * P] for t in range(4)]

        def target(q, k):
            if q < 8:
                m, kc, hf = q // 4, (q % 4) // 2, q % 2
                return wt[k][:, m, kc * F + hf * 512:kc * F + (hf + 1) * 512]
            if q < 12:
                return wt[k][:, 2, (q - 8) * 512:(q - 7) * 512]
            return xgT[k][:, :, :].rearrange("p a b -> p (a b)")

        @block.tensor
        def _(pe):
            pe.wait_ge(bn_in, 32)
            for m in range(2):
                last = nc.tensor.transpose(ops[:, 0, m * P:(m + 1) * P], bn[:, m, :], ident[:, :])
            last.then_inc(b_T, 1)

            def transposes(n, k):
                pe.wait_ge(w_in[k], n * 64 + 64)
                for q in range(NG):
                    b = q % 3
                    if q == 12:
                        pe.wait_ge(x_in[k], n * 32 + 32)
                    pe.wait_ge(tr_free[b], n * (2 * uses[b]) + (k * uses[b] + q // 3))
                    for t, s in enumerate(sources(q, k)):
                        last = nc.tensor.transpose(tr[b][:, t * P:(t + 1) * P], s, ident[:, :])
                    last.then_inc(tr_done[b], 1)

            def up_gate(n, k):
                for b in range(3):
                    pe.wait_ge(tr_free[b], n * (2 * uses[b]) + (k + 1) * uses[b])
                for ft in range(FT):
                    for m, (ps, done, taken) in enumerate(((ups, u_done, h_rdy), (gps, g_done, s_rdy))):
                        if ft >= 2:
                            pe.wait_ge(taken, n * (2 * FT) + (k * FT + ft - 1))
                        for kc in range(KC):
                            last = nc.tensor.matmul(ps[ft % 2][:, :], wt[k][:, m, kc * F + ft * P:kc * F + (ft + 1) * P],
                                                    xgT[k][:, kc, :], start=(kc == 0), stop=(kc == KC - 1))
                        last.then_inc(done, 1)

            def down(n, k):
                pe.wait_ge(h_rdy, n * (2 * FT) + (k + 1) * FT)
                for f in range(2):
                    for ft in range(FT):
                        last = nc.tensor.matmul(ops[:, f, :], hid[:, ft, f * P:(f + 1) * P], wt[k][:, 2, ft * D:(ft + 1) * D],
                                                start=(ft == 0), stop=(ft == FT - 1))
                last.then_inc(o_done, 1)

            pe.wait_ge(b_Te, 1)
            transposes(0, 0)
            with pe.Fori(0, PAIRS - 1) as n:
                up_gate(n, 0)
                transposes(n, 1)
                down(n, 0)
                up_gate(n, 1)
                transposes(n + 1, 0)
                down(n, 1)
            n = PAIRS - 1
            up_gate(n, 0)
            transposes(n, 1)
            down(n, 0)
            up_gate(n, 1)
            down(n, 1)

        @block.scalar
        def _(act):
            def take(n, k):
                for q in range(0, NG, 3):
                    act.wait_ge(tr_done[0], n * 10 + (k * 5 + q // 3 + 1))
                    ins = nc.scalar.activation(target(q, k), tr[0][:, :], ACT.Copy)
                    ins.then_inc(tr_free[0], 1)

            def silu(n, k, e):
                for ft in range(FT):
                    act.wait_ge(g_done, n * (2 * FT) + (k * FT + ft + 1))
                    if ft >= 2:
                        act.wait_ge(h_rdy, n * (2 * FT) + (k * FT + ft - 1))
                    nc.scalar.activation(sil[:, ft % 2, :], gps[ft % 2][:, :], ACT.Silu, bias=bT[:, 1, e_col(e, ft)]).then_inc(s_rdy, 1)

            def e_col(e, ft):
                return bass.ds(e * FT + ft, 1) if not isinstance(e, int) else slice(e * FT + ft, e * FT + ft + 1)

            act.wait_ge(b_T, 1)
            nc.scalar.activation(bT[:, :, :].rearrange("p a b -> p (a b)"), ops[:, 0, :], ACT.Copy).then_inc(b_Te, 1)
            act.wait_ge(b_Te, 1)
            take(0, 0)
            with act.Fori(0, PAIRS - 1) as n:
                silu(n, 0, n * 2)
                take(n, 1)
                silu(n, 1, n * 2 + 1)
                take(n + 1, 0)
            n = PAIRS - 1
            silu(n, 0, n * 2)
            take(n, 1)
            silu(n, 1, n * 2 + 1)

        @block.vector
        def _(dve):
            def take(n, k):
                for q in range(NG):
                    if q % 3:
                        dve.wait_ge(tr_done[q % 3], n * 8 + (k * 4 + q // 3 + 1))
                        nc.vector.tensor_copy(target(q, k), tr[q % 3][:, :]).then_inc(tr_free[q % 3], 1)

            def hidden(n, k, e):
                for ft in range(FT):
                    dve.wait_ge(s_rdy, n * (2 * FT) + (k * FT + ft + 1))
                    dve.wait_ge(u_done, n * (2 * FT) + (k * FT + ft + 1))
                    col = bass.ds(e * FT + ft, 1) if not isinstance(e, int) else slice(e * FT + ft, e * FT + ft + 1)
                    nc.vector.scalar_tensor_tensor(out=hid[:, ft, :], in0=ups[ft % 2][:, :], scalar=bT[:, 0, col], in1=sil[:, ft % 2, :],
                                                   op0=ALU.add, op1=ALU.mult).then_inc(h_rdy, 1)

            def output(n, k, e):
                dve.wait_ge(o_done, n * 2 + (k + 1))
                dve.wait_ge(so_free[k], n + 1)
                for f in range(2):
                    nc.vector.tensor_tensor(out=tmp[:, f, :], in0=ops[:, f, :], in1=db[k][:, :], op=ALU.add).then_inc(t_rdy, 1)
                dve.wait_ge(t_rdy, n * 4 + (2 * k + 2))
                for f in range(2):
                    col = bass.ds(e + D, 1) if not isinstance(e, int) else slice(e + D, e + D + 1)
                    nc.vector.tensor_scalar(out=so[:, k, f, :], in0=tmp[:, f, :], scalar1=xg[k][:, f, col], scalar2=None, op0=ALU.mult)\
                        .then_inc(o_rdy, 1)
                dve.wait_ge(o_rdy, n * 4 + (2 * k + 2))
                nc.vector.tensor_copy(tmp[:, 0, 0:1], tmp[:, 1, 0:1]).then_inc(ou[k], 1)

            take(0, 0)
            with dve.Fori(0, PAIRS - 1) as n:
                hidden(n, 0, n * 2)
                take(n, 1)
                output(n, 0, n * 2)
                hidden(n, 1, n * 2 + 1)
                take(n + 1, 0)
                output(n, 1, n * 2 + 1)
            n = PAIRS - 1
            hidden(n, 0, n * 2)
            take(n, 1)
            output(n, 0, n * 2)
            hidden(n, 1, n * 2 + 1)
            output(n, 1, n * 2 + 1)


def finish(nc, h):
    ctx = ExitStack()
    with ctx:
        sem = lambda name: ctx.enter_context(nc.semaphore(name))
        X, tg = h["X"], h["tg"]
        acc = ctx.enter_context(nc.sbuf_tensor("accF", [P, NT, D], F32))
        acc_in = [sem(f"acc_inF{b}") for b in range(B)]
        sums, stored = sem("sumsF"), sem("storedF")
        block = ctx.enter_context(nc.Block())
        av = h["accum"].rearrange("(t p) d -> p t d", p=P)
        ov = h["out"].rearrange("b (t p) d -> p (b t) d", p=P)

        @block.sync
        def _(sp):
            for b in range(B):
                sp.dma_start(acc[:, b * ST:(b + 1) * ST, :], av[:, b * ST:(b + 1) * ST, :]).then_inc(acc_in[b], 16)
            for b in range(B):
                sp.wait_ge(sums, b + 1)
                sp.dma_start(ov[:, b * ST:(b + 1) * ST, :], X[:, b * ST:(b + 1) * ST, :]).then_inc(stored, 16)
            sp.wait_ge(stored, 16 * B)

        @block.vector
        def _(dve):
            for b in range(B):
                dve.wait_ge(acc_in[b], 16)
                r = slice(b * ST, (b + 1) * ST)
                nc.vector.scalar_tensor_tensor(out=X[:, r, :], in0=acc[:, r, :], scalar=tg[:, 1:2], in1=X[:, r, :],
                                               op0=ALU.mult, op1=ALU.add).then_inc(sums, 1)


def build(nc, x, ctx_rows, g_xattn, g_ffn, gate_w, up_w, up_b, gw, gb, down_w, down_b, sh_gate_w, sh_up_w, sh_down_w, out):
    dram = lambda name, shape, dt=F32: nc.dram_tensor(name, shape, dt, kind="Internal").ap()
    h = dict(x=x, ctx=ctx_rows, g_xattn=g_xattn, g_ffn=g_ffn, gate_w=gate_w, up_w=up_w, up_b=up_b, gw=gw, gb=gb, down_w=down_w,
             down_b=down_b, sh_gate_w=sh_gate_w, sh_up_w=sh_up_w, sh_down_w=sh_down_w, out=out)
    h["dd"] = dram("distances", (P, DROWS, CELL))
    h["om"] = dram("on_path", (P, DROWS, MROW), BF16)
    h["hx"] = dram("token_rows", (NTOK, HROW))
    h["accum"] = dram("ffn_sum", (NTOK, D))
    ctx = ExitStack()
    with ctx:
        sb = lambda name, shape, dt=F32: ctx.enter_context(nc.sbuf_tensor(name, shape, dt))
        h["X"] = sb("X", [P, NT, D])
        h["ident"] = sb("ident", [P, P])
        h["identb"] = sb("identb", [P, P], BF16)
        h["first_block"] = sb("first_block", [P, 1])
        h["last_block"] = sb("last_block", [P, 1])
        h["tg"] = sb("tg", [P, 2])
        h["ids"] = sb("ids", [P, 2 * E_], I32)
        with ExitStack() as attend:
            h["C"] = attend.enter_context(nc.sbuf_tensor("C", [P, NT, D], F32))
            prepare_distances(nc, h)
            with ExitStack() as walk:
                h["marks"] = walk.enter_context(nc.sbuf_tensor("marks", [P, STEPS + 2, 3, W], BF16))
                accumulate_costs(nc, h)
                trace_path(nc, h)
            align(nc, h)
        route(nc, h)
        run_experts(nc, h)
        finish(nc, h)


_INS = ['x', 'ctx_1024', 'g_xattn', 'g_ffn', 'L0_ffn_gate_w', 'L0_ffn_up_w', 'L0_ffn_up_b', 'L0_ffn_gw', 'L0_ffn_gb',
        'L0_ffn_down_w', 'L0_ffn_down_b', 'L0_ffn_sh_gate_w', 'L0_ffn_sh_up_w', 'L0_ffn_sh_down_w']
_OUT = (B, S, D)


def kernel(**inputs):
    import numpy as np
    import concourse.bacc as bacc
    from concourse.bass_utils import run_bass_kernel_spmd

    nc = bacc.Bacc("TRN2", target_bir_lowering=False, num_devices=1)
    arrays, args = {}, []
    for name in _INS:
        a = np.ascontiguousarray(inputs[name])
        arrays[f"in_{name}"] = a
        args.append(nc.dram_tensor(f"in_{name}", a.shape, mybir.dt.from_np(a.dtype), kind="ExternalInput").ap())
    args.append(nc.dram_tensor("out_x", _OUT, F32, kind="ExternalOutput").ap())
    build(nc, *args)
    r = run_bass_kernel_spmd(nc, [arrays], core_ids=[0])
    return r.results[0]["out_x"]
```

```python
import concourse.bass as bass
from concourse import mybir
from contextlib import ExitStack

F32 = mybir.dt.float32
BF16 = mybir.dt.bfloat16
I32 = mybir.dt.int32
F16 = mybir.dt.float16
ALU = mybir.AluOpType
ACT = mybir.ActivationFunctionType

P = 128
B, S, D = 4, 512, 256
ST = S // P
NT = B * ST
KC = D // P
NK = 32
W = S // NK
CELL = W + 1
PAD = 32
STEPS = S + NK
HALF = 16
RING = 2 * HALF
CHUNKS = STEPS // RING
DROWS = PAD + S + NK
BIG = 1e30
EPS = 1e-5
TINY = 1e-18

E_, CAP, F = 16, 256, 1024
FT = F // P
SH = 512
SF = SH // P
NTOK = B * S
HROW = D + E_
SEG = 8
SEGT = NTOK // SEG


def prepare_distances(nc, h):
    ctx = ExitStack()
    with ctx:
        sb = lambda name, shape, dt=F32: ctx.enter_context(nc.sbuf_tensor(name, shape, dt))
        sem = lambda name: ctx.enter_context(nc.semaphore(name))
        X = h["X"]
        C = h["C"]
        ident = h["ident"]
        XN = sb("XN", [P, NT, D])
        CT = sb("CT", [P, KC, B, S])
        XT = sb("XT", [P, KC, B, S])
        XSQ = sb("XSQ", [P, KC, B, S])
        junk = sb("junkA", [P, D])
        bnst = sb("bnst", [P, NT, 6])
        mv = sb("mv", [P, NT, 2])
        sd = sb("sd", [P, 4, NT])
        aa = sb("aa", [P, NT])
        bbrow = sb("bbrow", [1, B, S])
        ones = sb("onesA", [P, P])
        d2 = sb("d2", [P, B, S])
        root = sb("root", [P, B, S])
        half_inv = sb("half_inv", [P, B, S])
        dt_ = [sb(f"dt{i}", [P, P, CELL]) for i in range(2)]
        bcol = sb("bcol", [P, 1])
        pidx = sb("pidx", [P, 2], I32)
        zpad = sb("zpad", [P, PAD * CELL])
        lnhalf = sb("lnhalf", [P, 1])
        bank = [ctx.enter_context(nc.psum_tensor(f"pA{i}", [P, 512], F32)) for i in range(8)]

        x_in, c_in, ident_ready, ones_ready = sem("x_in"), sem("c_in"), sem("ident_ready"), sem("ones_readyA")
        c_T, c_Te, x_T, x_Te = sem("c_T"), sem("c_Te"), sem("x_T"), sem("x_Te")
        xn_ready, var_ready, root_ready = sem("xn_ready"), sem("var_ready"), sem("sd_ready")
        aa_ready, sq_ready, bb_done, bb_ready = sem("aa_ready"), sem("sq_ready"), sem("bb_done"), sem("bb_ready")
        d_done, d_evac, inv_ready, newton = sem("d_done"), sem("d_evac"), sem("inv_ready"), sem("newton")
        w_T, w_evA, w_evD, d_out0, d_out1 = sem("w_T"), sem("w_evA"), sem("w_evD"), sem("d_out0"), sem("d_out1")
        zero_ready, pad_out = sem("zero_ready"), sem("pad_out")
        vch, ach, pch = sem("vchA"), sem("achA"), sem("pchA")
        bcol_ready, pidx_ready = sem("bcol_ready"), sem("pidx_ready")
        d_out = [d_out0, d_out1]
        block = ctx.enter_context(nc.Block())

        dd = h["dd"]

        @block.sync
        def _(sp):
            sp.dma_start(C[:, :, :], h["ctx"].rearrange("b (t p) d -> p (b t) d", p=P)).then_inc(c_in, 16)
            sp.wait_ge(zero_ready, 1)
            sp.dma_start(dd[:, 0:PAD, :], zpad[:, :].rearrange("p (r c) -> p r c", c=CELL)).then_inc(pad_out, 16)
            sp.dma_start(dd[:, PAD + S:DROWS, :], zpad[:, :].rearrange("p (r c) -> p r c", c=CELL)).then_inc(pad_out, 16)
            for it in range(ST):
                sp.wait_ge(w_evA, 2 * (it + 1))
                sp.wait_ge(w_evD, 2 * (it + 1))
                sp.dma_start(dd[:, PAD + it * P:PAD + (it + 1) * P, :], dt_[it % 2][:, :, :]).then_inc(d_out[it % 2], 16)
            sp.wait_ge(d_out0, 32)
            sp.wait_ge(d_out1, 32)
            sp.wait_ge(pad_out, 32)

        @block.gpsimd
        def _(pool):
            nc.gpsimd.memset(ident[:, :], 0.0).then_inc(pch, 1)
            pool.wait_ge(pch, 1)
            nc.gpsimd.affine_select(out=ident[:, :], in_=ident[:, :], compare_op=ALU.not_equal, fill=1.0, base=0,
                                    pattern=[[-1, P]], channel_multiplier=1).then_inc(ident_ready, 1)
            nc.gpsimd.memset(ones[:, :], 1.0).then_inc(ones_ready, 1)
            nc.gpsimd.memset(zpad[:, :], 0.0).then_inc(zero_ready, 1)
            nc.gpsimd.iota(pidx[:, 0:1], pattern=[[0, 1]], base=0, channel_multiplier=1).then_inc(pidx_ready, 1)

        @block.scalar
        def _(act):
            act.dma_start(X[:, :, :], h["x"].rearrange("b (t p) d -> p (b t) d", p=P)).then_inc(x_in, 16)
            act.wait_ge(c_in, 16)
            for i in range(NT):
                nc.scalar.activation(junk[:, :], C[:, i, :], ACT.Square, accum_out=aa[:, i:i + 1]).then_inc(ach, 1)
                act.wait_ge(ach, i + 1)
            act.wait_ge(var_ready, 1)
            nc.scalar.activation(sd[:, 1, :], sd[:, 0, :], ACT.Sqrt).then_inc(root_ready, 1)
            for g in range(KC * B):
                act.wait_ge(c_T, g + 1)
                nc.scalar.activation(CT[:, g % KC, g // KC, :], bank[g % 4][:, :], ACT.Copy, scale=-2.0).then_inc(c_Te, 1)
            for g in range(KC * B):
                act.wait_ge(x_Te, g + 1)
                nc.scalar.activation(XSQ[:, g % KC, g // KC, :], XT[:, g % KC, g // KC, :], ACT.Square).then_inc(sq_ready, 1)
            for it in range(ST):
                act.wait_ge(d_evac, 4 * (it + 1))
                nc.scalar.activation(half_inv[:, :, :], d2[:, :, :], ACT.Ln).then_inc(ach, 1)
                act.wait_ge(ach, NT + 2 * it + 1)
                nc.scalar.activation(half_inv[:, :, :], half_inv[:, :, :], ACT.Exp, scale=-0.5, bias=lnhalf[:, :]).then_inc(ach, 1)
                nc.scalar.activation(root[:, :, :], d2[:, :, :], ACT.Sqrt).then_inc(inv_ready, 1)
                for g in (0, 2):
                    act.wait_ge(w_T, 4 * it + g + 1)
                    if g == 0 and it >= 2:
                        act.wait_ge(d_out[it % 2], 16)
                    nc.scalar.activation(dt_[it % 2][:, :, 1 + 4 * g:5 + 4 * g].rearrange("p i w -> p w i"),
                                         bank[g][:, :].rearrange("p (w i) -> p w i", w=4), ACT.Copy).then_inc(w_evA, 1)

        @block.vector
        def _(dve):
            n = [0]

            def link(ins):
                n[0] += 1
                ins.then_inc(vch, 1)
                dve.wait_ge(vch, n[0])

            nc.vector.memset(lnhalf[:, :], -0.6931471805599453)
            dve.wait_ge(pidx_ready, 1)
            link(nc.vector.tensor_scalar(out=pidx[:, 1:2], in0=pidx[:, 0:1], scalar1=NK - 1, scalar2=None, op0=ALU.bitwise_and))
            link(nc.vector.tensor_scalar(out=bcol[:, 0:1], in0=pidx[:, 1:2], scalar1=0.0, scalar2=BIG, op0=ALU.is_equal, op1=ALU.mult))
            link(nc.vector.tensor_scalar(out=h["first_block"][:, :], in0=pidx[:, 1:2], scalar1=0.0, scalar2=None, op0=ALU.is_equal))
            link(nc.vector.tensor_scalar(out=h["not_first"][:, :], in0=pidx[:, 1:2], scalar1=0.0, scalar2=None, op0=ALU.not_equal))
            link(nc.vector.tensor_copy(h["block_id"][:, :], pidx[:, 1:2]))
            link(nc.vector.tensor_scalar(out=h["last_block"][:, :], in0=pidx[:, 1:2], scalar1=float(NK - 1), scalar2=None, op0=ALU.is_equal))
            dve.wait_ge(x_in, 16)
            for i in range(NT):
                last = nc.vector.bn_stats(bnst[:, i, :], X[:, i, :])
            link(last)
            for i in range(NT):
                last = nc.vector.bn_aggr(mv[:, i, :], bnst[:, i, :])
            link(last)
            nc.vector.tensor_scalar(out=sd[:, 0, :], in0=mv[:, :, 1], scalar1=EPS, scalar2=None, op0=ALU.add).then_inc(var_ready, 1)
            dve.wait_ge(root_ready, 1)
            dve.wait_ge(var_ready, 1)
            link(nc.vector.reciprocal(sd[:, 2, :], sd[:, 1, :]))
            link(nc.vector.tensor_tensor(out=sd[:, 3, :], in0=sd[:, 0, :], in1=sd[:, 2, :], op=ALU.mult))
            link(nc.vector.tensor_tensor(out=sd[:, 2, :], in0=sd[:, 3, :], in1=sd[:, 1, :], op=ALU.add))
            link(nc.vector.tensor_scalar(out=sd[:, 3, :], in0=sd[:, 2, :], scalar1=0.5, scalar2=None, op0=ALU.mult))
            link(nc.vector.reciprocal(sd[:, 2, :], sd[:, 3, :]))
            for i in range(NT):
                nc.vector.tensor_scalar(out=XN[:, i, :], in0=X[:, i, :], scalar1=mv[:, i, 0:1], scalar2=sd[:, 2, i:i + 1],
                                        op0=ALU.subtract, op1=ALU.mult).then_inc(xn_ready, 1)
            for g in range(KC * B):
                dve.wait_ge(x_T, g + 1)
                nc.vector.tensor_copy(XT[:, g % KC, g // KC, :], bank[4 + g % 4][:, :]).then_inc(x_Te, 1)
            for b in range(B):
                dve.wait_ge(bb_done, b + 1)
                nc.vector.tensor_copy(bbrow[0:1, b, :], bank[b][0:1, :]).then_inc(bb_ready, 1)
            for it in range(ST):
                if it:
                    dve.wait_ge(w_T, 4 * it)
                for b in range(B):
                    dve.wait_ge(d_done, 4 * it + b + 1)
                    nc.vector.tensor_scalar(out=d2[:, b, :], in0=bank[4 + b][:, :], scalar1=aa[:, b * ST + it:b * ST + it + 1],
                                            scalar2=TINY, op0=ALU.add, op1=ALU.max).then_inc(d_evac, 1)
                dve.wait_ge(inv_ready, it + 1)
                dve.wait_ge(d_evac, 4 * (it + 1))
                link(nc.vector.tensor_tensor(out=XSQ[:, 0, :, :], in0=root[:, :, :], in1=root[:, :, :], op=ALU.mult))
                link(nc.vector.tensor_tensor(out=XSQ[:, 1, :, :], in0=d2[:, :, :], in1=XSQ[:, 0, :, :], op=ALU.subtract))
                link(nc.vector.tensor_tensor(out=XSQ[:, 0, :, :], in0=XSQ[:, 1, :, :], in1=half_inv[:, :, :], op=ALU.mult))
                nc.vector.tensor_tensor(out=root[:, :, :], in0=root[:, :, :], in1=XSQ[:, 0, :, :], op=ALU.add).then_inc(newton, 1)
                if it >= 2:
                    dve.wait_ge(d_out[it % 2], 16)
                nc.vector.tensor_copy(dt_[it % 2][:, :, 0], bcol[:, 0:1].to_broadcast([P, P]))
                for g in (1, 3):
                    dve.wait_ge(w_T, 4 * it + g + 1)
                    last = nc.vector.tensor_copy(dt_[it % 2][:, :, 1 + 4 * g:5 + 4 * g].rearrange("p i w -> p w i"),
                                                 bank[g][:, :].rearrange("p (w i) -> p w i", w=4))
                    last.then_inc(w_evD, 1)

        @block.tensor
        def _(pe):
            pe.wait_ge(ident_ready, 1)
            pe.wait_ge(c_in, 16)
            for g in range(KC * B):
                if g >= 4:
                    pe.wait_ge(c_Te, g - 3)
                for t in range(ST):
                    last = nc.tensor.transpose(bank[g % 4][:, t * P:(t + 1) * P],
                                               C[:, (g // KC) * ST + t, (g % KC) * P:(g % KC + 1) * P], ident[:, :])
                last.then_inc(c_T, 1)
            for g in range(KC * B):
                pe.wait_ge(xn_ready, (g // KC + 1) * ST)
                if g >= 4:
                    pe.wait_ge(x_Te, g - 3)
                for t in range(ST):
                    last = nc.tensor.transpose(bank[4 + g % 4][:, t * P:(t + 1) * P],
                                               XN[:, (g // KC) * ST + t, (g % KC) * P:(g % KC + 1) * P], ident[:, :])
                last.then_inc(x_T, 1)
            pe.wait_ge(ones_ready, 1)
            pe.wait_ge(c_Te, KC * B)
            for b in range(B):
                pe.wait_ge(sq_ready, KC * (b + 1))
                for kc in range(KC):
                    last = nc.tensor.matmul(bank[b][0:1, :], ones[:, 0:1], XSQ[:, kc, b, :], start=(kc == 0), stop=(kc == KC - 1))
                last.then_inc(bb_done, 1)
            pe.wait_ge(bb_ready, B)
            pe.wait_ge(x_Te, KC * B)
            for it in range(ST):
                for b in range(B):
                    if it:
                        pe.wait_ge(d_evac, 4 * (it - 1) + b + 1)
                    for kc in range(KC):
                        nc.tensor.matmul(bank[4 + b][:, :], CT[:, kc, b, it * P:(it + 1) * P], XT[:, kc, b, :],
                                         start=(kc == 0), stop=False)
                    nc.tensor.matmul(bank[4 + b][:, :], ones[0:1, :], bbrow[0:1, b, :], start=False, stop=True).then_inc(d_done, 1)
                pe.wait_ge(newton, it + 1)
                if it:
                    pe.wait_ge(w_evA, 2 * it)
                    pe.wait_ge(w_evD, 2 * it)
                rv = root[:, :, :].rearrange("p b (k w) -> p (b k) w", w=W)
                for w in range(W):
                    last = nc.tensor.transpose(bank[w // 4][:, (w % 4) * P:(w % 4 + 1) * P], rv[:, :, w], ident[:, :])
                    if w % 4 == 3:
                        last.then_inc(w_T, 1)


def accumulate_costs(nc, h):
    ctx = ExitStack()
    with ctx:
        sb = lambda name, shape, dt=F32: ctx.enter_context(nc.sbuf_tensor(name, shape, dt))
        sem = lambda name: ctx.enter_context(nc.semaphore(name))
        GR = 4
        dist = [sb(f"dist{i}", [P, HALF * CELL]) for i in range(2)]
        rows = sb("rowsB", [P, RING + 1, CELL])
        upper = sb("upper", [P, RING, CELL])
        left0 = sb("left0", [P, 1])
        isup = sb("isup", [P, GR, W])
        points = [sb(f"points{i}", [P, W, 2, RING]) for i in range(2)]
        column = [sb(f"column{i}", [P, W, 2, RING]) for i in range(2)]
        leave = [sb(f"leave{i}", [P, W, RING + 1]) for i in range(2)]
        exit_ = sb("exit", [P, W, RING + 1])
        passed = sb("passed", [P, 2, RING])
        dexit_ring = [sb(f"dexit_ring{i}", [P, RING]) for i in range(2)]
        when = sb("when", [P, 2, STEPS])
        when0 = sb("when0", [P, 2, STEPS])
        tch, set_up = sem("tchB"), sem("set_upB")
        dist_in = [sem(f"dist_in{i}") for i in range(2)]
        rows_ready = [sem(f"rows_ready{i}") for i in range(2)]
        points_ready, first_ready, column_ready = sem("points_ready"), sem("first_ready"), sem("column_ready")
        leave_ready, leave_kept, exit_ready, exit_kept = sem("leave_ready"), sem("leave_kept"), sem("exit_ready"), sem("exit_kept")
        dleave, dexit, steps = h["dleave"], h["dexit"], h["steps"]
        dd = h["dd"]
        skew = bass.AP(dd.tensor, dd.offset, [[NK * DROWS * CELL, B], [(DROWS - 1) * CELL, NK], [1, DROWS * CELL]])
        block = ctx.enter_context(nc.Block())

        @block.sync
        def _(sp):
            with sp.Fori(0, CHUNKS) as c:
                for hf in range(2):
                    sp.wait_ge(rows_ready[hf], c + 1)
                    sp.dma_start(dist[hf][:, :], skew[:, :, bass.ds((c * RING + (PAD + hf * HALF)) * CELL, HALF * CELL)])\
                        .then_inc(dist_in[hf], 16)

        @block.vector
        def _(dve):
            def mark(c_par, slot):
                g, part = (slot // 8 - 1) % (RING // GR), slot % 8
                lo = g * GR
                pt = points[1 - c_par if slot < 8 else c_par]
                diag, up, left = rows[:, lo:lo + GR, 0:W], rows[:, lo:lo + GR, 1:CELL], rows[:, lo + 1:lo + 1 + GR, 0:W]
                out = lambda s: pt[:, :, s, lo:lo + GR].rearrange("p w t -> p t w")
                if part == 0:
                    nc.vector.tensor_tensor(out=isup[:, :, :], in0=up, in1=diag, op=ALU.is_lt)
                if part == 1:
                    nc.vector.tensor_tensor(out=out(0), in0=left, in1=upper[:, lo:lo + GR, 1:CELL], op=ALU.is_lt)
                if part == 3:
                    nc.vector.scalar_tensor_tensor(out=out(1), in0=isup[:, :, :], scalar=0.5, in1=out(0), op0=ALU.is_lt, op1=ALU.is_gt)

            def leave_block(c, c_par, slot):
                x = (slot - 8) % 64
                pt = points[1 - c_par if slot >= 8 else c_par]
                w, part = x // 4, x % 4
                if x == 0:
                    dve.wait_ge(exit_kept, c + 1)
                    nc.vector.tensor_tensor(out=dexit_ring[c_par][:, :], in0=exit_[:, W - 1, 1:RING + 1], in1=exit_[:, W - 1, 0:RING], op=ALU.subtract)
                    nc.vector.tensor_copy(exit_[:, 0:W - 1, 0], exit_[:, 0:W - 1, RING])
                elif x == 2:
                    dve.wait_ge(first_ready, c + 1)
                    col = column[1 - c_par]
                    nc.vector.tensor_tensor_scan(out=exit_[:, 0, 1:RING + 1], data0=col[:, 0, 0, :], data1=col[:, 0, 1, :],
                                                 initial=exit_[:, 0, 0:1], op0=ALU.max, op1=ALU.max)
                elif x == 5:
                    nc.vector.tensor_copy(exit_[:, W - 1:W, 0], exit_[:, W - 1:W, RING])
                elif w >= 1 and part == 0:
                    src = exit_[:, w - 1, 1:RING + 1]
                    nc.vector.tensor_tensor(out=passed[:, :, :], in0=pt[:, w, :, :],
                                            in1=bass.AP(src.tensor, src.offset, [list(src.ap[0]), [-1, 2], [1, RING]]), op=ALU.mult)
                elif w >= 1 and part == 2:
                    nc.vector.tensor_tensor_scan(out=exit_[:, w, 1:RING + 1], data0=passed[:, 0, :], data1=passed[:, 1, :],
                                                 initial=exit_[:, w, 0:1], op0=ALU.max, op1=ALU.max)

            def leave_column(c, c_par, slot):
                x = (slot - 17) % 64
                new = 1 - c_par if slot >= 17 else c_par
                if slot == 15:
                    dve.wait_ge(leave_kept, c + 1)
                    nc.vector.tensor_copy(leave[1 - c_par][:, :, 0], leave[c_par][:, :, RING])
                if x % 4:
                    return
                if x == 0:
                    dve.wait_ge(column_ready, c + 1)
                w = x // 4
                nc.vector.tensor_tensor_scan(out=leave[new][:, w, 1:RING + 1], data0=column[new][:, w, 0, :], data1=column[new][:, w, 1, :],
                                             initial=leave[new][:, w, 0:1], op0=ALU.max, op1=ALU.max)

            def aside(c, c_par, slot):
                mark(c_par, slot)
                if slot == 5:
                    nc.vector.tensor_copy(rows[:, 0, :], rows[:, RING, :])
                leave_block(c, c_par, slot)
                leave_column(c, c_par, slot)

            from_left = [(p - 1) % NK for p in range(NK)]

            def chunk(c, c_par):
                dve.sem_clear(tch)
                for u in range(RING):
                    hf = u // HALF
                    cur, prev = rows[:, u + 1, :], rows[:, u if u else RING, :]
                    shuffle = nc.vector.stream_shuffle(left0[:, :], prev[:, W:CELL], from_left)
                    if u % HALF == 0:
                        shuffle.then_inc(rows_ready[1 - hf], 1)
                    if u == 3:
                        shuffle.then_inc(points_ready, 1)
                    if u == 5:
                        shuffle.then_inc(exit_ready, 1)
                    if u == 8:
                        shuffle.then_inc(leave_ready, 1)
                    nc.vector.tensor_tensor(out=upper[:, u, 1:CELL], in0=prev[:, 0:W], in1=prev[:, 1:CELL], op=ALU.min).then_inc(tch, 1)
                    aside(c, c_par, 2 * u)
                    if u % HALF == 0:
                        dve.wait_ge(dist_in[hf], c * 16 + 16)
                    dve.wait_ge(tch, 2 * u + 1)
                    nc.vector.tensor_tensor_scan(out=cur, data0=upper[:, u, :], data1=dist[hf][:, (u % HALF) * CELL:(u % HALF + 1) * CELL],
                                                 initial=left0[:, :], op0=ALU.min, op1=ALU.add).then_inc(tch, 1)
                    aside(c, c_par, 2 * u + 1)
                    dve.wait_ge(tch, 2 * u + 2)

            nc.vector.memset(rows[:, :, :], BIG)
            for i in range(2):
                nc.vector.memset(points[i][:, :, :, :], 0.0)
                nc.vector.memset(leave[i][:, :, :], 0.0)
            nc.vector.memset(exit_[:, :, :], 0.0)
            nc.vector.memset(upper[:, :, :], BIG).then_inc(tch, 1)
            dve.wait_ge(tch, 1)
            nc.vector.tensor_scalar(out=rows[:, RING, 0:1], in0=h["first_block"][:, :], scalar1=-BIG, scalar2=BIG,
                                    op0=ALU.mult, op1=ALU.add).then_inc(tch, 1)
            dve.wait_ge(tch, 2)
            dve.wait_ge(set_up, 3)
            dve.sem_inc(rows_ready[0], 1)
            with dve.Fori(0, CHUNKS // 2) as n:
                for c_par in range(2):
                    chunk(n * 2 + c_par, c_par)
            chunk(CHUNKS - 1, 0)
            dve.sem_clear(tch)
            n = 0
            for c, slots in (CHUNKS, 64), (CHUNKS + 1, 14):
                for slot in range(slots):
                    if slot % 2 and slot % 4 == 3 and slot not in (3, 15):
                        continue
                    if c == CHUNKS:
                        aside(c, c % 2, slot)
                    else:
                        if slot <= 8:
                            leave_block(c, c % 2, slot)
                        leave_column(c, c % 2, slot)
                    n += 1
                    nc.vector.tensor_copy(left0[:, :], upper[:, 0, 0:1]).then_inc(tch, 1)
                    dve.wait_ge(tch, n)
                    if (c, slot) == (CHUNKS, 4):
                        dve.sem_inc(points_ready, 1)
                    if slot == 8:
                        dve.sem_inc(exit_ready, 1)
                    if slot == 13:
                        dve.sem_inc(leave_ready, 1)

        @block.scalar
        def _(act):
            act.sem_inc(exit_kept, 4)
            with act.Fori(0, CHUNKS // 2) as n:
                for c_par in range(2):
                    act.wait_ge(exit_ready, n * 2 + (c_par + 3))
                    nc.scalar.activation(dexit[:, bass.ds(n * (2 * RING) + c_par * RING, RING)], dexit_ring[c_par][:, :], ACT.Copy).then_inc(exit_kept, 1)
            act.wait_ge(exit_ready, CHUNKS + 2)
            nc.scalar.activation(dexit[:, (CHUNKS - 1) * RING:], dexit_ring[0][:, :], ACT.Copy).then_inc(exit_kept, 1)

        @block.gpsimd
        def _(pool):
            nc.gpsimd.iota(steps[:, :], pattern=[[1, STEPS]], base=0, channel_multiplier=0,
                           allow_small_or_imprecise_dtypes=True).then_inc(set_up, 1)
            for i in range(2):
                nc.gpsimd.memset(column[i][:, :, :, :], 0.0).then_inc(set_up, 1)
            pool.wait_ge(set_up, 3)
            nc.gpsimd.tensor_scalar(out=when[:, 0, :], in0=steps[:, :], scalar1=0.0, scalar2=None, op0=ALU.add).then_inc(set_up, 1)
            nc.gpsimd.tensor_scalar(out=when[:, 1, :], in0=steps[:, :], scalar1=-0.75, scalar2=None, op0=ALU.add).then_inc(set_up, 1)
            pool.wait_ge(set_up, 5)
            nc.gpsimd.tensor_scalar(out=when0[:, :, :], in0=when[:, :, :], scalar1=h["not_first"][:, :], scalar2=None, op0=ALU.mult).then_inc(set_up, 1)
            pool.wait_ge(set_up, 6)
            pool.sem_inc(first_ready, 1)
            pool.sem_inc(column_ready, 1)
            pool.sem_inc(leave_kept, 2)

            def entries(c, c_par):
                pool.wait_ge(points_ready, c + 2)
                at = lambda tab: tab[:, :, bass.ds(c * RING, RING)]
                nc.gpsimd.tensor_tensor(out=column[c_par][:, 0, :, :], in0=points[c_par][:, 0, :, :], in1=at(when0), op=ALU.mult).then_inc(first_ready, 1)
                nc.gpsimd.tensor_tensor(out=column[c_par][:, 1:W, :, :], in0=points[c_par][:, 1:W, :, :],
                                        in1=at(when).unsqueeze(1).to_broadcast([P, W - 1, 2, RING]), op=ALU.mult).then_inc(column_ready, 1)

            def keep(c, c_par):
                pool.wait_ge(leave_ready, c + 3)
                nc.gpsimd.tensor_tensor(out=dleave[:, :, bass.ds(c * RING + RING, RING)], in0=leave[c_par][:, :, 1:RING + 1],
                                        in1=leave[c_par][:, :, 0:RING], op=ALU.subtract).then_inc(leave_kept, 1)

            with pool.Fori(0, CHUNKS // 2) as n:
                for c_par in range(2):
                    entries(n * 2 + c_par, c_par)
                    keep(n * 2 + (c_par - 1), 1 - c_par)
            entries(CHUNKS - 1, 0)
            keep(CHUNKS - 2, 1)
            keep(CHUNKS - 1, 0)


def trace_path(nc, h):
    ctx = ExitStack()
    with ctx:
        sb = lambda name, shape, dt=F32: ctx.enter_context(nc.sbuf_tensor(name, shape, dt))
        sem = lambda name: ctx.enter_context(nc.semaphore(name))
        dleave, dexit, steps = h["dleave"], h["dexit"], h["steps"]
        step1 = sb("step1", [P, STEPS])
        junk = sb("junkC", [P, STEPS])
        last, not_last = h["last_block"], sb("not_last", [P, 1])
        entry = sb("entry", [P, 1])
        found = sb("found", [P, 2])
        at = sb("at", [P, W + 1])
        ati = sb("ati", [P, W + 1], I32)
        atf = sb("atf", [P, W + 1])
        span = sb("span", [P, 2, W], F16)
        tch, span_ready, span_out = sem("tchC"), sem("span_ready"), sem("span_out")
        block = ctx.enter_context(nc.Block())

        @block.vector
        def _(dve):
            n = [0]

            def link(ins):
                n[0] += 1
                ins.then_inc(tch, 1)
                dve.wait_ge(tch, n[0])

            def look(out, steps_, e, table):
                link(nc.vector.scalar_tensor_tensor(out=junk[:, :], in0=steps_, scalar=e, in1=table, op0=ALU.is_le, op1=ALU.mult, accum_out=out))

            nc.vector.memset(entry[:, :], float(STEPS - 1))
            nc.vector.tensor_scalar(out=not_last[:, :], in0=last[:, :], scalar1=-1.0, scalar2=1.0, op0=ALU.mult, op1=ALU.add)
            link(nc.vector.tensor_scalar(out=step1[:, :], in0=steps[:, :], scalar1=1.0, scalar2=None, op0=ALU.add))
            look(found[:, 0:1], step1[:, :], entry[:, :], dexit[:, :])
            link(nc.vector.tensor_scalar(out=dexit[:, :], in0=dexit[:, :], scalar1=not_last[:, :], scalar2=None, op0=ALU.mult))
            link(nc.vector.scalar_tensor_tensor(out=dexit[:, 0:1], in0=found[:, 0:1], scalar=last[:, :], in1=dexit[:, 0:1], op0=ALU.mult, op1=ALU.add))
            from_right = [min(k + 1, NK - 1) for k in range(NK)]
            with dve.Fori(0, NK - 1) as _:
                dve.sem_clear(tch)
                nc.vector.stream_shuffle(entry[:, :], found[:, 0:1], from_right).then_inc(tch, 1)
                dve.wait_ge(tch, 1)
                nc.vector.scalar_tensor_tensor(out=junk[:, :], in0=step1[:, :], scalar=entry[:, :], in1=dexit[:, :], op0=ALU.is_le,
                                               op1=ALU.mult, accum_out=found[:, 0:1]).then_inc(tch, 1)
                dve.wait_ge(tch, 2)
            dve.sem_clear(tch)
            n[0] = 0
            link(nc.vector.tensor_scalar(out=entry[:, :], in0=entry[:, :], scalar1=not_last[:, :], scalar2=None, op0=ALU.mult))
            link(nc.vector.scalar_tensor_tensor(out=entry[:, :], in0=last[:, :], scalar=float(STEPS - 1), in1=entry[:, :], op0=ALU.mult, op1=ALU.add))
            link(nc.vector.tensor_scalar(out=at[:, W:W + 1], in0=entry[:, :], scalar1=-1.0, scalar2=None, op0=ALU.add))
            for w in reversed(range(W)):
                look(at[:, w:w + 1], steps[:, :], at[:, w + 1:w + 2], dleave[:, w, RING:])
            link(nc.vector.tensor_copy(ati[:, :], at[:, :]))
            link(nc.vector.tensor_copy(atf[:, :], ati[:, :]))
            link(nc.vector.tensor_tensor(out=at[:, :], in0=at[:, :], in1=atf[:, :], op=ALU.subtract))
            link(nc.vector.scalar_tensor_tensor(out=at[:, :], in0=at[:, :], scalar=4.0, in1=atf[:, :], op0=ALU.mult, op1=ALU.add))
            nc.vector.tensor_scalar(out=span[:, 0, :], in0=at[:, 0:W], scalar1=h["block_id"][:, :], scalar2=None, op0=ALU.subtract)
            nc.vector.tensor_scalar(out=span[:, 1, :], in0=atf[:, 1:W + 1], scalar1=h["block_id"][:, :], scalar2=None, op0=ALU.subtract)\
                .then_inc(span_ready, 1)

        @block.sync
        def _(sp):
            sp.wait_ge(span_ready, 1)
            sp.dma_start(h["spans"].rearrange("s p w -> p s w"), span[:, :, :]).then_inc(span_out, 16)
            sp.wait_ge(span_out, 16)


def align(nc, h):
    ctx = ExitStack()
    with ctx:
        sb = lambda name, shape, dt=F32: ctx.enter_context(nc.sbuf_tensor(name, shape, dt))
        sem = lambda name: ctx.enter_context(nc.semaphore(name))
        X, C = h["X"], h["C"]
        span = sb("spanD", [P, 2, B * S], F16)
        begun = sb("begun", [P, 2, B * S], F16)
        path = sb("path", [P, ST, B * S])
        row = sb("row_id", [P, ST])
        g = sb("gD", [P, 2])
        tg = h["tg"]
        acc = [ctx.enter_context(nc.psum_tensor(f"aD{i}", [P, 2 * D], F32)) for i in range(8)]
        span_in, row_ready, g_in, tg_ready = sem("span_in"), sem("row_ready"), sem("g_in"), sem("tg_ready")
        begun_ready, path_ready, sums = sem("begun_ready"), sem("path_ready"), sem("sums")
        block = ctx.enter_context(nc.Block())

        @block.sync
        def _(sp):
            sv = h["spans"].rearrange("s p w -> (s p w)")
            sp.dma_start(span[:, :, :].rearrange("p s j -> p (s j)"), bass.AP(sv.tensor, sv.offset, [[0, P], [1, 2 * B * S]])).then_inc(span_in, 16)
            sp.dma_start(g[:, 0:1], bass.AP(h["g_xattn"].tensor, h["g_xattn"].offset, [[0, P], [1, 1]])).then_inc(g_in, 16)
            sp.dma_start(g[:, 1:2], bass.AP(h["g_ffn"].tensor, h["g_ffn"].offset, [[0, P], [1, 1]])).then_inc(g_in, 16)

        @block.gpsimd
        def _(pool):
            nc.gpsimd.iota(row[:, :], pattern=[[P, ST]], base=0, channel_multiplier=1, allow_small_or_imprecise_dtypes=True).then_inc(row_ready, 1)

        @block.scalar
        def _(act):
            act.wait_ge(g_in, 32)
            nc.scalar.activation(tg[:, :], g[:, :], ACT.Tanh).then_inc(tg_ready, 1)

        @block.vector
        def _(dve):
            dve.wait_ge(row_ready, 1)
            dve.wait_ge(span_in, 16)
            for it in range(ST):
                nc.vector.tensor_scalar(out=begun[:, it % 2, :], in0=span[:, 0, :], scalar1=row[:, it:it + 1], scalar2=None, op0=ALU.is_le).then_inc(begun_ready, 1)
                dve.wait_ge(begun_ready, it + 1)
                nc.vector.scalar_tensor_tensor(out=path[:, it, :], in0=span[:, 1, :], scalar=row[:, it:it + 1], in1=begun[:, it % 2, :],
                                               op0=ALU.is_ge, op1=ALU.mult).then_inc(path_ready, 1)
            dve.wait_ge(tg_ready, 1)
            for n in range(2 * B):
                dve.wait_ge(sums, n + 1)
                for j in range(2):
                    nc.vector.scalar_tensor_tensor(out=X[:, 2 * n + j, :], in0=acc[n][:, j * D:(j + 1) * D], scalar=tg[:, 0:1],
                                                   in1=X[:, 2 * n + j, :], op0=ALU.mult, op1=ALU.add)

        @block.tensor
        def _(pe):
            for n in range(2 * B):
                b, jp = n // 2, n % 2
                for j in range(2):
                    jt = 2 * jp + j
                    for it in range(ST):
                        if n == 0 and j == 0:
                            pe.wait_ge(path_ready, it + 1)
                        last = nc.tensor.matmul(acc[n][:, j * D:(j + 1) * D], path[:, it, b * S + jt * P:b * S + (jt + 1) * P],
                                                C[:, b * ST + it, :], start=(it == 0), stop=(it == ST - 1))
                last.then_inc(sums, 1)


def route(nc, h):
    ctx = ExitStack()
    with ctx:
        sb = lambda name, shape, dt=F32: ctx.enter_context(nc.sbuf_tensor(name, shape, dt))
        sem = lambda name: ctx.enter_context(nc.semaphore(name))
        X, ident, ids = h["X"], h["ident"], h["ids"]
        H = sb("H", [P, NT, D])
        HT = sb("HT", [P, KC, NTOK])
        bnst = sb("bnstR", [P, NT, 6])
        mv = sb("mvR", [P, NT, 2])
        sd = sb("sdR", [P, 4, NT])
        gw = sb("gwR", [E_, D])
        gz = sb("gz", [P, KC, SEG, P])
        swn = sb("swn", [P, 2, SF, D])
        sdn = sb("sdn", [P, KC, SH])
        swT = sb("swT", [P, 2, KC, SH])
        sdT = sb("sdT", [P, SF, D])
        sil = sb("sil", [P, 2, 512])
        hid = sb("hid", [P, 2, SF, 512])
        sout = sb("sout", [P, 2, 2 * D])
        score = sb("score", [P, SEGT])
        scT = sb("scT", [P, 2, P])
        junk = sb("junkR", [P, SEGT])
        T = sb("T", [P, 8])
        bit = sb("bit", [P, 1], I32)
        cnt = sb("cnt", [P, 2])
        off = sb("off", [P, 4])
        gt, eq = sb("gt", [P, SEGT]), sb("eq", [P, SEGT])
        gtc, eqc = sb("gtc", [P, SEGT]), sb("eqc", [P, SEGT])
        zero = sb("zeroR", [P, SEGT])
        pos = sb("pos", [P, SEGT])
        posi = sb("posi", [P, 3, 2 * P], I32)
        posf = sb("posf", [P, 2, 2 * P])
        iot = sb("iot", [P, P], I32)
        iof = sb("iof", [P, 16])
        v0 = sb("v0", [P, 16])
        v1 = sb("v1", [P, 1])
        pm = sb("pm", [P, 4, P])
        oa = sb("oa", [P, 2 * P, 16], BF16)
        ob = sb("ob", [P, 2, 2 * P, 16], BF16)
        idv = sb("idv", [P, 2, P])
        idl = sb("idl", [P, 2, 16])
        lsp = sb("lsp", [P, 4, P])
        bank = [ctx.enter_context(nc.psum_tensor(f"pR{i}", [P, 512], F32)) for i in range(8)]

        w_in, gw_in, sdn_in = sem("w_inR"), sem("gw_inR"), sem("sdn_inR")
        varr, rootr, h_ready = sem("varR"), sem("rootR"), sem("h_readyR")
        h_T, h_Te, g_T, g_Te = sem("h_TR"), sem("h_TeR"), sem("g_TR"), sem("g_TeR")
        s_done, s_ready, c_ready, t_done = sem("s_doneR"), sem("s_readyR"), sem("c_readyR"), sem("t_doneR")
        masks, pos_ready, pos_T, oh_ready, idl_done = sem("masksR"), sem("pos_readyR"), sem("pos_TR"), sem("oh_readyR"), sem("idl_doneR")
        scT_done, scT_ready, lsp_ready, ids_done, off_done = sem("scT_doneR"), sem("scT_readyR"), sem("lsp_readyR"), sem("ids_doneR"), sem("off_doneR")
        sw_T, sw_Te, gu_done, sil_ready, hid_ready, dn_done, so_ready = [sem(n) for n in (
            "sw_TR", "sw_TeR", "gu_doneR", "sil_readyR", "hid_readyR", "dn_doneR", "so_readyR")]
        so_out = [sem(f"so_outR{i}") for i in range(2)]
        hx_out = sem("hx_outR")
        vch, ach, pch, sch = sem("vchR"), sem("achR"), sem("pchR"), sem("schR")
        hx, accum = h["hx"], h["accum"]
        PIECES = [("weights", g) for g in range(6)]
        for m in range(B * SF):
            PIECES.append(("gate_up", m))
            if m >= SF and m % SF < 2:
                PIECES.append(("down", 2 * (m // SF - 1) + m % SF))
        PIECES += [("down", 2 * B - 2), ("down", 2 * B - 1)]
        ROUNDS = len(PIECES)
        assert ROUNDS == 30
        block = ctx.enter_context(nc.Block())

        @block.sync
        def _(sp):
            sp.dma_start(gw[:, :], h["gate_w"]).then_inc(gw_in, 16)
            sp.dma_start(swn[:, 0, :, :], h["sh_gate_w"].rearrange("(t p) d -> p t d", p=P)).then_inc(w_in, 16)
            sp.dma_start(swn[:, 1, :, :], h["sh_up_w"].rearrange("(t p) d -> p t d", p=P)).then_inc(w_in, 16)
            sp.dma_start(sdn[:, :, :], h["sh_down_w"].rearrange("(t p) f -> p t f", p=P)).then_inc(w_in, 16)
            sp.wait_ge(h_ready, NT)
            sp.dma_start(hx[:, 0:D].rearrange("(t p) d -> p t d", p=P), H[:, :, :]).then_inc(hx_out, 16)
            sp.wait_ge(scT_ready, 1)
            hv = hx[:, D:HROW].rearrange("(s f p) e -> p f s e", f=2, p=P)
            for f in range(2):
                sp.dma_start(hv[:, f, :, :], scT[:, f, :].rearrange("p (s e) -> p s e", e=E_)).then_inc(hx_out, 16)
            av = accum.rearrange("(t p) d -> p t d", p=P)
            for n in range(2 * B):
                sp.wait_ge(so_ready, n + 1)
                sp.dma_start(av[:, 2 * n:2 * n + 2, :], sout[:, n % 2, :].rearrange("p (t d) -> p t d", t=2)).then_inc(so_out[n % 2], 16)
            sp.wait_ge(hx_out, 48)
            for i in range(2):
                sp.wait_ge(so_out[i], 16 * B)

        @block.gpsimd
        def _(pool):
            nc.gpsimd.iota(iot[:, :], pattern=[[1, P]], base=0, channel_multiplier=0).then_inc(pch, 1)
            nc.gpsimd.iota(posi[:, 2, 0:1], pattern=[[0, 1]], base=0, channel_multiplier=1).then_inc(pch, 1)
            nc.gpsimd.memset(gz[:, :, :, :], 0.0).then_inc(pch, 1)
            nc.gpsimd.memset(zero[:, :], 0.0).then_inc(pch, 1)
            nc.gpsimd.iota(bit[:, :], pattern=[[0, 1]], base=1 << ROUNDS, channel_multiplier=0).then_inc(pch, 1)
            nc.gpsimd.memset(T[:, :], 0.0).then_inc(pch, 1)

        @block.scalar
        def _(act):
            a = [0]
            act.wait_ge(varr, 1)
            nc.scalar.activation(sd[:, 1, :], sd[:, 0, :], ACT.Sqrt).then_inc(rootr, 1)
            act.wait_ge(pch, 6)
            act.wait_ge(g_T, 1)
            for s in range(SEG):
                last = nc.scalar.activation(gz[:, :, s, E_ * s:E_ * (s + 1)], bank[7][:, 0:KC * E_].rearrange("p (k e) -> p k e", k=KC), ACT.Copy)
            last.then_inc(g_Te, 1)
            for g in range(0, KC * B, 2):
                act.wait_ge(h_T, g + 1)
                nc.scalar.activation(HT[:, g % KC, (g // KC) * 512:(g // KC + 1) * 512], bank[g % 4][:, :], ACT.Copy).then_inc(h_Te, 1)
            act.wait_ge(s_done, 1)
            nc.scalar.activation(score[:, :], bank[6][:, 0:SEGT], ACT.Sigmoid).then_inc(s_ready, 1)
            act.wait_ge(scT_done, 1)
            nc.scalar.activation(scT[:, :, :].rearrange("p a b -> p (a b)"), bank[5][:, 0:2 * P], ACT.Copy).then_inc(scT_ready, 1)
            for kind, m in PIECES:
                if kind == "weights":
                    act.wait_ge(sw_T, m + 1)
                    dst = swT[:, m // 2, m % 2, :] if m < 4 else sdT[:, 2 * (m - 4):2 * (m - 4) + 2, :].rearrange("p f d -> p (f d)")
                    nc.scalar.activation(dst, bank[m % 2][:, :], ACT.Copy).then_inc(sw_Te, 1)
                if kind == "gate_up":
                    act.wait_ge(gu_done, m + 1)
                    if m >= 2:
                        act.wait_ge(hid_ready, m - 1)
                    nc.scalar.activation(sil[:, m % 2, :], bank[m % 2][:, :], ACT.Silu).then_inc(sil_ready, 1)
                if kind == "down":
                    act.wait_ge(dn_done, m + 1)
                    if m >= 2:
                        act.wait_ge(so_out[m % 2], 16 * (m // 2))
                    nc.scalar.activation(sout[:, m % 2, :], bank[4 if m % 2 == 0 else 7][:, :], ACT.Copy).then_inc(so_ready, 1)

        @block.vector
        def _(dve):
            n = [0]

            def link(ins):
                n[0] += 1
                ins.then_inc(vch, 1)
                dve.wait_ge(vch, n[0])

            for i in range(NT):
                last = nc.vector.bn_stats(bnst[:, i, :], X[:, i, :])
            link(last)
            for i in range(NT):
                last = nc.vector.bn_aggr(mv[:, i, :], bnst[:, i, :])
            link(last)
            nc.vector.tensor_scalar(out=sd[:, 0, :], in0=mv[:, :, 1], scalar1=EPS, scalar2=None, op0=ALU.add).then_inc(varr, 1)
            dve.wait_ge(rootr, 1)
            dve.wait_ge(varr, 1)
            link(nc.vector.reciprocal(sd[:, 2, :], sd[:, 1, :]))
            link(nc.vector.tensor_tensor(out=sd[:, 3, :], in0=sd[:, 0, :], in1=sd[:, 2, :], op=ALU.mult))
            link(nc.vector.tensor_tensor(out=sd[:, 2, :], in0=sd[:, 3, :], in1=sd[:, 1, :], op=ALU.add))
            link(nc.vector.tensor_scalar(out=sd[:, 3, :], in0=sd[:, 2, :], scalar1=0.5, scalar2=None, op0=ALU.mult))
            link(nc.vector.reciprocal(sd[:, 2, :], sd[:, 3, :]))
            for i in range(NT):
                nc.vector.tensor_scalar(out=H[:, i, :], in0=X[:, i, :], scalar1=mv[:, i, 0:1], scalar2=sd[:, 2, i:i + 1],
                                        op0=ALU.subtract, op1=ALU.mult).then_inc(h_ready, 1)
            for g in range(1, KC * B, 2):
                dve.wait_ge(h_T, g + 1)
                nc.vector.tensor_copy(HT[:, g % KC, (g // KC) * 512:(g // KC + 1) * 512], bank[g % 4][:, :]).then_inc(c_ready, 1)

            dve.wait_ge(pch, 6)
            link(nc.vector.tensor_copy(v1[:, :], posi[:, 2, 0:1]))
            link(nc.vector.tensor_scalar(out=posi[:, 0, 0:P], in0=iot[:, :], scalar1=15, scalar2=None, op0=ALU.bitwise_and))
            link(nc.vector.tensor_scalar(out=posi[:, 1, 0:P], in0=iot[:, :], scalar1=4, scalar2=None, op0=ALU.logical_shift_right))
            link(nc.vector.tensor_scalar(out=posi[:, 2, 1:2], in0=posi[:, 2, 0:1], scalar1=15, scalar2=None, op0=ALU.bitwise_and))
            link(nc.vector.tensor_scalar(out=posi[:, 2, 2:3], in0=posi[:, 2, 0:1], scalar1=4, scalar2=None, op0=ALU.logical_shift_right))
            link(nc.vector.tensor_copy(T[:, 4:6], posi[:, 2, 1:3]))
            link(nc.vector.tensor_copy(pm[:, 2:4, :], posi[:, 0:2, 0:P]))
            link(nc.vector.tensor_copy(iof[:, :], pm[:, 2, 0:16]))
            link(nc.vector.tensor_scalar(out=pm[:, 0, :], in0=pm[:, 2, :], scalar1=T[:, 4:5], scalar2=None, op0=ALU.is_equal))
            link(nc.vector.scalar_tensor_tensor(out=pm[:, 1, :], in0=pm[:, 3, :], scalar=T[:, 5:6], in1=pm[:, 0, :],
                                                op0=ALU.is_gt, op1=ALU.mult))
            nc.vector.tensor_scalar(out=pm[:, 3, :], in0=pm[:, 3, :], scalar1=T[:, 5:6], scalar2=None, op0=ALU.is_equal).then_inc(masks, 1)

            def hidden_units(m):
                dve.wait_ge(sil_ready, m + 1)
                if m >= 2 * SF and m % SF == 0:
                    dve.wait_ge(dn_done, 2 * (m // SF - 1))
                nc.vector.tensor_tensor(out=hid[:, (m // SF) % 2, m % SF, :], in0=sil[:, m % 2, :], in1=bank[2 + m % 2][:, :],
                                        op=ALU.mult).then_inc(hid_ready, 1)

            dve.wait_ge(masks, 1)
            dve.wait_ge(s_ready, 1)
            Ti, Ci = T[:, 0:1].bitcast(I32), T[:, 1:2].bitcast(I32)
            dve.sem_clear(sch)
            for r in range(ROUNDS):
                nc.vector.tensor_scalar(out=bit[:, :], in0=bit[:, :], scalar1=1, scalar2=None, op0=ALU.logical_shift_right).then_inc(sch, 1)
                dve.wait_ge(sch, 4 * r + 1)
                nc.vector.tensor_tensor(out=Ci, in0=Ti, in1=bit[:, :], op=ALU.bitwise_or).then_inc(sch, 1)
                dve.wait_ge(sch, 4 * r + 2)
                nc.vector.tensor_scalar(out=junk[:, :], in0=score[:, :], scalar1=T[:, 1:2], scalar2=0.0, op0=ALU.is_ge, op1=ALU.add,
                                        accum_out=cnt[:, 0:1]).then_inc(t_done, 1)
                if r >= 2 and PIECES[r - 2][0] == "gate_up":
                    hidden_units(PIECES[r - 2][1])
                dve.wait_ge(off_done, r + 1)
                nc.vector.scalar_tensor_tensor(out=T[:, 2:3], in0=bank[6][:, 256:257], scalar=float(CAP), in1=T[:, 1:2],
                                               op0=ALU.is_ge, op1=ALU.mult).then_inc(sch, 1)
                dve.wait_ge(sch, 4 * r + 3)
                nc.vector.tensor_tensor(out=T[:, 0:1], in0=T[:, 0:1], in1=T[:, 2:3], op=ALU.max).then_inc(sch, 1)
                dve.wait_ge(sch, 4 * r + 4)
            nc.vector.tensor_scalar(out=gt[:, :], in0=score[:, :], scalar1=T[:, 0:1], scalar2=0.0, op0=ALU.is_gt, op1=ALU.add,
                                    accum_out=cnt[:, 0:1])
            nc.vector.tensor_scalar(out=eq[:, :], in0=score[:, :], scalar1=T[:, 0:1], scalar2=0.0, op0=ALU.is_equal, op1=ALU.add,
                                    accum_out=cnt[:, 1:2]).then_inc(t_done, 1)
            dve.wait_ge(t_done, ROUNDS + 1)
            nc.vector.tensor_tensor_scan(out=gtc[:, :], data0=gt[:, :], data1=zero[:, :], initial=0.0, op0=ALU.add, op1=ALU.add)
            link(nc.vector.tensor_tensor_scan(out=eqc[:, :], data0=eq[:, :], data1=zero[:, :], initial=0.0, op0=ALU.add, op1=ALU.add))
            dve.wait_ge(off_done, ROUNDS + 1)
            link(nc.vector.tensor_copy(off[:, :], bank[6][:, 264:268]))
            link(nc.vector.tensor_tensor(out=off[:, 1:2], in0=off[:, 1:2], in1=off[:, 2:3], op=ALU.add))
            link(nc.vector.tensor_scalar(out=off[:, 0:2], in0=off[:, 0:2], scalar1=-4097.0, scalar2=None, op0=ALU.add))
            link(nc.vector.scalar_tensor_tensor(out=gtc[:, :], in0=gtc[:, :], scalar=off[:, 0:1], in1=gt[:, :], op0=ALU.add, op1=ALU.mult))
            link(nc.vector.scalar_tensor_tensor(out=eqc[:, :], in0=eqc[:, :], scalar=off[:, 1:2], in1=eq[:, :], op0=ALU.add, op1=ALU.mult))
            nc.vector.scalar_tensor_tensor(out=pos[:, :], in0=gtc[:, :], scalar=4096.0, in1=eqc[:, :], op0=ALU.add, op1=ALU.add)\
                .then_inc(pos_ready, 1)
            dve.wait_ge(pos_T, 1)
            link(nc.vector.tensor_copy(posi[:, 0, :], bank[4][:, 0:2 * P]))
            nc.vector.tensor_scalar(out=posi[:, 1, :], in0=posi[:, 0, :], scalar1=4, scalar2=None, op0=ALU.logical_shift_right)
            link(nc.vector.tensor_scalar(out=posi[:, 2, :], in0=posi[:, 0, :], scalar1=15, scalar2=None, op0=ALU.bitwise_and))
            link(nc.vector.tensor_copy(posf[:, :, :], posi[:, 1:3, :]))
            link(nc.vector.tensor_scalar(out=v0[:, 0:8], in0=iof[:, 0:8], scalar1=2.0, scalar2=None, op0=ALU.mult))
            link(nc.vector.tensor_scalar(out=v0[:, 8:16], in0=v0[:, 0:8], scalar1=1.0, scalar2=None, op0=ALU.add))
            ia = bass.AP(iof[:, :].tensor, iof[:, :].offset, [list(iof[:, :].ap[0]), [0, 2 * P], [1, 16]])
            pa = lambda i: posf[:, i, :].unsqueeze(2).to_broadcast([P, 2 * P, 16])
            nc.vector.tensor_tensor(out=oa[:, :, :], in0=pa(0), in1=ia, op=ALU.is_equal)
            link(nc.vector.tensor_tensor(out=ob[:, 1, :, :], in0=pa(1), in1=ia, op=ALU.is_equal))
            v0b = bass.AP(v0[:, :].tensor, v0[:, :].offset, [list(v0[:, :].ap[0]), [1, 16], [0, E_ * 16]])
            nc.vector.tensor_tensor(out=ob[:, 0, :, :].rearrange("p (c e) b -> p c (e b)", c=16),
                                    in0=ob[:, 1, :, :].rearrange("p (c e) b -> p c (e b)", c=16), in1=v0b, op=ALU.mult).then_inc(oh_ready, 1)
            dve.wait_ge(oh_ready, 1)
            nc.vector.tensor_scalar(out=ob[:, 1, :, :], in0=ob[:, 1, :, :], scalar1=v1[:, 0:1], scalar2=None, op0=ALU.mult).then_inc(oh_ready, 1)
            dve.wait_ge(idl_done, 2)
            for g in range(2):
                link(nc.vector.tensor_copy(idv[:, 0, :], bank[2 + g][:, P:2 * P]))
                link(nc.vector.scalar_tensor_tensor(out=idv[:, 1, :], in0=bank[2 + g][:, 0:P], scalar=float(P), in1=idv[:, 0, :],
                                                    op0=ALU.mult, op1=ALU.add))
                link(nc.vector.tensor_tensor(out=idv[:, 0, :].rearrange("p (e b) -> p e b", e=8),
                                             in0=idv[:, 1, :].rearrange("p (e b) -> p e b", e=8),
                                             in1=pm[:, 3, 0:P].rearrange("p (e b) -> p e b", e=8), op=ALU.mult))
                link(nc.vector.tensor_reduce(out=idl[:, g, :], in_=idv[:, 0, :].rearrange("p (e b) -> p b e", e=8),
                                             axis=mybir.AxisListType.X, op=ALU.add))
                for f in range(2):
                    last = nc.vector.tensor_tensor(out=lsp[:, 2 * g + f, :].rearrange("p (b a) -> p b a", a=16),
                                                   in0=idl[:, g, 8 * f:8 * f + 8].unsqueeze(2).to_broadcast([P, 8, 16]),
                                                   in1=pm[:, 0, :].rearrange("p (b a) -> p b a", a=16), op=ALU.mult)
                link(last)
            nc.vector.tensor_copy(v1[:, :], v0[:, 0:1]).then_inc(lsp_ready, 1)
            dve.wait_ge(ids_done, 1)
            nc.vector.tensor_copy(ids[:, :], bank[1][:, 0:2 * E_]).then_inc(c_ready, 1)

        @block.tensor
        def _(pe):
            pe.wait_ge(gw_in, 16)
            for kc in range(KC):
                last = nc.tensor.transpose(bank[7][:, kc * E_:(kc + 1) * E_], gw[:, kc * P:(kc + 1) * P], ident[0:E_, 0:E_])
            last.then_inc(g_T, 1)
            for g in range(KC * B):
                pe.wait_ge(h_ready, (g // KC + 1) * ST)
                if g >= 4:
                    pe.wait_ge((h_Te, c_ready)[g % 2], (g - 4) // 2 + 1)
                for t in range(ST):
                    last = nc.tensor.transpose(bank[g % 4][:, t * P:(t + 1) * P],
                                               H[:, (g // KC) * ST + t, (g % KC) * P:(g % KC + 1) * P], ident[:, :])
                last.then_inc(h_T, 1)
            pe.wait_ge(g_Te, 1)
            pe.wait_ge(h_Te, B)
            pe.wait_ge(c_ready, B)
            for s in range(SEG):
                for kc in range(KC):
                    last = nc.tensor.matmul(bank[6][:, 0:SEGT], gz[:, kc, s, :], HT[:, kc, s * SEGT:(s + 1) * SEGT],
                                            start=(s == 0 and kc == 0), stop=(s == SEG - 1 and kc == KC - 1))
            last.then_inc(s_done, 1)
            pe.wait_ge(masks, 1)
            pe.wait_ge(s_ready, 1)
            for f in range(2):
                last = nc.tensor.transpose(bank[5][:, f * P:(f + 1) * P], score[:, f * P:(f + 1) * P], ident[:, :])
            last.then_inc(scT_done, 1)
            def weights(g):
                if g == 0:
                    pe.wait_ge(w_in, 48)
                if g >= 2:
                    pe.wait_ge(sw_Te, g - 1)
                for t in range(4):
                    if g < 4:
                        src = swn[:, g // 2, t, (g % 2) * P:(g % 2 + 1) * P]
                    else:
                        src = sdn[:, t % 2, (2 * (g - 4) + t // 2) * P:(2 * (g - 4) + t // 2 + 1) * P]
                    last = nc.tensor.transpose(bank[g % 2][:, t * P:(t + 1) * P], src, ident[:, :])
                last.then_inc(sw_T, 1)

            def gate_up(m):
                tg, ft = m // SF, m % SF
                if m == 0:
                    pe.wait_ge(sw_Te, 6)
                if m >= 2:
                    pe.wait_ge(sil_ready, m - 1)
                    pe.wait_ge(hid_ready, m - 1)
                for v in range(2):
                    for kc in range(KC):
                        last = nc.tensor.matmul(bank[2 * v + m % 2][:, :], swT[:, v, kc, ft * P:(ft + 1) * P],
                                                HT[:, kc, tg * 512:(tg + 1) * 512], start=(kc == 0), stop=(kc == KC - 1))
                last.then_inc(gu_done, 1)

            def down(m):
                tg, jp = m // 2, m % 2
                pe.wait_ge(hid_ready, (tg + 1) * SF)
                if m >= 2:
                    pe.wait_ge(so_ready, m - 1)
                for j in range(2):
                    for ft in range(SF):
                        last = nc.tensor.matmul(bank[4 if m % 2 == 0 else 7][:, j * D:(j + 1) * D],
                                                hid[:, tg % 2, ft, (2 * jp + j) * P:(2 * jp + j + 1) * P], sdT[:, ft, :],
                                                start=(ft == 0), stop=(ft == SF - 1))
                last.then_inc(dn_done, 1)

            for kind, m in PIECES:
                r = PIECES.index((kind, m))
                pe.wait_ge(t_done, r + 1)
                nc.tensor.matmul(bank[6][:, 256:257], pm[:, 0, :], cnt[:, 0:1], start=True, stop=True).then_inc(off_done, 1)
                {"weights": weights, "gate_up": gate_up, "down": down}[kind](m)
            pe.wait_ge(t_done, ROUNDS + 1)
            nc.tensor.matmul(bank[6][:, 264:266], pm[:, 1, :], cnt[:, :], start=True, stop=True)
            nc.tensor.matmul(bank[6][:, 266:268], pm[:, 0, :], cnt[:, :], start=True, stop=True).then_inc(off_done, 1)
            pe.wait_ge(pos_ready, 1)
            pe.wait_ge(so_ready, 2 * B)
            pe.wait_ge(hid_ready, B * SF)
            for f in range(2):
                last = nc.tensor.transpose(bank[4][:, f * P:(f + 1) * P], pos[:, f * P:(f + 1) * P], ident[:, :])
            last.then_inc(pos_T, 1)
            pe.wait_ge(oh_ready, 2)
            for g in range(2):
                for c in range(16):
                    lhs = oa[:, c * E_ + 8 * g:c * E_ + 8 * g + 8, :].rearrange("p e a -> p (e a)")
                    rhs = ob[:, :, c * E_ + 8 * g:c * E_ + 8 * g + 8, :].rearrange("p v e b -> p v (e b)")
                    last = nc.tensor.matmul(bank[2 + g][:, 0:2 * P], lhs, rhs, start=(c == 0), stop=(c == 15))
                last.then_inc(idl_done, 1)
            pe.wait_ge(lsp_ready, 1)
            for f in range(2):
                for g in range(2):
                    last = nc.tensor.matmul(bank[1][:, E_ * f + 8 * g:E_ * f + 8 * g + 8], lsp[:, 2 * g + f, :],
                                            pm[:, 3, :].rearrange("p (e a) -> p e a", a=16)[:, :, 0], start=True, stop=True)
            last.then_inc(ids_done, 1)


def run_experts(nc, h):
    ctx = ExitStack()
    with ctx:
        sb = lambda name, shape, dt=F32: ctx.enter_context(nc.sbuf_tensor(name, shape, dt))
        sem = lambda name: ctx.enter_context(nc.semaphore(name))
        two = lambda name: [sem(f"{name}{i}") for i in range(2)]
        ident, ids = h["ident"], h["ids"]
        wn = [sb(f"wn{i}", [P, 2 * FT * D + KC * F]) for i in range(2)]
        wt = [sb(f"wt{i}", [P, 3, KC * F]) for i in range(2)]
        xg = [sb(f"xg{i}", [P, 2, HROW]) for i in range(2)]
        xgT = [sb(f"xgT{i}", [P, KC, CAP]) for i in range(2)]
        bn = sb("bn", [P, 2, P])
        bT = sb("bT", [P, 2, E_ * FT])
        db = [sb(f"db{i}", [P, D]) for i in range(2)]
        sil = sb("silE", [P, 2, CAP])
        hid = sb("hidE", [P, FT, CAP])
        so = sb("so", [P, 2, 2, D])
        tmp = sb("tmpE", [P, 2, D])
        tr = [ctx.enter_context(nc.psum_tensor(f"tr{i}", [P, 512], F32)) for i in range(3)]
        gps = [ctx.enter_context(nc.psum_tensor(f"gps{i}", [P, CAP], F32)) for i in range(2)]
        ups = [ctx.enter_context(nc.psum_tensor(f"ups{i}", [P, CAP], F32)) for i in range(2)]
        ops = ctx.enter_context(nc.psum_tensor("ops", [P, 2, D], F32))
        w_in, x_in, scattered = two("w_inE"), two("x_inE"), two("scattered")
        bn_in, b_T, b_Te = sem("bn_inE"), sem("b_TE"), sem("b_TeE")
        tr_done, tr_free = [sem(f"tr_done{i}") for i in range(3)], [sem(f"tr_free{i}") for i in range(3)]
        ou, so_free = two("output_usedE"), two("so_freeE")
        g_done, u_done, s_rdy, h_rdy, o_done, o_rdy, t_rdy = [sem(n) for n in ("g_doneE", "u_doneE", "s_rdyE", "h_rdyE", "o_doneE", "o_rdyE", "t_rdyE")]
        block = ctx.enter_context(nc.Block())
        NG = 13
        uses = [5, 4, 4]
        WU, WG, WD = 0, FT * D, 2 * FT * D
        hx, accum = h["hx"], h["accum"]
        up_w = h["up_w"].rearrange("e (t p) d -> p e t d", p=P)
        gw = h["gw"].rearrange("e (t p) d -> p e t d", p=P)
        dw = h["down_w"].rearrange("e (t p) f -> p e t f", p=P)
        dbv = bass.AP(h["down_b"].tensor, h["down_b"].offset, [[0, P], [D, E_], [1, D]])
        PAIRS = E_ // 2

        def one(e):
            return bass.ds(e, 1) if not isinstance(e, int) else slice(e, e + 1)

        @block.sync
        def _(sp):
            sp.dma_start(bn[:, 0, :], h["up_b"].rearrange("e (t p) -> (e t) p", p=P)).then_inc(bn_in, 16)
            sp.dma_start(bn[:, 1, :], h["gb"].rearrange("e (t p) -> (e t) p", p=P)).then_inc(bn_in, 16)

            def load(n, k):
                    e = n * 2 + k
                    sp.dma_start(wn[k][:, WU:WG].rearrange("p (o t d) -> p o t d", o=1, t=FT), up_w[:, one(e), :, :]).then_inc(w_in[k], 16)
                    sp.dma_start(wn[k][:, WG:WD].rearrange("p (o t d) -> p o t d", o=1, t=FT), gw[:, one(e), :, :]).then_inc(w_in[k], 16)
                    sp.dma_start(wn[k][:, WD:].rearrange("p (o t f) -> p o t f", o=1, t=KC), dw[:, one(e), :, :]).then_inc(w_in[k], 16)
                    sp.dma_start(db[k][:, :].rearrange("p (o d) -> p o d", o=1), dbv[:, one(e), :]).then_inc(w_in[k], 16)

            for k in range(2):
                load(0, k)
            with sp.Fori(1, PAIRS) as n:
                for k in range(2):
                    sp.wait_ge(tr_done[2], n * 8 + (4 * k - 4))
                    sp.wait_ge(ou[k], n)
                    load(n, k)

        @block.gpsimd
        def _(pool):
            def gather(e):
                k = e % 2
                if e >= 2:
                    pool.wait_ge(ou[k], e // 2)
                for f in range(2):
                    nc.gpsimd.indirect_dma_start(out=xg[k][:, f, :], out_offset=None, in_=hx[:, :],
                                                 in_offset=bass.IndirectOffsetOnAxis(ap=ids[:, E_ * f + e:E_ * f + e + 1], axis=0),
                                                 bounds_check=NTOK - 1).then_inc(x_in[k], 16)

            for k in range(2):
                pool.sem_inc(so_free[k], 1)
            gather(0)
            for e in range(E_):
                k = e % 2
                if e + 1 < E_:
                    gather(e + 1)
                if e:
                    pool.wait_ge(scattered[1 - k], 32 * ((e + 1) // 2))
                    pool.sem_inc(so_free[1 - k], 1)
                pool.wait_ge(o_rdy, 2 * (e + 1))
                for f in range(2):
                    nc.gpsimd.indirect_dma_start(out=accum[:, :],
                                                 out_offset=bass.IndirectOffsetOnAxis(ap=ids[:, E_ * f + e:E_ * f + e + 1], axis=0),
                                                 in_=so[:, k, f, :], in_offset=None, bounds_check=NTOK - 1,
                                                 compute_op=ALU.add).then_inc(scattered[k], 16)
            for k in range(2):
                pool.wait_ge(scattered[k], 32 * PAIRS)

        def sources(q, k):
            if q < 8:
                m, kc, hf = q // 4, (q % 4) // 2, q % 2
                base = (WU, WG)[m]
                return [wn[k][:, base + (4 * hf + t) * D + kc * P:base + (4 * hf + t) * D + (kc + 1) * P] for t in range(4)]
            if q < 12:
                return [wn[k][:, WD + (t % 2) * F + (2 * (q - 8) + t // 2) * P:WD + (t % 2) * F + (2 * (q - 8) + t // 2 + 1) * P] for t in range(4)]
            return [xg[k][:, t % 2, (t // 2) * P:(t // 2 + 1) * P] for t in range(4)]

        def target(q, k):
            if q < 8:
                m, kc, hf = q // 4, (q % 4) // 2, q % 2
                return wt[k][:, m, kc * F + hf * 512:kc * F + (hf + 1) * 512]
            if q < 12:
                return wt[k][:, 2, (q - 8) * 512:(q - 7) * 512]
            return xgT[k][:, :, :].rearrange("p a b -> p (a b)")

        @block.tensor
        def _(pe):
            pe.wait_ge(bn_in, 32)
            for m in range(2):
                last = nc.tensor.transpose(ops[:, 0, m * P:(m + 1) * P], bn[:, m, :], ident[:, :])
            last.then_inc(b_T, 1)

            def transposes(n, k):
                pe.wait_ge(w_in[k], n * 64 + 64)
                for q in range(NG):
                    b = q % 3
                    if q == 12:
                        pe.wait_ge(x_in[k], n * 32 + 32)
                    pe.wait_ge(tr_free[b], n * (2 * uses[b]) + (k * uses[b] + q // 3))
                    for t, s in enumerate(sources(q, k)):
                        last = nc.tensor.transpose(tr[b][:, t * P:(t + 1) * P], s, ident[:, :])
                    last.then_inc(tr_done[b], 1)

            def up_gate(n, k):
                for b in range(3):
                    pe.wait_ge(tr_free[b], n * (2 * uses[b]) + (k + 1) * uses[b])
                for ft in range(FT):
                    for m, (ps, done, taken) in enumerate(((ups, u_done, h_rdy), (gps, g_done, s_rdy))):
                        if ft >= 2:
                            pe.wait_ge(taken, n * (2 * FT) + (k * FT + ft - 1))
                        for kc in range(KC):
                            last = nc.tensor.matmul(ps[ft % 2][:, :], wt[k][:, m, kc * F + ft * P:kc * F + (ft + 1) * P],
                                                    xgT[k][:, kc, :], start=(kc == 0), stop=(kc == KC - 1))
                        last.then_inc(done, 1)

            def down(n, k):
                pe.wait_ge(h_rdy, n * (2 * FT) + (k + 1) * FT)
                for f in range(2):
                    for ft in range(FT):
                        last = nc.tensor.matmul(ops[:, f, :], hid[:, ft, f * P:(f + 1) * P], wt[k][:, 2, ft * D:(ft + 1) * D],
                                                start=(ft == 0), stop=(ft == FT - 1))
                last.then_inc(o_done, 1)

            pe.wait_ge(b_Te, 1)
            transposes(0, 0)
            with pe.Fori(0, PAIRS - 1) as n:
                up_gate(n, 0)
                transposes(n, 1)
                down(n, 0)
                up_gate(n, 1)
                transposes(n + 1, 0)
                down(n, 1)
            n = PAIRS - 1
            up_gate(n, 0)
            transposes(n, 1)
            down(n, 0)
            up_gate(n, 1)
            down(n, 1)

        @block.scalar
        def _(act):
            def take(n, k):
                for q in range(0, NG, 3):
                    act.wait_ge(tr_done[0], n * 10 + (k * 5 + q // 3 + 1))
                    ins = nc.scalar.activation(target(q, k), tr[0][:, :], ACT.Copy)
                    ins.then_inc(tr_free[0], 1)

            def silu(n, k, e):
                for ft in range(FT):
                    act.wait_ge(g_done, n * (2 * FT) + (k * FT + ft + 1))
                    if ft >= 2:
                        act.wait_ge(h_rdy, n * (2 * FT) + (k * FT + ft - 1))
                    nc.scalar.activation(sil[:, ft % 2, :], gps[ft % 2][:, :], ACT.Silu, bias=bT[:, 1, e_col(e, ft)]).then_inc(s_rdy, 1)

            def e_col(e, ft):
                return bass.ds(e * FT + ft, 1) if not isinstance(e, int) else slice(e * FT + ft, e * FT + ft + 1)

            act.wait_ge(b_T, 1)
            nc.scalar.activation(bT[:, :, :].rearrange("p a b -> p (a b)"), ops[:, 0, :], ACT.Copy).then_inc(b_Te, 1)
            act.wait_ge(b_Te, 1)
            take(0, 0)
            with act.Fori(0, PAIRS - 1) as n:
                silu(n, 0, n * 2)
                take(n, 1)
                silu(n, 1, n * 2 + 1)
                take(n + 1, 0)
            n = PAIRS - 1
            silu(n, 0, n * 2)
            take(n, 1)
            silu(n, 1, n * 2 + 1)

        @block.vector
        def _(dve):
            def take(n, k):
                for q in range(NG):
                    if q % 3:
                        dve.wait_ge(tr_done[q % 3], n * 8 + (k * 4 + q // 3 + 1))
                        nc.vector.tensor_copy(target(q, k), tr[q % 3][:, :]).then_inc(tr_free[q % 3], 1)

            def hidden(n, k, e):
                for ft in range(FT):
                    dve.wait_ge(s_rdy, n * (2 * FT) + (k * FT + ft + 1))
                    dve.wait_ge(u_done, n * (2 * FT) + (k * FT + ft + 1))
                    col = bass.ds(e * FT + ft, 1) if not isinstance(e, int) else slice(e * FT + ft, e * FT + ft + 1)
                    nc.vector.scalar_tensor_tensor(out=hid[:, ft, :], in0=ups[ft % 2][:, :], scalar=bT[:, 0, col], in1=sil[:, ft % 2, :],
                                                   op0=ALU.add, op1=ALU.mult).then_inc(h_rdy, 1)

            def output(n, k, e):
                dve.wait_ge(o_done, n * 2 + (k + 1))
                dve.wait_ge(so_free[k], n + 1)
                for f in range(2):
                    nc.vector.tensor_tensor(out=tmp[:, f, :], in0=ops[:, f, :], in1=db[k][:, :], op=ALU.add).then_inc(t_rdy, 1)
                dve.wait_ge(t_rdy, n * 4 + (2 * k + 2))
                for f in range(2):
                    col = bass.ds(e + D, 1) if not isinstance(e, int) else slice(e + D, e + D + 1)
                    nc.vector.tensor_scalar(out=so[:, k, f, :], in0=tmp[:, f, :], scalar1=xg[k][:, f, col], scalar2=None, op0=ALU.mult)\
                        .then_inc(o_rdy, 1)
                dve.wait_ge(o_rdy, n * 4 + (2 * k + 2))
                nc.vector.tensor_copy(tmp[:, 0, 0:1], tmp[:, 1, 0:1]).then_inc(ou[k], 1)

            take(0, 0)
            with dve.Fori(0, PAIRS - 1) as n:
                hidden(n, 0, n * 2)
                take(n, 1)
                output(n, 0, n * 2)
                hidden(n, 1, n * 2 + 1)
                take(n + 1, 0)
                output(n, 1, n * 2 + 1)
            n = PAIRS - 1
            hidden(n, 0, n * 2)
            take(n, 1)
            output(n, 0, n * 2)
            hidden(n, 1, n * 2 + 1)
            output(n, 1, n * 2 + 1)


def finish(nc, h):
    ctx = ExitStack()
    with ctx:
        sem = lambda name: ctx.enter_context(nc.semaphore(name))
        X, tg = h["X"], h["tg"]
        acc = ctx.enter_context(nc.sbuf_tensor("accF", [P, NT, D], F32))
        acc_in = [sem(f"acc_inF{b}") for b in range(B)]
        sums, stored = sem("sumsF"), sem("storedF")
        block = ctx.enter_context(nc.Block())
        av = h["accum"].rearrange("(t p) d -> p t d", p=P)
        ov = h["out"].rearrange("b (t p) d -> p (b t) d", p=P)

        @block.sync
        def _(sp):
            for b in range(B):
                sp.dma_start(acc[:, b * ST:(b + 1) * ST, :], av[:, b * ST:(b + 1) * ST, :]).then_inc(acc_in[b], 16)
            for b in range(B):
                sp.wait_ge(sums, b + 1)
                sp.dma_start(ov[:, b * ST:(b + 1) * ST, :], X[:, b * ST:(b + 1) * ST, :]).then_inc(stored, 16)
            sp.wait_ge(stored, 16 * B)

        @block.vector
        def _(dve):
            for b in range(B):
                dve.wait_ge(acc_in[b], 16)
                r = slice(b * ST, (b + 1) * ST)
                nc.vector.scalar_tensor_tensor(out=X[:, r, :], in0=acc[:, r, :], scalar=tg[:, 1:2], in1=X[:, r, :],
                                               op0=ALU.mult, op1=ALU.add).then_inc(sums, 1)


def build(nc, x, ctx_rows, g_xattn, g_ffn, gate_w, up_w, up_b, gw, gb, down_w, down_b, sh_gate_w, sh_up_w, sh_down_w, out):
    dram = lambda name, shape, dt=F32: nc.dram_tensor(name, shape, dt, kind="Internal").ap()
    h = dict(x=x, ctx=ctx_rows, g_xattn=g_xattn, g_ffn=g_ffn, gate_w=gate_w, up_w=up_w, up_b=up_b, gw=gw, gb=gb, down_w=down_w,
             down_b=down_b, sh_gate_w=sh_gate_w, sh_up_w=sh_up_w, sh_down_w=sh_down_w, out=out)
    h["dd"] = dram("distances", (P, DROWS, CELL))
    h["spans"] = dram("spans", (2, P, W), F16)
    h["hx"] = dram("token_rows", (NTOK, HROW))
    h["accum"] = dram("ffn_sum", (NTOK, D))
    ctx = ExitStack()
    with ctx:
        sb = lambda name, shape, dt=F32: ctx.enter_context(nc.sbuf_tensor(name, shape, dt))
        h["X"] = sb("X", [P, NT, D])
        h["ident"] = sb("ident", [P, P])
        h["block_id"] = sb("block_id", [P, 1])
        h["not_first"] = sb("not_first", [P, 1])
        h["first_block"] = sb("first_block", [P, 1])
        h["last_block"] = sb("last_block", [P, 1])
        h["tg"] = sb("tg", [P, 2])
        h["ids"] = sb("ids", [P, 2 * E_], I32)
        with ExitStack() as attend:
            h["C"] = attend.enter_context(nc.sbuf_tensor("C", [P, NT, D], F32))
            prepare_distances(nc, h)
            with ExitStack() as walk:
                h["dleave"] = walk.enter_context(nc.sbuf_tensor("dleave", [P, W, RING + STEPS], F32))
                h["dexit"] = walk.enter_context(nc.sbuf_tensor("dexit", [P, STEPS], F32))
                h["steps"] = walk.enter_context(nc.sbuf_tensor("steps", [P, STEPS], F32))
                accumulate_costs(nc, h)
                trace_path(nc, h)
            align(nc, h)
        route(nc, h)
        run_experts(nc, h)
        finish(nc, h)


_INS = ['x', 'ctx_1024', 'g_xattn', 'g_ffn', 'L0_ffn_gate_w', 'L0_ffn_up_w', 'L0_ffn_up_b', 'L0_ffn_gw', 'L0_ffn_gb',
        'L0_ffn_down_w', 'L0_ffn_down_b', 'L0_ffn_sh_gate_w', 'L0_ffn_sh_up_w', 'L0_ffn_sh_down_w']
_OUT = (B, S, D)


def kernel(**inputs):
    import numpy as np
    import concourse.bacc as bacc
    from concourse.bass_utils import run_bass_kernel_spmd

    nc = bacc.Bacc("TRN2", target_bir_lowering=False, num_devices=1)
    arrays, args = {}, []
    for name in _INS:
        a = np.ascontiguousarray(inputs[name])
        arrays[f"in_{name}"] = a
        args.append(nc.dram_tensor(f"in_{name}", a.shape, mybir.dt.from_np(a.dtype), kind="ExternalInput").ap())
    args.append(nc.dram_tensor("out_x", _OUT, F32, kind="ExternalOutput").ap())
    build(nc, *args)
    r = run_bass_kernel_spmd(nc, [arrays], core_ids=[0])
    return r.results[0]["out_x"]
```

```python
import concourse.bass as bass
from concourse import mybir
from contextlib import ExitStack

F32 = mybir.dt.float32
BF16 = mybir.dt.bfloat16
I32 = mybir.dt.int32
F16 = mybir.dt.float16
F32R = mybir.dt.float32r
ALU = mybir.AluOpType
ACT = mybir.ActivationFunctionType

P = 128
B, S, D = 4, 512, 256
ST = S // P
NT = B * ST
KC = D // P
NK = 32
W = S // NK
CELL = W + 1
PAD = 32
STEPS = S + NK
HALF = 16
RING = 2 * HALF
CHUNKS = STEPS // RING
DROWS = PAD + S + NK
BIG = 1e30
EPS = 1e-5
TINY = 1e-18

E_, CAP, F = 16, 256, 1024
FT = F // P
SH = 512
SF = SH // P
NTOK = B * S
HROW = D + E_
SEG = 8
SEGT = NTOK // SEG
UP0, GATE0, DOWN0, WSIZE = 0, FT * D, 2 * FT * D, 2 * FT * D + KC * F
WG = 12


def load_weights(engine, h, e, wn, loaded):
    up, gate = (h[w].rearrange("e (t p) d -> p e t d", p=P) for w in ("up_w", "gw"))
    down = h["down_w"].rearrange("e (t p) f -> p e t f", p=P)
    engine.dma_start(wn[:, UP0:GATE0].rearrange("p (o t d) -> p o t d", o=1, t=FT), up[:, e, :, :]).then_inc(loaded, 16)
    engine.dma_start(wn[:, GATE0:DOWN0].rearrange("p (o t d) -> p o t d", o=1, t=FT), gate[:, e, :, :]).then_inc(loaded, 16)
    engine.dma_start(wn[:, DOWN0:].rearrange("p (o t f) -> p o t f", o=1, t=KC), down[:, e, :, :]).then_inc(loaded, 16)


def weight_tiles(wn, q):
    if q < 8:
        base, kc, half = (UP0, GATE0)[q // 4], (q % 4) // 2, q % 2
        return [wn[:, base + (4 * half + t) * D + kc * P:base + (4 * half + t) * D + (kc + 1) * P] for t in range(4)]
    return [wn[:, DOWN0 + (t % 2) * F + (2 * (q - 8) + t // 2) * P:DOWN0 + (t % 2) * F + (2 * (q - 8) + t // 2 + 1) * P] for t in range(4)]


def weight_place(wt, q, part):
    if q < 8:
        m, kc, half = q // 4, (q % 4) // 2, q % 2
        return wt[:, part, m, kc * F + half * 512:kc * F + (half + 1) * 512]
    return wt[:, part, 2, (q - 8) * 512:(q - 7) * 512]


def distance_matmuls(nc, pe, h, bank, it, done, taken):
    for b in range(B):
        taken(b)
        for kc in range(KC):
            nc.tensor.matmul(bank[4 + b][:, :], h["CT"][:, kc, b, it * P:(it + 1) * P], h["XT"][:, kc, b, :], start=(kc == 0), stop=False)
        nc.tensor.matmul(bank[4 + b][:, :], h["ones_row"][0:1, :], h["bbrow"][0:1, b, :], start=False, stop=True).then_inc(done, 1)


def distance_transposes(nc, h, bank, done):
    rv = h["root"].rearrange("p b (k w) -> p (b k) w", w=W)
    for w in range(W):
        last = nc.tensor.transpose(bank[w // 4][:, (w % 4) * P:(w % 4 + 1) * P], rv[:, :, w], h["ident"][:, :])
        if w % 4 == 3:
            last.then_inc(done, 1)


def prepare_distances(nc, h):
    ctx = ExitStack()
    with ctx:
        sb = lambda name, shape, dt=F32: ctx.enter_context(nc.sbuf_tensor(name, shape, dt))
        sem = lambda name: ctx.enter_context(nc.semaphore(name))
        X = h["X"]
        C = h["C"]
        ident = h["ident"]
        XN = sb("XN", [P, NT, D])
        CT, XT = h["CT"], h["XT"]
        XSQ = XN[:, :, :].rearrange("p t d -> p (t d)").rearrange("p (b k s) -> p b k s", b=B, k=KC)
        temp = XN[:, :, :].rearrange("p t d -> p (t d)").rearrange("p (k b s) -> p k b s", b=B, k=KC)
        junk = sb("junkA", [P, D])
        bnst = sb("bnst", [P, NT, 6])
        mv = sb("mv", [P, NT, 2])
        sd = sb("sd", [P, 4, NT])
        aa, bbrow, ones, lnhalf = h["aa"], h["bbrow"], h["ones_row"], h["lnhalf"]
        d2, root, half_inv, laid = h["d2"], h["root"], h["half_inv"], h["laid"]
        bcol = sb("bcol", [P, 1])
        pidx = sb("pidx", [P, 2], I32)
        zpad = sb("zpad", [P, PAD * CELL])
        bank = [ctx.enter_context(nc.psum_tensor(f"pA{i}", [P, 512], F32)) for i in range(8)]

        x_in = [sem(f"x_in{b}") for b in range(B)]
        c_in, ident_ready, ones_ready = sem("c_in"), sem("ident_ready"), sem("ones_readyA")
        c_T, c_Te, x_T, x_Te = sem("c_T"), sem("c_Te"), sem("x_T"), sem("x_Te")
        xn_ready, var_ready, root_ready = sem("xn_ready"), sem("var_ready"), sem("sd_ready")
        aa_ready, sq_ready, bb_done, bb_ready = sem("aa_ready"), sem("sq_ready"), sem("bb_done"), sem("bb_ready")
        d_done, d_evac, inv_ready, newton = sem("d_done"), sem("d_evac"), sem("inv_ready"), sem("newton")
        w_T, w_evA, w_evD, d_out = sem("w_T"), sem("w_evA"), sem("w_evD"), sem("d_outA")
        zero_ready, pad_out = sem("zero_ready"), sem("pad_out")
        vch, ach, pch = sem("vchA"), sem("achA"), sem("pchA")
        pidx_ready, rough_ready, not_first_ready = sem("pidx_ready"), sem("rough_readyA"), sem("not_first_ready")
        block = ctx.enter_context(nc.Block())

        dd = h["dd"]

        @block.sync
        def _(sp):
            for b in range(B):
                tiles = slice(b * ST, (b + 1) * ST)
                sp.dma_start(X[:, tiles, :], h["x"].rearrange("b (t p) d -> p (b t) d", p=P)[:, tiles, :]).then_inc(x_in[b], 16)
            sp.dma_start(C[:, :, :], h["ctx"].rearrange("b (t p) d -> p (b t) d", p=P)).then_inc(c_in, 16)
            sp.wait_ge(zero_ready, 1)
            sp.dma_start(dd[:, 0:PAD, :], zpad[:, :].rearrange("p (r c) -> p r c", c=CELL)).then_inc(pad_out, 16)
            sp.dma_start(dd[:, PAD + S:DROWS, :], zpad[:, :].rearrange("p (r c) -> p r c", c=CELL)).then_inc(pad_out, 16)
            sp.wait_ge(w_evA, 2)
            sp.wait_ge(w_evD, 2)
            sp.dma_start(dd[:, PAD:PAD + P, :], laid).then_inc(d_out, 16)
            sp.wait_ge(d_out, 16)
            sp.wait_ge(pad_out, 32)

        @block.gpsimd
        def _(pool):
            nc.gpsimd.memset(ident[:, :], 0.0).then_inc(pch, 1)
            pool.wait_ge(pch, 1)
            nc.gpsimd.affine_select(out=ident[:, :], in_=ident[:, :], compare_op=ALU.not_equal, fill=1.0, base=0,
                                    pattern=[[-1, P]], channel_multiplier=1).then_inc(ident_ready, 1)
            nc.gpsimd.memset(ones[:, :], 1.0).then_inc(ones_ready, 1)
            nc.gpsimd.memset(zpad[:, :], 0.0).then_inc(zero_ready, 1)
            nc.gpsimd.iota(pidx[:, 0:1], pattern=[[0, 1]], base=0, channel_multiplier=1).then_inc(pidx_ready, 1)
            steps, when = h["steps"], h["when"]
            nc.gpsimd.iota(steps[:, :], pattern=[[1, STEPS]], base=0, channel_multiplier=0,
                           allow_small_or_imprecise_dtypes=True).then_inc(pch, 1)
            pool.wait_ge(pch, 2)
            nc.gpsimd.tensor_scalar(out=when[:, 0, :], in0=steps[:, :], scalar1=0.0, scalar2=None, op0=ALU.add)
            nc.gpsimd.tensor_scalar(out=when[:, 1, :], in0=steps[:, :], scalar1=-0.75, scalar2=None, op0=ALU.add).then_inc(pch, 1)
            nc.gpsimd.memset(h["rows"][:, :, :], BIG)
            nc.gpsimd.memset(h["upper"][:, :, :], BIG)
            nc.gpsimd.memset(h["exit"][:, :, :], 0.0)
            for i in range(2):
                nc.gpsimd.memset(h["points"][i][:, :, :, :], 0.0)
                nc.gpsimd.memset(h["column"][i][:, :, :, :], 0.0)
                nc.gpsimd.memset(h["leave"][i][:, :, :], 0.0)
            pool.wait_ge(pch, 3)
            pool.wait_ge(not_first_ready, 1)
            nc.gpsimd.tensor_scalar(out=h["when0"][:, :, :], in0=when[:, :, :], scalar1=h["not_first"][:, :], scalar2=None, op0=ALU.mult)

        @block.scalar
        def _(act):
            act.wait_ge(var_ready, 1)
            nc.scalar.activation(sd[:, 1, :], sd[:, 0, :], ACT.Sqrt).then_inc(root_ready, 1)
            for g in range(KC * B):
                act.wait_ge(x_Te, (g // KC + 1) * KC)
                nc.scalar.activation(XSQ[:, g // KC, g % KC, :], XT[:, g % KC, g // KC, :], ACT.Square).then_inc(sq_ready, 1)
            for g in range(KC * B):
                act.wait_ge(c_T, g + 1)
                nc.scalar.activation(CT[:, g % KC, g // KC, :], bank[g % 4][:, :], ACT.Copy, scale=-2.0).then_inc(c_Te, 1)

            def squares(n, i):
                nc.scalar.activation(junk[:, :], C[:, i, :], ACT.Square, accum_out=aa[:, i:i + 1]).then_inc(aa_ready, 1)
                act.wait_ge(aa_ready, n + 1)

            for b in range(B):
                squares(b, b * ST)
            for b in range(B):
                act.wait_ge(d_evac, b + 1)
                nc.scalar.activation(root[:, b, :], d2[:, b, :], ACT.Sqrt).then_inc(rough_ready, 1)
            nc.scalar.activation(half_inv, d2, ACT.Ln).then_inc(ach, 1)
            act.wait_ge(ach, 1)
            nc.scalar.activation(half_inv, half_inv, ACT.Exp, scale=-0.5, bias=lnhalf[:, :]).then_inc(inv_ready, 1)
            for n, i in enumerate(i for i in range(NT) if i % ST):
                squares(B + n, i)
            for g in (0, 2):
                act.wait_ge(w_T, g + 1)
                nc.scalar.activation(laid[:, :, 1 + 4 * g:5 + 4 * g].rearrange("p i w -> p w i"),
                                     bank[g][:, :].rearrange("p (w i) -> p w i", w=4), ACT.Copy).then_inc(w_evA, 1)

        @block.vector
        def _(dve):
            n = [0]

            def link(ins):
                n[0] += 1
                ins.then_inc(vch, 1)
                dve.wait_ge(vch, n[0])

            nc.vector.memset(lnhalf[:, :], -0.6931471805599453)
            nc.vector.memset(h["tiny"][:, :], TINY)
            dve.wait_ge(pidx_ready, 1)
            link(nc.vector.tensor_scalar(out=pidx[:, 1:2], in0=pidx[:, 0:1], scalar1=NK - 1, scalar2=None, op0=ALU.bitwise_and))
            link(nc.vector.tensor_scalar(out=bcol[:, 0:1], in0=pidx[:, 1:2], scalar1=0.0, scalar2=BIG, op0=ALU.is_equal, op1=ALU.mult))
            link(nc.vector.tensor_scalar(out=h["first_block"][:, :], in0=pidx[:, 1:2], scalar1=0.0, scalar2=None, op0=ALU.is_equal))
            link(nc.vector.tensor_scalar(out=h["not_first"][:, :], in0=pidx[:, 1:2], scalar1=0.0, scalar2=None, op0=ALU.not_equal))
            dve.sem_inc(not_first_ready, 1)
            link(nc.vector.tensor_copy(h["block_id"][:, :], pidx[:, 1:2]))
            link(nc.vector.tensor_scalar(out=h["last_block"][:, :], in0=pidx[:, 1:2], scalar1=float(NK - 1), scalar2=None, op0=ALU.is_equal))
            for i in range(NT):
                if i % ST == 0:
                    dve.wait_ge(x_in[i // ST], 16)
                last = nc.vector.bn_stats(bnst[:, i, :], X[:, i, :])
            link(last)
            for i in range(NT):
                last = nc.vector.bn_aggr(mv[:, i, :], bnst[:, i, :])
            link(last)
            nc.vector.tensor_scalar(out=sd[:, 0, :], in0=mv[:, :, 1], scalar1=EPS, scalar2=None, op0=ALU.add).then_inc(var_ready, 1)
            dve.wait_ge(root_ready, 1)
            dve.wait_ge(var_ready, 1)
            link(nc.vector.reciprocal(sd[:, 2, :], sd[:, 1, :]))
            link(nc.vector.tensor_tensor(out=sd[:, 3, :], in0=sd[:, 0, :], in1=sd[:, 2, :], op=ALU.mult))
            link(nc.vector.tensor_tensor(out=sd[:, 2, :], in0=sd[:, 3, :], in1=sd[:, 1, :], op=ALU.add))
            link(nc.vector.tensor_scalar(out=sd[:, 3, :], in0=sd[:, 2, :], scalar1=0.5, scalar2=None, op0=ALU.mult))
            link(nc.vector.reciprocal(sd[:, 2, :], sd[:, 3, :]))
            for i in range(NT):
                nc.vector.tensor_scalar(out=XN[:, i, :], in0=X[:, i, :], scalar1=mv[:, i, 0:1], scalar2=sd[:, 2, i:i + 1],
                                        op0=ALU.subtract, op1=ALU.mult).then_inc(xn_ready, 1)
            for g in range(KC * B):
                dve.wait_ge(x_T, g + 1)
                nc.vector.tensor_copy(XT[:, g % KC, g // KC, :], bank[4 + g % 4][:, :]).then_inc(x_Te, 1)
            for b in range(B):
                dve.wait_ge(bb_done, b + 1)
                nc.vector.tensor_copy(bbrow[0:1, b, :], bank[4 + b][0:1, :]).then_inc(bb_ready, 1)
            nc.vector.tensor_copy(laid[:, :, 0], bcol[:, 0:1].to_broadcast([P, P]))
            dve.wait_ge(aa_ready, B)
            for b in range(B):
                dve.wait_ge(d_done, b + 1)
                nc.vector.tensor_scalar(out=d2[:, b, :], in0=bank[4 + b][:, :], scalar1=aa[:, b * ST:b * ST + 1],
                                        scalar2=TINY, op0=ALU.add, op1=ALU.max).then_inc(d_evac, 1)
            dve.wait_ge(rough_ready, B)
            dve.wait_ge(d_evac, B)
            link(nc.vector.tensor_tensor(out=temp[:, 0, :, :], in0=root, in1=root, op=ALU.mult))
            link(nc.vector.tensor_tensor(out=temp[:, 1, :, :], in0=d2, in1=temp[:, 0, :, :], op=ALU.subtract))
            dve.wait_ge(inv_ready, 1)
            link(nc.vector.tensor_tensor(out=temp[:, 0, :, :], in0=temp[:, 1, :, :], in1=half_inv, op=ALU.mult))
            nc.vector.tensor_tensor(out=root, in0=root, in1=temp[:, 0, :, :], op=ALU.add).then_inc(newton, 1)
            for g in (1, 3):
                dve.wait_ge(w_T, g + 1)
                nc.vector.tensor_copy(laid[:, :, 1 + 4 * g:5 + 4 * g].rearrange("p i w -> p w i"),
                                      bank[g][:, :].rearrange("p (w i) -> p w i", w=4)).then_inc(w_evD, 1)

        @block.tensor
        def _(pe):
            pe.wait_ge(ident_ready, 1)
            for g in range(KC * B):
                pe.wait_ge(xn_ready, (g // KC + 1) * ST)
                if g >= 4:
                    pe.wait_ge(x_Te, g - 3)
                for t in range(ST):
                    last = nc.tensor.transpose(bank[4 + g % 4][:, t * P:(t + 1) * P],
                                               XN[:, (g // KC) * ST + t, (g % KC) * P:(g % KC + 1) * P], ident[:, :])
                last.then_inc(x_T, 1)
            pe.wait_ge(c_in, 16)
            for g in range(KC * B):
                if g >= 4:
                    pe.wait_ge(c_Te, g - 3)
                for t in range(ST):
                    last = nc.tensor.transpose(bank[g % 4][:, t * P:(t + 1) * P],
                                               C[:, (g // KC) * ST + t, (g % KC) * P:(g % KC + 1) * P], ident[:, :])
                last.then_inc(c_T, 1)
                if g == 3:
                    pe.wait_ge(ones_ready, 1)
                    pe.wait_ge(x_Te, KC * B)
                    for b in range(B):
                        pe.wait_ge(sq_ready, KC * (b + 1))
                        for kc in range(KC):
                            last = nc.tensor.matmul(bank[4 + b][0:1, :], ones[:, 0:1], XSQ[:, b, kc, :], start=(kc == 0), stop=(kc == KC - 1))
                        last.then_inc(bb_done, 1)
            pe.wait_ge(bb_ready, B)
            pe.wait_ge(c_Te, KC * B)
            distance_matmuls(nc, pe, h, bank, 0, d_done, lambda b: None)
            pe.wait_ge(newton, 1)
            distance_transposes(nc, h, bank, w_T)


def accumulate_costs(nc, h):
    ctx = ExitStack()
    with ctx:
        sb = lambda name, shape, dt=F32: ctx.enter_context(nc.sbuf_tensor(name, shape, dt))
        sem = lambda name: ctx.enter_context(nc.semaphore(name))
        GR = 8
        EXIT0, LEAVE0 = 16, 25
        dist = [sb(f"dist{i}", [P, HALF * CELL]) for i in range(2)]
        rows, upper, exit_, when, when0 = (h[name] for name in ("rows", "upper", "exit", "when", "when0"))
        points, column, leave = h["points"], h["column"], h["leave"]
        left0 = sb("left0", [P, 1])
        isup = sb("isup", [P, GR, W])
        passed = sb("passed", [P, 2, RING])
        dexit_ring = [sb(f"dexit_ring{i}", [P, RING]) for i in range(2)]
        tch = sem("tchB")
        dist_in = [sem(f"dist_in{i}") for i in range(2)]
        rows_ready = [sem(f"rows_ready{i}") for i in range(2)]
        points_ready, first_ready, column_ready = sem("points_ready"), sem("first_ready"), sem("column_ready")
        leave_ready, leave_kept, exit_ready, exit_kept = sem("leave_ready"), sem("leave_kept"), sem("exit_ready"), sem("exit_kept")
        dleave, dexit = h["dleave"], h["dexit"]
        d2, root, half_inv, laid, residual = h["d2"], h["root"], h["half_inv"], h["laid"], h["residual"]
        bank = [ctx.enter_context(nc.psum_tensor(f"pB{i}", [P, 512], F32)) for i in range(8)]
        d_done, d_evac, root_ready, newton, w_T, w_ev, d_out, log_ready = [sem(n) for n in (
            "d_doneB", "d_evacB", "root_readyB", "newtonB", "w_TB", "w_evB", "d_outB", "log_readyB")]
        nch = sem("nchB")
        PER = CHUNKS // ST
        dd = h["dd"]
        skew = bass.AP(dd.tensor, dd.offset, [[NK * DROWS * CELL, B], [(DROWS - 1) * CELL, NK], [1, DROWS * CELL]])
        block = ctx.enter_context(nc.Block())

        @block.sync
        def _(sp):
            def load(c):
                for hf in range(2):
                    sp.wait_ge(rows_ready[hf], c + 1)
                    sp.dma_start(dist[hf][:, :], skew[:, :, bass.ds((c * RING + (PAD + hf * HALF)) * CELL, HALF * CELL)])\
                        .then_inc(dist_in[hf], 16)

            sp.sem_inc(d_out, 16)
            with sp.Fori(0, ST) as it:
                sp.wait_ge(d_out, it * 16 + 16)
                for i in range(PER):
                    load(it * PER + i)
            load(CHUNKS - 1)

        @block.vector
        def _(dve):
            def mark(c_par, slot):
                g, part = (slot // 16 - 1) % (RING // GR), slot % 16
                lo = g * GR
                pt = points[1 - c_par if slot < 16 else c_par]
                diag, up, left = rows[:, lo:lo + GR, 0:W], rows[:, lo:lo + GR, 1:CELL], rows[:, lo + 1:lo + 1 + GR, 0:W]
                out = lambda s: pt[:, :, s, lo:lo + GR].rearrange("p w t -> p t w")
                if part == 3:
                    return nc.vector.tensor_tensor(out=isup[:, :, :], in0=up, in1=diag, op=ALU.is_lt)
                if part == 7:
                    return nc.vector.tensor_tensor(out=out(0), in0=left, in1=upper[:, lo:lo + GR, 1:CELL], op=ALU.is_lt)
                if part == 11:
                    return nc.vector.scalar_tensor_tensor(out=out(1), in0=isup[:, :, :], scalar=0.5, in1=out(0), op0=ALU.is_lt, op1=ALU.is_gt)

            def leave_block(c, c_par, slot):
                x = (slot - EXIT0) % 64
                pt = points[1 - c_par if slot >= EXIT0 else c_par]
                w, part = x // 4, x % 4
                if x == 0:
                    dve.wait_ge(exit_kept, c + 1)
                    nc.vector.tensor_tensor(out=dexit_ring[c_par][:, :], in0=exit_[:, W - 1, 1:RING + 1], in1=exit_[:, W - 1, 0:RING], op=ALU.subtract)
                    return nc.vector.tensor_copy(exit_[:, 0:W - 1, 0], exit_[:, 0:W - 1, RING])
                elif x == 2:
                    dve.wait_ge(first_ready, c + 1)
                    col = column[1 - c_par]
                    return nc.vector.tensor_tensor_scan(out=exit_[:, 0, 1:RING + 1], data0=col[:, 0, 0, :], data1=col[:, 0, 1, :],
                                                        initial=exit_[:, 0, 0:1], op0=ALU.max, op1=ALU.max)
                elif x == 5:
                    return nc.vector.tensor_copy(exit_[:, W - 1:W, 0], exit_[:, W - 1:W, RING])
                elif w >= 1 and part == 0:
                    src = exit_[:, w - 1, 1:RING + 1]
                    return nc.vector.tensor_tensor(out=passed[:, :, :], in0=pt[:, w, :, :],
                                                   in1=bass.AP(src.tensor, src.offset, [list(src.ap[0]), [-1, 2], [1, RING]]), op=ALU.mult)
                elif w >= 1 and part == 2:
                    return nc.vector.tensor_tensor_scan(out=exit_[:, w, 1:RING + 1], data0=passed[:, 0, :], data1=passed[:, 1, :],
                                                        initial=exit_[:, w, 0:1], op0=ALU.max, op1=ALU.max)

            def leave_column(c, c_par, slot):
                x = (slot - LEAVE0) % 64
                new = 1 - c_par if slot >= LEAVE0 else c_par
                if slot == LEAVE0 - 2:
                    dve.wait_ge(leave_kept, c + 1)
                    return nc.vector.tensor_copy(leave[1 - c_par][:, :, 0], leave[c_par][:, :, RING])
                if x == 0:
                    dve.wait_ge(column_ready, c + 1)
                if x % 4 == 0:
                    w = x // 4
                    return nc.vector.tensor_tensor_scan(out=leave[new][:, w, 1:RING + 1], data0=column[new][:, w, 0, :], data1=column[new][:, w, 1, :],
                                                        initial=leave[new][:, w, 0:1], op0=ALU.max, op1=ALU.max)

            def aside(c, c_par, slot):
                done = [mark(c_par, slot), leave_block(c, c_par, slot), leave_column(c, c_par, slot)]
                if slot == 5:
                    done.append(nc.vector.tensor_copy(rows[:, 0, :], rows[:, RING, :]))
                return ([None] + [last for last in done if last is not None])[-1]

            from_left = [(p - 1) % NK for p in range(NK)]

            def chunk(c, c_par):
                dve.sem_clear(tch)
                for u in range(RING):
                    hf = u // HALF
                    cur, prev = rows[:, u + 1, :], rows[:, u if u else RING, :]
                    shuffle = nc.vector.stream_shuffle(left0[:, :], prev[:, W:CELL], from_left)
                    if u % HALF == 0:
                        shuffle.then_inc(rows_ready[1 - hf], 1)
                    if u == 6:
                        shuffle.then_inc(points_ready, 1)
                    if u == EXIT0 // 2 + 1:
                        shuffle.then_inc(exit_ready, 1)
                    if u == LEAVE0 // 2 - 1:
                        shuffle.then_inc(leave_ready, 1)
                    nc.vector.tensor_tensor(out=upper[:, u, 1:CELL], in0=prev[:, 0:W], in1=prev[:, 1:CELL], op=ALU.min).then_inc(tch, 1)
                    aside(c, c_par, 2 * u)
                    if u % HALF == 0:
                        dve.wait_ge(dist_in[hf], c * 16 + 16)
                    dve.wait_ge(tch, 2 * u + 1)
                    nc.vector.tensor_tensor_scan(out=cur, data0=upper[:, u, :], data1=dist[hf][:, (u % HALF) * CELL:(u % HALF + 1) * CELL],
                                                 initial=left0[:, :], op0=ALU.min, op1=ALU.add).then_inc(tch, 1)
                    aside(c, c_par, 2 * u + 1)
                    dve.wait_ge(tch, 2 * u + 2)

            nc.vector.tensor_scalar(out=rows[:, RING, 0:1], in0=h["first_block"][:, :], scalar1=-BIG, scalar2=BIG,
                                    op0=ALU.mult, op1=ALU.add).then_inc(tch, 1)
            dve.wait_ge(tch, 1)
            dve.sem_inc(rows_ready[0], 1)
            with dve.Fori(0, ST) as n:
                for i in range(PER):
                    chunk(n * PER + i, i % 2)
            chunk(CHUNKS - 1, 0)
            dve.sem_clear(tch)
            at, waited = [], 0
            for c, slots in (CHUNKS, 64), (CHUNKS + 1, LEAVE0 - 3):
                for slot in range(slots):
                    now = 64 * c + slot
                    before = sum(x <= now - 2 for x in at)
                    if before > waited:
                        dve.wait_ge(tch, before)
                        waited = before
                    if (c, slot) == (CHUNKS, 13):
                        dve.sem_inc(points_ready, 1)
                    if slot == EXIT0 + 2:
                        dve.sem_inc(exit_ready, 1)
                    if c == CHUNKS:
                        last = aside(c, c % 2, slot)
                    elif slot <= EXIT0 and slot % 2 == 0:
                        last = leave_block(c, c % 2, slot)
                    else:
                        last = leave_column(c, c % 2, slot)
                    if last is not None:
                        at.append(now)
                        last.then_inc(tch, 1)
                    if slot == LEAVE0 - 4:
                        waited = len(at)
                        dve.wait_ge(tch, waited)
                        dve.sem_inc(leave_ready, 1)

        @block.tensor
        def _(pe):
            for n, it in enumerate(range(1, ST)):
                distance_matmuls(nc, pe, h, bank, it, d_done, lambda b: pe.wait_ge(d_evac, B * (n - 1) + b + 1) if n else None)
                pe.wait_ge(newton, n + 1)
                if n:
                    pe.wait_ge(w_ev, B * n)
                distance_transposes(nc, h, bank, w_T)

        @block.scalar
        def _(act):
            for n, it in enumerate(range(1, ST)):
                for b in range(B):
                    act.wait_ge(d_done, B * n + b + 1)
                    nc.scalar.activation(d2[:, b, :], bank[4 + b][:, :], ACT.Relu, bias=h["aa"][:, b * ST + it:b * ST + it + 1]).then_inc(d_evac, 1)
                act.wait_ge(d_evac, B * (n + 1))
                nc.scalar.activation(half_inv, d2, ACT.Ln, bias=h["tiny"][:, :]).then_inc(log_ready, 1)
                act.wait_ge(log_ready, n + 1)
                nc.scalar.activation(half_inv, half_inv, ACT.Exp, scale=-0.5, bias=h["lnhalf"][:, :])
                nc.scalar.activation(root, d2, ACT.Sqrt).then_inc(root_ready, 1)
                act.wait_ge(d_out, 16 * (n + 1))
                for g in range(4):
                    act.wait_ge(w_T, 4 * n + g + 1)
                    nc.scalar.activation(laid[:, :, 1 + 4 * g:5 + 4 * g].rearrange("p i w -> p w i"),
                                         bank[g][:, :].rearrange("p (w i) -> p w i", w=4), ACT.Copy).then_inc(w_ev, 1)
                act.wait_ge(w_ev, 4 * (n + 1))
                act.dma_start(dd[:, PAD + it * P:PAD + (it + 1) * P, :], laid).then_inc(d_out, 16)

        @block.gpsimd
        def _(pool):
            pool.sem_inc(first_ready, 1)
            pool.sem_inc(column_ready, 1)
            pool.sem_inc(leave_kept, 2)
            pool.sem_inc(exit_kept, 3)

            def entries(c, c_par):
                pool.wait_ge(points_ready, c + 2)
                at = lambda tab: tab[:, :, bass.ds(c * RING, RING)]
                nc.gpsimd.tensor_tensor(out=column[c_par][:, 0, :, :], in0=points[c_par][:, 0, :, :], in1=at(when0), op=ALU.mult).then_inc(first_ready, 1)
                nc.gpsimd.tensor_tensor(out=column[c_par][:, 1:W, :, :], in0=points[c_par][:, 1:W, :, :],
                                        in1=at(when).unsqueeze(1).to_broadcast([P, W - 1, 2, RING]), op=ALU.mult).then_inc(column_ready, 1)

            def keep(c, c_par):
                pool.wait_ge(exit_ready, c + 3)
                nc.gpsimd.tensor_copy(dexit[:, bass.ds(c * RING + RING, RING)], dexit_ring[c_par][:, :]).then_inc(exit_kept, 1)
                pool.wait_ge(leave_ready, c + 3)
                nc.gpsimd.tensor_tensor(out=dleave[:, :, bass.ds(c * RING + RING, RING)], in0=leave[c_par][:, :, 1:RING + 1],
                                        in1=leave[c_par][:, :, 0:RING], op=ALU.subtract).then_inc(leave_kept, 1)

            def refine(tile, b):
                pool.wait_ge(root_ready, tile)
                r, done = root[:, b, :], 4 * b
                if b:
                    pool.wait_ge(nch, done)
                nc.gpsimd.tensor_tensor(out=residual, in0=r, in1=r, op=ALU.mult).then_inc(nch, 1)
                pool.wait_ge(nch, done + 1)
                nc.gpsimd.tensor_tensor(out=residual, in0=d2[:, b, :], in1=residual, op=ALU.subtract).then_inc(nch, 1)
                pool.wait_ge(nch, done + 2)
                nc.gpsimd.tensor_tensor(out=residual, in0=residual, in1=half_inv[:, b, :], op=ALU.mult).then_inc(nch, 1)
                pool.wait_ge(nch, done + 3)
                nc.gpsimd.tensor_tensor(out=r, in0=r, in1=residual, op=ALU.add).then_inc(nch, 1)
                if b == B - 1:
                    pool.wait_ge(nch, 4 * B)
                    pool.sem_inc(newton, 1)

            def tile_chunks(n, next_tile):
                if next_tile:
                    pool.sem_clear(nch)
                for i in range(PER):
                    c = n * PER + i
                    entries(c, i % 2)
                    keep(c - 1, 1 - i % 2)
                    if next_tile and i < 2:
                        refine(n + 1, 2 * i)
                        refine(n + 1, 2 * i + 1)

            with pool.Fori(0, ST - 1) as n:
                tile_chunks(n, True)
            tile_chunks(ST - 1, False)
            entries(CHUNKS - 1, 0)
            keep(CHUNKS - 2, 1)
            keep(CHUNKS - 1, 0)


def trace_path(nc, h):
    ctx = ExitStack()
    with ctx:
        sb = lambda name, shape, dt=F32: ctx.enter_context(nc.sbuf_tensor(name, shape, dt))
        sem = lambda name: ctx.enter_context(nc.semaphore(name))
        dleave, dexit, steps = h["dleave"], h["dexit"], h["steps"]
        step1 = sb("step1", [P, STEPS])
        junk = sb("junkC", [P, STEPS])
        last, not_last = h["last_block"], sb("not_last", [P, 1])
        entry = sb("entry", [P, 1])
        found = sb("found", [P, 2])
        at = sb("at", [P, W + 1])
        ati = sb("ati", [P, W + 1], I32)
        atf = sb("atf", [P, W + 1])
        AT_ONCE = 16
        span = sb("span", [P, 2, W], F16)
        tch, span_ready, span_out, c_high = sem("tchC"), sem("span_ready"), sem("span_out"), sem("c_high")
        wn = h["wn1"]
        full = sb("full", [P, 2, 512])
        bank = [ctx.enter_context(nc.psum_tensor(f"pC{i}", [P, 512], F32)) for i in range(2)]
        w_in, w_T, w_high, w_low = sem("w_inC"), sem("w_TC"), sem("w_highC"), sem("w_lowC")
        block = ctx.enter_context(nc.Block())

        @block.vector
        def _(dve):
            n = [0]

            def link(ins):
                n[0] += 1
                ins.then_inc(tch, 1)
                dve.wait_ge(tch, n[0])

            def look(out, steps_, e, table):
                link(nc.vector.scalar_tensor_tensor(out=junk[:, :], in0=steps_, scalar=e, in1=table, op0=ALU.is_le, op1=ALU.mult, accum_out=out))

            nc.vector.memset(entry[:, :], float(STEPS - 1))
            nc.vector.tensor_scalar(out=not_last[:, :], in0=last[:, :], scalar1=-1.0, scalar2=1.0, op0=ALU.mult, op1=ALU.add)
            link(nc.vector.tensor_scalar(out=step1[:, :], in0=steps[:, :], scalar1=1.0, scalar2=None, op0=ALU.add))
            look(found[:, 0:1], step1[:, :], entry[:, :], dexit[:, RING:])
            link(nc.vector.tensor_scalar(out=dexit[:, :], in0=dexit[:, :], scalar1=not_last[:, :], scalar2=None, op0=ALU.mult))
            link(nc.vector.scalar_tensor_tensor(out=dexit[:, RING:RING + 1], in0=found[:, 0:1], scalar=last[:, :], in1=dexit[:, RING:RING + 1], op0=ALU.mult, op1=ALU.add))
            from_right = [min(k + 1, NK - 1) for k in range(NK)]
            with dve.Fori(0, NK // AT_ONCE) as _:
                dve.sem_clear(tch)
                for i in range(AT_ONCE):
                    nc.vector.stream_shuffle(entry[:, :], found[:, 0:1], from_right).then_inc(tch, 1)
                    dve.wait_ge(tch, 2 * i + 1)
                    nc.vector.scalar_tensor_tensor(out=junk[:, :], in0=step1[:, :], scalar=entry[:, :], in1=dexit[:, RING:], op0=ALU.is_le,
                                                   op1=ALU.mult, accum_out=found[:, 0:1]).then_inc(tch, 1)
                    dve.wait_ge(tch, 2 * i + 2)
            dve.sem_clear(tch)
            n[0] = 0
            link(nc.vector.tensor_scalar(out=entry[:, :], in0=entry[:, :], scalar1=not_last[:, :], scalar2=None, op0=ALU.mult))
            link(nc.vector.scalar_tensor_tensor(out=entry[:, :], in0=last[:, :], scalar=float(STEPS - 1), in1=entry[:, :], op0=ALU.mult, op1=ALU.add))
            link(nc.vector.tensor_scalar(out=at[:, W:W + 1], in0=entry[:, :], scalar1=-1.0, scalar2=None, op0=ALU.add))
            for w in reversed(range(W)):
                look(at[:, w:w + 1], steps[:, :], at[:, w + 1:w + 2], dleave[:, w, RING:])
            link(nc.vector.tensor_copy(ati[:, :], at[:, :]))
            link(nc.vector.tensor_copy(atf[:, :], ati[:, :]))
            link(nc.vector.tensor_tensor(out=at[:, :], in0=at[:, :], in1=atf[:, :], op=ALU.subtract))
            link(nc.vector.scalar_tensor_tensor(out=at[:, :], in0=at[:, :], scalar=4.0, in1=atf[:, :], op0=ALU.mult, op1=ALU.add))
            nc.vector.tensor_scalar(out=span[:, 0, :], in0=at[:, 0:W], scalar1=h["block_id"][:, :], scalar2=None, op0=ALU.subtract)
            nc.vector.tensor_scalar(out=span[:, 1, :], in0=atf[:, 1:W + 1], scalar1=h["block_id"][:, :], scalar2=None, op0=ALU.subtract)\
                .then_inc(span_ready, 1)

        @block.tensor
        def _(pe):
            pe.wait_ge(w_in, 48)
            for q in range(WG):
                if q >= 2:
                    pe.wait_ge(w_high, q - 1)
                for t, src in enumerate(weight_tiles(wn, q)):
                    last = nc.tensor.transpose(bank[q % 2][:, t * P:(t + 1) * P], src, h["ident"][:, :])
                last.then_inc(w_T, 1)

        @block.scalar
        def _(act):
            for q in range(WG):
                act.wait_ge(w_T, q + 1)
                if q >= 2:
                    act.wait_ge(w_low, q - 1)
                nc.scalar.activation(full[:, q % 2, :], bank[q % 2][:, :], ACT.Copy)
                nc.scalar.activation(weight_place(h["wt0"], q, 0), bank[q % 2][:, :], ACT.Copy).then_inc(w_high, 1)
            for b in range(B):
                r = slice(b * ST, (b + 1) * ST)
                nc.scalar.activation(h["C_parts"][:, 0, r, :], h["C"][:, r, :], ACT.Copy).then_inc(c_high, 1)

        @block.gpsimd
        def _(pool):
            for q in range(WG):
                pool.wait_ge(w_high, q + 1)
                nc.gpsimd.tensor_tensor(out=weight_place(h["wt0"], q, 1), in0=full[:, q % 2, :], in1=weight_place(h["wt0"], q, 0).bitcast(F32),
                                        op=ALU.subtract).then_inc(w_low, 1)
            for b in range(B):
                r = slice(b * ST, (b + 1) * ST)
                pool.wait_ge(c_high, b + 1)
                nc.gpsimd.tensor_tensor(out=h["C_parts"][:, 1, r, :], in0=h["C"][:, r, :], in1=h["C_parts"][:, 0, r, :].bitcast(F32), op=ALU.subtract)

        @block.sync
        def _(sp):
            load_weights(sp, h, slice(0, 1), wn, w_in)
            sp.wait_ge(span_ready, 1)
            sp.dma_start(h["spans"].rearrange("s p w -> p s w"), span[:, :, :]).then_inc(span_out, 16)
            sp.wait_ge(span_out, 16)


def align(nc, h):
    ctx = ExitStack()
    with ctx:
        sb = lambda name, shape, dt=F32: ctx.enter_context(nc.sbuf_tensor(name, shape, dt))
        sem = lambda name: ctx.enter_context(nc.semaphore(name))
        X, parts = h["X"], h["C_parts"]
        span = sb("spanD", [P, 2, B * S], F16)
        begun = sb("begun", [P, ST, S], F16)
        path = sb("path", [P, ST, B * S], F32R)
        row = sb("row_id", [P, ST])
        g = sb("gD", [P, 2])
        tg = h["tg"]
        acc = [ctx.enter_context(nc.psum_tensor(f"aD{i}", [P, 2 * D], F32)) for i in range(8)]
        w_in = sem("w_inD")
        span_in, row_ready, g_in, tg_ready = sem("span_in"), sem("row_ready"), sem("g_in"), sem("tg_ready")
        begun_ready, path_ready, sums, x_ready = sem("begun_ready"), sem("path_ready"), sem("sums"), sem("x_readyD")
        block = ctx.enter_context(nc.Block())

        @block.sync
        def _(sp):
            sv = h["spans"].rearrange("s p w -> (s p w)")
            sp.dma_start(span[:, :, :].rearrange("p s j -> p (s j)"), bass.AP(sv.tensor, sv.offset, [[0, P], [1, 2 * B * S]])).then_inc(span_in, 16)
            sp.dma_start(g[:, 0:1], bass.AP(h["g_xattn"].tensor, h["g_xattn"].offset, [[0, P], [1, 1]])).then_inc(g_in, 16)
            sp.dma_start(g[:, 1:2], bass.AP(h["g_ffn"].tensor, h["g_ffn"].offset, [[0, P], [1, 1]])).then_inc(g_in, 16)
            sp.dma_start(h["gw_rows"][:, :], h["gate_w"]).then_inc(w_in, 16)
            sp.dma_start(h["swn"][:, 0, :, :], h["sh_gate_w"].rearrange("(t p) d -> p t d", p=P)).then_inc(w_in, 16)
            sp.dma_start(h["swn"][:, 1, :, :], h["sh_up_w"].rearrange("(t p) d -> p t d", p=P)).then_inc(w_in, 16)
            sp.dma_start(h["sdn"][:, :, :], h["sh_down_w"].rearrange("(t p) f -> p t f", p=P)).then_inc(w_in, 16)
            sp.wait_ge(w_in, 64)

        @block.gpsimd
        def _(pool):
            nc.gpsimd.iota(row[:, :], pattern=[[P, ST]], base=0, channel_multiplier=1, allow_small_or_imprecise_dtypes=True).then_inc(row_ready, 1)

        @block.scalar
        def _(act):
            act.wait_ge(g_in, 32)
            nc.scalar.activation(tg[:, :], g[:, :], ACT.Tanh).then_inc(tg_ready, 1)

        @block.vector
        def _(dve):
            dve.wait_ge(row_ready, 1)
            dve.wait_ge(span_in, 16)
            for b in range(B):
                js = slice(b * S, (b + 1) * S)
                for it in range(ST):
                    nc.vector.tensor_scalar(out=begun[:, it, :], in0=span[:, 0, js], scalar1=row[:, it:it + 1], scalar2=None, op0=ALU.is_le)\
                        .then_inc(begun_ready, 1)
                for it in range(ST):
                    dve.wait_ge(begun_ready, b * ST + it + 1)
                    nc.vector.scalar_tensor_tensor(out=path[:, it, js], in0=span[:, 1, js], scalar=row[:, it:it + 1], in1=begun[:, it, :],
                                                   op0=ALU.is_ge, op1=ALU.mult).then_inc(path_ready, 1)
                if b < B - 1:
                    dve.wait_ge(path_ready, (b + 1) * ST)
            dve.wait_ge(tg_ready, 1)

            def statistics(n):
                dve.wait_ge(x_ready, 2 * n + 2)
                for j in range(2):
                    nc.vector.bn_stats(h["bnst"][:, 2 * n + j, :], X[:, 2 * n + j, :])

            for n in range(2 * B):
                dve.wait_ge(sums, n + 1)
                for j in range(2):
                    nc.vector.scalar_tensor_tensor(out=X[:, 2 * n + j, :], in0=acc[n][:, j * D:(j + 1) * D], scalar=tg[:, 0:1],
                                                   in1=X[:, 2 * n + j, :], op0=ALU.mult, op1=ALU.add).then_inc(x_ready, 1)
                if n:
                    statistics(n - 1)
            statistics(2 * B - 1)

        @block.tensor
        def _(pe):
            for n in range(2 * B):
                b, jp = n // 2, n % 2
                for j in range(2):
                    jt = 2 * jp + j
                    for it in range(ST):
                        if n % 2 == 0 and j == 0:
                            pe.wait_ge(path_ready, b * ST + it + 1)
                        for part in range(2):
                            last = nc.tensor.matmul(acc[n][:, j * D:(j + 1) * D], path[:, it, b * S + jt * P:b * S + (jt + 1) * P],
                                                    parts[:, part, b * ST + it, :], start=(it == 0 and part == 0), stop=(it == ST - 1 and part == 1))
                last.then_inc(sums, 1)


def gather_tokens(nc, h, e, xg, gathered):
    for f in range(2):
        col = E_ * f + e
        nc.gpsimd.indirect_dma_start(out=xg[:, f, :], out_offset=None, in_=h["hx"][:, :],
                                     in_offset=bass.IndirectOffsetOnAxis(ap=h["ids"][:, col:col + 1], axis=0),
                                     bounds_check=NTOK - 1).then_inc(gathered, 16)


def route(nc, h):
    ctx = ExitStack()
    with ctx:
        sb = lambda name, shape, dt=F32: ctx.enter_context(nc.sbuf_tensor(name, shape, dt))
        sem = lambda name: ctx.enter_context(nc.semaphore(name))
        X, ident, ids = h["X"], h["ident"], h["ids"]
        H = h["wn1"][:, 0:NT * D].rearrange("p (t d) -> p t d", d=D)
        swn, sdn, gw = h["swn"], h["sdn"], h["gw_rows"]
        HT = sb("HT", [P, KC, NTOK])
        bnst = h["bnst"]
        mv = sb("mvR", [P, NT, 2])
        sd = sb("sdR", [P, 4, NT])
        gz = sb("gz", [P, KC, SEG, P])
        swT = sb("swT", [P, 2, KC, SH])
        sdT = sb("sdT", [P, SF, D])
        sil = sb("sil", [P, 2, 512])
        hid = sb("hid", [P, 2, SF, 512])
        sout = sb("sout", [P, 2, 2 * D])
        score = sb("score", [P, SEGT])
        scT = sb("scT", [P, 2, P])
        junk = sb("junkR", [P, SEGT])
        T = sb("T", [P, 8])
        bit = sb("bit", [P, 1], I32)
        cnt = sb("cnt", [P, 2])
        off = sb("off", [P, 4])
        gt, eq = sb("gt", [P, SEGT]), sb("eq", [P, SEGT])
        gtc, eqc = sb("gtc", [P, SEGT]), sb("eqc", [P, SEGT])
        zero = sb("zeroR", [P, SEGT])
        pos = sb("pos", [P, SEGT])
        posi = sb("posi", [P, 3, 2 * P], I32)
        posf = sb("posf", [P, 2, 2 * P], BF16)
        iot = sb("iot", [P, P], I32)
        iof = sb("iof", [P, 16])
        v0 = sb("v0", [P, 16])
        v0_col = sb("v0_col", [P, 2 * P], BF16)
        v1 = sb("v1", [P, 1])
        pm = sb("pm", [P, 5, P])
        oa = sb("oa", [P, 2 * E_, 16, 8], BF16)
        ob = sb("ob", [P, 2, 16, 2 * P], BF16)
        idv = sb("idv", [P, 2, P])
        idl = sb("idl", [P, 2, 16])
        lsp = sb("lsp", [P, 4, P])
        bank = [ctx.enter_context(nc.psum_tensor(f"pR{i}", [P, 512], F32)) for i in range(8)]

        varr, rootr, h_ready = sem("varR"), sem("rootR"), sem("h_readyR")
        h_T, h_Te, g_T, g_Te = sem("h_TR"), sem("h_TeR"), sem("g_TR"), sem("g_TeR")
        s_done, s_ready, c_ready, t_done = sem("s_doneR"), sem("s_readyR"), sem("c_readyR"), sem("t_doneR")
        masks, pos_ready, pos_T, oh_ready, idl_done = sem("masksR"), sem("pos_readyR"), sem("pos_TR"), sem("oh_readyR"), sem("idl_doneR")
        scT_done, scT_ready, lsp_ready, ids_done, off_done = sem("scT_doneR"), sem("scT_readyR"), sem("lsp_readyR"), sem("ids_doneR"), sem("off_doneR")
        sw_T, sw_Te, gu_done, sil_ready, hid_ready, dn_done, so_ready = [sem(n) for n in (
            "sw_TR", "sw_TeR", "gu_doneR", "sil_readyR", "hid_readyR", "dn_doneR", "so_readyR")]
        so_out = [sem(f"so_outR{i}") for i in range(2)]
        hx_out, w1_in, hx_stored, x0_in = sem("hx_outR"), sem("w1_inR"), sem("hx_storedR"), sem("x0_inR")
        vch, pch, sch = sem("vchR"), sem("pchR"), sem("schR")
        hx, out = h["hx"], h["out"].rearrange("b s d -> (b s) d")
        idl_sum = lambda g: bank[5][:, 2 * P:4 * P] if g == 0 else bank[6][:, 0:2 * P]
        ROUNDS = 30
        PIECES = []
        for m in range(B * SF):
            PIECES.append(("gate_up", m))
            if m >= SF and m % SF < 2:
                PIECES.append(("down", 2 * (m // SF - 1) + m % SF))
        PIECES += [("down", 2 * B - 2), ("down", 2 * B - 1)]
        SEARCH = ROUNDS // 2
        TAKEN = (ROUNDS - 1 - 3) // 2 + 1
        SW = 6
        PLACES, LISTS, IDS, REST = (PIECES[i:j] for i, j in ((SEARCH, SEARCH + 1), (SEARCH + 1, SEARCH + 3), (SEARCH + 3, SEARCH + 4), (SEARCH + 4, None)))
        block = ctx.enter_context(nc.Block())

        @block.sync
        def _(sp):
            sp.wait_ge(h_ready, NT)
            sp.dma_start(hx[:, 0:D].rearrange("(t p) d -> p t d", p=P), H[:, :, :]).then_inc(hx_out, 16)
            sp.wait_ge(scT_ready, 1)
            hv = hx[:, D:HROW].rearrange("(s f p) e -> p f s e", f=2, p=P)
            for f in range(2):
                sp.dma_start(hv[:, f, :, :], scT[:, f, :].rearrange("p (s e) -> p s e", e=E_)).then_inc(hx_out, 16)
            ov = out.rearrange("(t p) d -> p t d", p=P)
            sp.wait_ge(sw_T, SW)
            sp.wait_ge(hx_out, 48)
            sp.sem_inc(hx_stored, 1)
            load_weights(sp, h, slice(1, 2), h["wn1"], w1_in)
            sp.dma_start(h["bn"][:, 0, :], h["up_b"].rearrange("e (t p) -> (e t) p", p=P)).then_inc(w1_in, 16)
            sp.dma_start(h["bn"][:, 1, :], h["gb"].rearrange("e (t p) -> (e t) p", p=P)).then_inc(w1_in, 16)
            for n in range(2 * B):
                sp.wait_ge(so_ready, n + 1)
                sp.dma_start(ov[:, 2 * n:2 * n + 2, :], sout[:, n % 2, :].rearrange("p (t d) -> p t d", t=2)).then_inc(so_out[n % 2], 16)
            for i in range(2):
                sp.wait_ge(so_out[i], 16 * B)
            sp.wait_ge(w1_in, 80)

        @block.gpsimd
        def _(pool):
            nc.gpsimd.iota(iot[:, :], pattern=[[1, P]], base=0, channel_multiplier=0).then_inc(pch, 1)
            nc.gpsimd.iota(posi[:, 2, 0:1], pattern=[[0, 1]], base=0, channel_multiplier=1).then_inc(pch, 1)
            nc.gpsimd.memset(gz[:, :, :, :], 0.0).then_inc(pch, 1)
            nc.gpsimd.memset(zero[:, :], 0.0).then_inc(pch, 1)
            nc.gpsimd.iota(bit[:, :], pattern=[[0, 1]], base=1 << ROUNDS, channel_multiplier=0).then_inc(pch, 1)
            nc.gpsimd.memset(T[:, :], 0.0).then_inc(pch, 1)
            pool.wait_ge(hx_stored, 1)
            pool.wait_ge(c_ready, B + 1)
            gather_tokens(nc, h, 0, h["xg0"], x0_in)
            pool.wait_ge(x0_in, 32)

        @block.scalar
        def _(act):
            act.wait_ge(varr, 1)
            nc.scalar.activation(sd[:, 1, :], sd[:, 0, :], ACT.Sqrt).then_inc(rootr, 1)
            act.wait_ge(pch, 6)
            act.wait_ge(g_T, 1)
            for s in range(SEG):
                last = nc.scalar.activation(gz[:, :, s, E_ * s:E_ * (s + 1)], bank[7][:, 0:KC * E_].rearrange("p (k e) -> p k e", k=KC), ACT.Copy)
            last.then_inc(g_Te, 1)
            for g in range(SW):
                act.wait_ge(sw_T, g + 1)
                dst = swT[:, g // 2, g % 2, :] if g < 4 else sdT[:, 2 * (g - 4):2 * (g - 4) + 2, :].rearrange("p f d -> p (f d)")
                nc.scalar.activation(dst, bank[5 + g % 2][:, :], ACT.Copy).then_inc(sw_Te, 1)
            for g in range(0, KC * B, 2):
                act.wait_ge(h_T, g + 1)
                nc.scalar.activation(HT[:, g % KC, (g // KC) * 512:(g // KC + 1) * 512], bank[g % 4][:, :], ACT.Copy).then_inc(h_Te, 1)
            act.wait_ge(s_done, 1)
            nc.scalar.activation(score[:, :], bank[6][:, 0:SEGT], ACT.Sigmoid).then_inc(s_ready, 1)
            act.wait_ge(scT_done, 1)
            nc.scalar.activation(scT[:, :, :].rearrange("p a b -> p (a b)"), bank[5][:, 0:2 * P], ACT.Copy).then_inc(scT_ready, 1)
            for kind, m in PIECES:
                if kind == "gate_up":
                    act.wait_ge(gu_done, m + 1)
                    if m >= 2:
                        act.wait_ge(hid_ready, m - 1)
                    nc.scalar.activation(sil[:, m % 2, :], bank[m % 2][:, :], ACT.Silu).then_inc(sil_ready, 1)

        @block.vector
        def _(dve):
            n = [0]

            def link(ins):
                n[0] += 1
                ins.then_inc(vch, 1)
                dve.wait_ge(vch, n[0])

            for i in range(NT):
                last = nc.vector.bn_aggr(mv[:, i, :], bnst[:, i, :])
            link(last)
            nc.vector.tensor_scalar(out=sd[:, 0, :], in0=mv[:, :, 1], scalar1=EPS, scalar2=None, op0=ALU.add).then_inc(varr, 1)
            dve.wait_ge(rootr, 1)
            dve.wait_ge(varr, 1)
            link(nc.vector.reciprocal(sd[:, 2, :], sd[:, 1, :]))
            link(nc.vector.tensor_tensor(out=sd[:, 3, :], in0=sd[:, 0, :], in1=sd[:, 2, :], op=ALU.mult))
            link(nc.vector.tensor_tensor(out=sd[:, 2, :], in0=sd[:, 3, :], in1=sd[:, 1, :], op=ALU.add))
            link(nc.vector.tensor_scalar(out=sd[:, 3, :], in0=sd[:, 2, :], scalar1=0.5, scalar2=None, op0=ALU.mult))
            link(nc.vector.reciprocal(sd[:, 2, :], sd[:, 3, :]))
            for i in range(NT):
                nc.vector.tensor_scalar(out=H[:, i, :], in0=X[:, i, :], scalar1=mv[:, i, 0:1], scalar2=sd[:, 2, i:i + 1],
                                        op0=ALU.subtract, op1=ALU.mult).then_inc(h_ready, 1)
            for g in range(1, KC * B, 2):
                dve.wait_ge(h_T, g + 1)
                nc.vector.tensor_copy(HT[:, g % KC, (g // KC) * 512:(g // KC + 1) * 512], bank[g % 4][:, :]).then_inc(c_ready, 1)

            dve.wait_ge(pch, 6)
            link(nc.vector.tensor_copy(v1[:, :], posi[:, 2, 0:1]))
            link(nc.vector.tensor_scalar(out=posi[:, 0, 0:P], in0=iot[:, :], scalar1=15, scalar2=None, op0=ALU.bitwise_and))
            link(nc.vector.tensor_scalar(out=posi[:, 1, 0:P], in0=iot[:, :], scalar1=4, scalar2=None, op0=ALU.logical_shift_right))
            link(nc.vector.tensor_scalar(out=posi[:, 2, 1:2], in0=posi[:, 2, 0:1], scalar1=15, scalar2=None, op0=ALU.bitwise_and))
            link(nc.vector.tensor_scalar(out=posi[:, 2, 2:3], in0=posi[:, 2, 0:1], scalar1=4, scalar2=None, op0=ALU.logical_shift_right))
            link(nc.vector.tensor_copy(T[:, 4:6], posi[:, 2, 1:3]))
            link(nc.vector.tensor_copy(pm[:, 2:4, :], posi[:, 0:2, 0:P]))
            link(nc.vector.tensor_copy(iof[:, :], pm[:, 2, 0:16]))
            link(nc.vector.tensor_scalar(out=pm[:, 0, :], in0=pm[:, 2, :], scalar1=T[:, 4:5], scalar2=None, op0=ALU.is_equal))
            link(nc.vector.scalar_tensor_tensor(out=pm[:, 1, :], in0=pm[:, 3, :], scalar=T[:, 5:6], in1=pm[:, 0, :],
                                                op0=ALU.is_gt, op1=ALU.mult))
            link(nc.vector.tensor_scalar(out=v0[:, 0:8], in0=iof[:, 0:8], scalar1=2.0, scalar2=None, op0=ALU.mult))
            link(nc.vector.tensor_scalar(out=v0[:, 8:16], in0=v0[:, 0:8], scalar1=1.0, scalar2=None, op0=ALU.add))
            link(nc.vector.tensor_copy(v0_col[:, :].rearrange("p (c e) -> p c e", e=E_), v0[:, :].unsqueeze(2).to_broadcast([P, 16, E_])))
            link(nc.vector.tensor_scalar(out=posi[:, 2, 1:2], in0=posi[:, 2, 0:1], scalar1=7, scalar2=None, op0=ALU.bitwise_and))
            link(nc.vector.tensor_scalar(out=posi[:, 2, 2:3], in0=posi[:, 2, 0:1], scalar1=3, scalar2=None, op0=ALU.logical_shift_right))
            link(nc.vector.tensor_copy(T[:, 6:8], posi[:, 2, 1:3]))
            nc.vector.tensor_scalar(out=pm[:, 4, :], in0=pm[:, 2, :], scalar1=T[:, 7:8], scalar2=None, op0=ALU.is_equal)
            nc.vector.tensor_scalar(out=pm[:, 3, :], in0=pm[:, 3, :], scalar1=T[:, 6:7], scalar2=None, op0=ALU.is_equal).then_inc(masks, 1)

            def hidden_units(m):
                dve.wait_ge(sil_ready, m + 1)
                if m >= 2 * SF and m % SF == 0:
                    dve.wait_ge(dn_done, 2 * (m // SF - 1))
                nc.vector.tensor_tensor(out=hid[:, (m // SF) % 2, m % SF, :], in0=sil[:, m % 2, :], in1=bank[2 + m % 2][:, :],
                                        op=ALU.mult).then_inc(hid_ready, 1)

            def output(m):
                dve.wait_ge(dn_done, m + 1)
                if m >= 2:
                    dve.wait_ge(so_out[m % 2], 16 * (m // 2))
                nc.vector.scalar_tensor_tensor(out=sout[:, m % 2, :], in0=bank[4 if m % 2 == 0 else 7][:, :], scalar=h["tg"][:, 1:2],
                                               in1=X[:, 2 * m:2 * m + 2, :].rearrange("p t d -> p (t d)"), op0=ALU.mult, op1=ALU.add).then_inc(so_ready, 1)

            def take(pieces):
                for kind, m in pieces:
                    hidden_units(m) if kind == "gate_up" else output(m)

            dve.wait_ge(masks, 1)
            dve.wait_ge(s_ready, 1)
            Ti, Ci = T[:, 0:1].bitcast(I32), T[:, 1:2].bitcast(I32)
            dve.sem_clear(sch)
            for r in range(ROUNDS):
                nc.vector.tensor_scalar(out=bit[:, :], in0=bit[:, :], scalar1=1, scalar2=None, op0=ALU.logical_shift_right).then_inc(sch, 1)
                dve.wait_ge(sch, 4 * r + 1)
                nc.vector.tensor_tensor(out=Ci, in0=Ti, in1=bit[:, :], op=ALU.bitwise_or).then_inc(sch, 1)
                dve.wait_ge(sch, 4 * r + 2)
                nc.vector.tensor_scalar(out=junk[:, :], in0=score[:, :], scalar1=T[:, 1:2], scalar2=0.0, op0=ALU.is_ge, op1=ALU.add,
                                        accum_out=cnt[:, 0:1]).then_inc(t_done, 1)
                done, half = divmod(r - 3, 2)
                if done >= 0 and half == 0:
                    take([PIECES[done]])
                dve.wait_ge(off_done, r + 1)
                nc.vector.scalar_tensor_tensor(out=T[:, 2:3], in0=bank[6][:, 256:257], scalar=float(CAP), in1=T[:, 1:2],
                                               op0=ALU.is_ge, op1=ALU.mult).then_inc(sch, 1)
                dve.wait_ge(sch, 4 * r + 3)
                nc.vector.tensor_tensor(out=T[:, 0:1], in0=T[:, 0:1], in1=T[:, 2:3], op=ALU.max).then_inc(sch, 1)
                dve.wait_ge(sch, 4 * r + 4)
            nc.vector.tensor_scalar(out=gt[:, :], in0=score[:, :], scalar1=T[:, 0:1], scalar2=0.0, op0=ALU.is_gt, op1=ALU.add,
                                    accum_out=cnt[:, 0:1])
            nc.vector.tensor_scalar(out=eq[:, :], in0=score[:, :], scalar1=T[:, 0:1], scalar2=0.0, op0=ALU.is_equal, op1=ALU.add,
                                    accum_out=cnt[:, 1:2]).then_inc(t_done, 1)
            take(PIECES[TAKEN:SEARCH])
            dve.wait_ge(t_done, ROUNDS + 1)
            nc.vector.tensor_tensor_scan(out=gtc[:, :], data0=gt[:, :], data1=zero[:, :], initial=0.0, op0=ALU.add, op1=ALU.add)
            link(nc.vector.tensor_tensor_scan(out=eqc[:, :], data0=eq[:, :], data1=zero[:, :], initial=0.0, op0=ALU.add, op1=ALU.add))
            dve.wait_ge(off_done, ROUNDS + 1)
            link(nc.vector.tensor_copy(off[:, :], bank[6][:, 264:268]))
            link(nc.vector.tensor_tensor(out=off[:, 1:2], in0=off[:, 1:2], in1=off[:, 2:3], op=ALU.add))
            link(nc.vector.tensor_scalar(out=off[:, 0:2], in0=off[:, 0:2], scalar1=-4097.0, scalar2=None, op0=ALU.add))
            link(nc.vector.scalar_tensor_tensor(out=gtc[:, :], in0=gtc[:, :], scalar=off[:, 0:1], in1=gt[:, :], op0=ALU.add, op1=ALU.mult))
            link(nc.vector.scalar_tensor_tensor(out=eqc[:, :], in0=eqc[:, :], scalar=off[:, 1:2], in1=eq[:, :], op0=ALU.add, op1=ALU.mult))
            nc.vector.scalar_tensor_tensor(out=pos[:, :], in0=gtc[:, :], scalar=4096.0, in1=eqc[:, :], op0=ALU.add, op1=ALU.add)\
                .then_inc(pos_ready, 1)
            take(PLACES)
            dve.wait_ge(pos_T, 1)
            link(nc.vector.tensor_copy(posi[:, 0, :], bank[5][:, 0:2 * P]))
            nc.vector.tensor_scalar(out=posi[:, 1, :], in0=posi[:, 0, :], scalar1=4, scalar2=None, op0=ALU.logical_shift_right)
            link(nc.vector.tensor_scalar(out=posi[:, 2, :], in0=posi[:, 0, :], scalar1=15, scalar2=None, op0=ALU.bitwise_and))
            link(nc.vector.tensor_copy(posf[:, :, :], posi[:, 1:3, :]))
            for v in range(16):
                nc.vector.tensor_scalar(out=oa[:, :, v, :], in0=posf[:, 0, :].rearrange("p (c e) -> p c e", e=8), scalar1=float(v), scalar2=None, op0=ALU.is_equal)
                last = nc.vector.tensor_scalar(out=ob[:, 1, v, :], in0=posf[:, 1, :], scalar1=float(v), scalar2=None, op0=ALU.is_equal)
            link(last)
            vc = v0_col[:, :]
            nc.vector.tensor_tensor(out=ob[:, 0, :, :], in0=ob[:, 1, :, :], in1=bass.AP(vc.tensor, vc.offset, [list(vc.ap[0]), [0, 16], [1, 2 * P]]),
                                    op=ALU.mult).then_inc(oh_ready, 1)
            dve.wait_ge(oh_ready, 1)
            nc.vector.tensor_scalar(out=ob[:, 1, :, :], in0=ob[:, 1, :, :], scalar1=v1[:, 0:1], scalar2=None, op0=ALU.mult).then_inc(oh_ready, 1)
            take(LISTS)
            dve.wait_ge(idl_done, 2)
            for g in range(2):
                eb = lambda ap: ap.rearrange("p (e b) -> p e b", e=8)
                part = lambda v: idl_sum(g)[:, v * P:(v + 1) * P].rearrange("p (b e) -> p e b", e=8)
                link(nc.vector.tensor_copy(eb(idv[:, 0, :]), part(1)))
                link(nc.vector.scalar_tensor_tensor(out=eb(idv[:, 1, :]), in0=part(0), scalar=float(P), in1=eb(idv[:, 0, :]),
                                                    op0=ALU.mult, op1=ALU.add))
                link(nc.vector.tensor_tensor(out=idv[:, 0, :].rearrange("p (e b) -> p e b", e=8),
                                             in0=idv[:, 1, :].rearrange("p (e b) -> p e b", e=8),
                                             in1=pm[:, 3, 0:P].rearrange("p (e b) -> p e b", e=8), op=ALU.mult))
                link(nc.vector.tensor_reduce(out=idl[:, g, :], in_=idv[:, 0, :].rearrange("p (e b) -> p b e", e=8),
                                             axis=mybir.AxisListType.X, op=ALU.add))
                for f in range(2):
                    last = nc.vector.tensor_tensor(out=lsp[:, 2 * g + f, :].rearrange("p (b a) -> p b a", a=16),
                                                   in0=idl[:, g, 8 * f:8 * f + 8].unsqueeze(2).to_broadcast([P, 8, 16]),
                                                   in1=pm[:, 4, :].rearrange("p (b a) -> p b a", a=16), op=ALU.mult)
                link(last)
            nc.vector.tensor_copy(v1[:, :], v0[:, 0:1]).then_inc(lsp_ready, 1)
            take(IDS)
            dve.wait_ge(ids_done, 1)
            nc.vector.tensor_copy(ids[:, :], bank[5][:, 0:2 * E_]).then_inc(c_ready, 1)
            take(REST)

        @block.tensor
        def _(pe):
            for kc in range(KC):
                last = nc.tensor.transpose(bank[7][:, kc * E_:(kc + 1) * E_], gw[:, kc * P:(kc + 1) * P], ident[0:E_, 0:E_])
            last.then_inc(g_T, 1)

            def weights(g):
                if g >= 2:
                    pe.wait_ge(sw_Te, g - 1)
                for t in range(4):
                    if g < 4:
                        src = swn[:, g // 2, t, (g % 2) * P:(g % 2 + 1) * P]
                    else:
                        src = sdn[:, t % 2, (2 * (g - 4) + t // 2) * P:(2 * (g - 4) + t // 2 + 1) * P]
                    last = nc.tensor.transpose(bank[5 + g % 2][:, t * P:(t + 1) * P], src, ident[:, :])
                last.then_inc(sw_T, 1)

            for g in range(SW):
                weights(g)
            for g in range(KC * B):
                pe.wait_ge(h_ready, (g // KC + 1) * ST)
                if g >= 4:
                    pe.wait_ge((h_Te, c_ready)[g % 2], (g - 4) // 2 + 1)
                for t in range(ST):
                    last = nc.tensor.transpose(bank[g % 4][:, t * P:(t + 1) * P],
                                               H[:, (g // KC) * ST + t, (g % KC) * P:(g % KC + 1) * P], ident[:, :])
                last.then_inc(h_T, 1)
            pe.wait_ge(g_Te, 1)
            pe.wait_ge(sw_Te, SW)
            pe.wait_ge(h_Te, B)
            pe.wait_ge(c_ready, B)
            for s in range(SEG):
                for kc in range(KC):
                    last = nc.tensor.matmul(bank[6][:, 0:SEGT], gz[:, kc, s, :], HT[:, kc, s * SEGT:(s + 1) * SEGT],
                                            start=(s == 0 and kc == 0), stop=(s == SEG - 1 and kc == KC - 1))
            last.then_inc(s_done, 1)
            pe.wait_ge(masks, 1)
            pe.wait_ge(s_ready, 1)
            for f in range(2):
                last = nc.tensor.transpose(bank[5][:, f * P:(f + 1) * P], score[:, f * P:(f + 1) * P], ident[:, :])
            last.then_inc(scT_done, 1)
            def gate_up(m, halves=(0, 1)):
                tg, ft = m // SF, m % SF
                for v in halves:
                    if m == 0 and v == 0:
                        pe.wait_ge(sw_Te, SW)
                    if m >= 2 and v == 0:
                        pe.wait_ge(sil_ready, m - 1)
                        pe.wait_ge(hid_ready, m - 1)
                    for kc in range(KC):
                        last = nc.tensor.matmul(bank[2 * v + m % 2][:, :], swT[:, v, kc, ft * P:(ft + 1) * P],
                                                HT[:, kc, tg * 512:(tg + 1) * 512], start=(kc == 0), stop=(kc == KC - 1))
                    if v == 1:
                        last.then_inc(gu_done, 1)

            def down(m, halves=(0, 1)):
                tg, jp = m // 2, m % 2
                for j in halves:
                    if j == 0:
                        pe.wait_ge(hid_ready, (tg + 1) * SF)
                    if m >= 2 and j == 0:
                        pe.wait_ge(so_ready, m - 1)
                    for ft in range(SF):
                        last = nc.tensor.matmul(bank[4 if m % 2 == 0 else 7][:, j * D:(j + 1) * D],
                                                hid[:, tg % 2, ft, (2 * jp + j) * P:(2 * jp + j + 1) * P], sdT[:, ft, :],
                                                start=(ft == 0), stop=(ft == SF - 1))
                    if j == 1:
                        last.then_inc(dn_done, 1)

            def make(pieces, *halves):
                for kind, m in pieces:
                    (gate_up if kind == "gate_up" else down)(m, *halves)

            for r in range(ROUNDS):
                pe.wait_ge(t_done, r + 1)
                nc.tensor.matmul(bank[6][:, 256:257], pm[:, 0, :], cnt[:, 0:1], start=True, stop=True).then_inc(off_done, 1)
                make([PIECES[r // 2]], [r % 2])
            pe.wait_ge(t_done, ROUNDS + 1)
            nc.tensor.matmul(bank[6][:, 264:266], pm[:, 1, :], cnt[:, :], start=True, stop=True)
            nc.tensor.matmul(bank[6][:, 266:268], pm[:, 0, :], cnt[:, :], start=True, stop=True).then_inc(off_done, 1)
            make(PLACES)
            pe.wait_ge(pos_ready, 1)
            for f in range(2):
                last = nc.tensor.transpose(bank[5][:, f * P:(f + 1) * P], pos[:, f * P:(f + 1) * P], ident[:, :])
            last.then_inc(pos_T, 1)
            make(LISTS)
            pe.wait_ge(oh_ready, 2)
            for g in range(2):
                for c in range(16):
                    lhs = oa[:, 2 * c + g, :, :].rearrange("p a e -> p (a e)")
                    rhs = ob[:, :, :, c * E_ + 8 * g:c * E_ + 8 * g + 8]
                    last = nc.tensor.matmul(idl_sum(g), lhs, rhs, start=(c == 0), stop=(c == 15))
                last.then_inc(idl_done, 1)
            make(IDS)
            pe.wait_ge(lsp_ready, 1)
            for f in range(2):
                for g in range(2):
                    last = nc.tensor.matmul(bank[5][:, E_ * f + 8 * g:E_ * f + 8 * g + 8], lsp[:, 2 * g + f, :],
                                            pm[:, 3, :].rearrange("p (e a) -> p e a", a=16)[:, :, 0], start=True, stop=True)
            last.then_inc(ids_done, 1)
            make(REST)


def run_experts(nc, h):
    ctx = ExitStack()
    with ctx:
        sb = lambda name, shape, dt=F32: ctx.enter_context(nc.sbuf_tensor(name, shape, dt))
        sem = lambda name: ctx.enter_context(nc.semaphore(name))
        two = lambda name: [sem(f"{name}{i}") for i in range(2)]
        ident, ids = h["ident"], h["ids"]
        wn = [sb("wn0", [P, WSIZE]), h["wn1"]]
        wt = [h["wt0"], sb("wt1", [P, 2, 3, KC * F], F32R)]
        xg = [h["xg0"], sb("xg1", [P, 2, HROW])]
        xgT = [sb(f"xgT{i}", [P, 2, KC, CAP], F32R) for i in range(2)]
        bT = sb("bT", [P, 2, E_ * FT])
        db = [sb(f"db{i}", [P, D]) for i in range(2)]
        sil = sb("silE", [P, 2, CAP])
        FREE = 4
        hidden_full = sb("hidden_full", [P, FREE, CAP])
        hid = sb("hidE", [P, 2, FT, CAP], F32R)
        so = sb("so", [P, 2, 2, D])
        tmp = sb("tmpE", [P, 2, D])
        tr = [ctx.enter_context(nc.psum_tensor(f"tr{i}", [P, 512], F32)) for i in range(3)]
        gps = [ctx.enter_context(nc.psum_tensor(f"gps{i}", [P, CAP], F32)) for i in range(2)]
        ups = [ctx.enter_context(nc.psum_tensor(f"ups{i}", [P, CAP], F32)) for i in range(2)]
        ops = ctx.enter_context(nc.psum_tensor("ops", [P, 2, D], F32))
        w_in, x_in, scattered = two("w_inE"), two("x_inE"), two("scattered")
        db_in = two("db_inE")
        b_T, b_Te = sem("b_TE"), sem("b_TeE")
        tr_done, tr_high, tr_low = sem("tr_done"), sem("tr_high"), sem("tr_low")
        ou, so_free = two("output_usedE"), two("so_freeE")
        g_done, u_done, s_rdy, h_rdy, o_done, o_rdy, t_rdy = [sem(n) for n in ("g_doneE", "u_doneE", "s_rdyE", "h_rdyE", "o_doneE", "o_rdyE", "t_rdyE")]
        h_high, h_low = sem("h_highE"), sem("h_lowE")
        block = ctx.enter_context(nc.Block())
        NG = WG + 1
        TERMS = ((0, 0), (1, 0), (0, 1))
        out = h["out"].rearrange("b s d -> (b s) d")
        dbv = bass.AP(h["down_b"].tensor, h["down_b"].offset, [[0, P], [D, E_], [1, D]])
        PAIRS = E_ // 2

        def one(e):
            return bass.ds(e, 1) if not isinstance(e, int) else slice(e, e + 1)

        def count(n, k, per, more):
            return n * (2 * per) + (k * per + more)

        def experts(engine, step):
            with engine.Fori(0, PAIRS - 1) as n:
                step(n, 0, (n, 1))
                step(n, 1, (n + 1, 0))
            step(PAIRS - 1, 0, (PAIRS - 1, 1))
            step(PAIRS - 1, 1, None)

        @block.sync
        def _(sp):
            def load_bias(n, k):
                sp.dma_start(db[k][:, :].rearrange("p (o d) -> p o d", o=1), dbv[:, one(n * 2 + k), :]).then_inc(db_in[k], 16)

            for k in range(2):
                sp.sem_inc(w_in[k], 48)
                load_bias(0, k)
            with sp.Fori(1, PAIRS) as n:
                for k in range(2):
                    sp.wait_ge(tr_done, count(n, k, NG, -NG - 1))
                    load_weights(sp, h, one(n * 2 + k), wn[k], w_in[k])
                    sp.wait_ge(ou[k], n)
                    load_bias(n, k)

        @block.gpsimd
        def _(pool):
            def gather(e):
                k = e % 2
                if e >= 2:
                    pool.wait_ge(ou[k], e // 2)
                gather_tokens(nc, h, e, xg[k], x_in[k])

            for k in range(2):
                pool.sem_inc(so_free[k], 1)
            pool.sem_inc(h_low, FREE)
            for e in range(E_):
                k = e % 2
                if e + 1 < E_:
                    gather(e + 1)
                for ft in range(FT):
                    pool.wait_ge(h_high, e * FT + ft + 1)
                    nc.gpsimd.tensor_tensor(out=hid[:, 1, ft, :], in0=hidden_full[:, ft % FREE, :], in1=hid[:, 0, ft, :].bitcast(F32),
                                            op=ALU.subtract).then_inc(h_low, 1)
                if e:
                    pool.wait_ge(scattered[1 - k], 32 * ((e + 1) // 2))
                    pool.sem_inc(so_free[1 - k], 1)
                pool.wait_ge(o_rdy, 2 * (e + 1))
                for f in range(2):
                    nc.gpsimd.indirect_dma_start(out=out[:, :],
                                                 out_offset=bass.IndirectOffsetOnAxis(ap=ids[:, E_ * f + e:E_ * f + e + 1], axis=0),
                                                 in_=so[:, k, f, :], in_offset=None, bounds_check=NTOK - 1,
                                                 compute_op=ALU.add).then_inc(scattered[k], 16)
            for k in range(2):
                pool.wait_ge(scattered[k], 32 * PAIRS)

        def sources(q, k):
            return weight_tiles(wn[k], q) if q < WG else [xg[k][:, t % 2, (t // 2) * P:(t // 2 + 1) * P] for t in range(4)]

        def target(q, k, part):
            return weight_place(wt[k], q, part) if q < WG else xgT[k][:, part, :, :].rearrange("p a b -> p (a b)")

        @block.tensor
        def _(pe):
            for m in range(2):
                last = nc.tensor.transpose(ops[:, 0, m * P:(m + 1) * P], h["bn"][:, m, :], ident[:, :])
            last.then_inc(b_T, 1)

            def transposes(n, k, groups):
                for q in groups:
                    if q == 0:
                        pe.wait_ge(w_in[k], n * 48 + 48)
                    if q == WG and k == 1:
                        pe.wait_ge(x_in[k], n * 32 + 32)
                    if q == WG and k == 0 and not (isinstance(n, int) and n == 0):
                        pe.wait_ge(x_in[k], n * 32)
                    before = 0 if q == 0 else -2
                    if not isinstance(n, int) or count(n, k, NG, q + before) > 0:
                        pe.wait_ge(tr_low, count(n, k, NG, q + before))
                    for t, s in enumerate(sources(q, k)):
                        last = nc.tensor.transpose(tr[q % 3][:, t * P:(t + 1) * P], s, ident[:, :])
                    last.then_inc(tr_done, 1)

            def up_gate(n, k, ft):
                for m, (ps, done, taken) in enumerate(((ups, u_done, h_rdy), (gps, g_done, s_rdy))):
                    if ft >= 2:
                        pe.wait_ge(taken, count(n, k, FT, ft - 1))
                    for kc in range(KC):
                        for i, (w, x) in enumerate(TERMS):
                            last = nc.tensor.matmul(ps[ft % 2][:, :], wt[k][:, w, m, kc * F + ft * P:kc * F + (ft + 1) * P],
                                                    xgT[k][:, x, kc, :], start=(kc == 0 and i == 0), stop=(kc == KC - 1 and i == len(TERMS) - 1))
                    last.then_inc(done, 1)

            def down(n, k, f, fts):
                for ft in fts:
                    if f == 0:
                        pe.wait_ge(h_low, count(n, k, FT, ft + 1 + FREE))
                    for i, (w, x) in enumerate(TERMS):
                        last = nc.tensor.matmul(ops[:, f, :], hid[:, x, ft, f * P:(f + 1) * P], wt[k][:, w, 2, ft * D:(ft + 1) * D],
                                                start=(ft == 0 and i == 0), stop=(ft == FT - 1 and i == len(TERMS) - 1))
                return last

            def step(n, k, following):
                more = (lambda *groups: transposes(*following, groups)) if following else (lambda *groups: None)
                pe.wait_ge(tr_low, count(n, k, NG, NG))
                for ft in range(FT):
                    up_gate(n, k, ft)
                    more(ft)
                more(8, 9)
                down(n, k, 0, range(0, 4))
                more(10, 11)
                down(n, k, 0, range(4, FT))
                more(12)
                down(n, k, 1, range(FT)).then_inc(o_done, 1)

            pe.wait_ge(b_Te, 1)
            pe.sem_inc(tr_done, WG)
            transposes(0, 0, [WG])
            experts(pe, step)

        @block.scalar
        def _(act):
            def take(n, k, q):
                act.wait_ge(tr_done, count(n, k, NG, q + 1))
                nc.scalar.activation(target(q, k, 0), tr[q % 3][:, :], ACT.Copy).then_inc(tr_high, 1)

            def silu(n, k, ft):
                act.wait_ge(g_done, count(n, k, FT, ft + 1))
                if ft >= 2:
                    act.wait_ge(h_rdy, count(n, k, FT, ft - 1))
                e = n * 2 + k
                col = bass.ds(e * FT + ft, 1) if not isinstance(e, int) else slice(e * FT + ft, e * FT + ft + 1)
                nc.scalar.activation(sil[:, ft % 2, :], gps[ft % 2][:, :], ACT.Silu, bias=bT[:, 1, col]).then_inc(s_rdy, 1)

            def step(n, k, following):
                for ft in range(FT):
                    silu(n, k, ft)
                    if following:
                        take(*following, ft)
                if following:
                    for q in range(FT, NG):
                        take(*following, q)

            act.wait_ge(b_T, 1)
            nc.scalar.activation(bT[:, :, :].rearrange("p a b -> p (a b)"), ops[:, 0, :], ACT.Copy).then_inc(b_Te, 1)
            act.wait_ge(b_Te, 1)
            act.sem_inc(tr_high, WG)
            take(0, 0, WG)
            experts(act, step)

        @block.vector
        def _(dve):
            def take(n, k, q):
                dve.wait_ge(tr_high, count(n, k, NG, q + 1))
                nc.vector.tensor_tensor(out=target(q, k, 1), in0=tr[q % 3][:, :], in1=target(q, k, 0).bitcast(F32), op=ALU.subtract)\
                    .then_inc(tr_low, 1)

            def hidden(n, k, ft):
                dve.wait_ge(s_rdy, count(n, k, FT, ft + 1))
                dve.wait_ge(u_done, count(n, k, FT, ft + 1))
                dve.wait_ge(h_low, count(n, k, FT, ft + 1))
                e = n * 2 + k
                col = bass.ds(e * FT + ft, 1) if not isinstance(e, int) else slice(e * FT + ft, e * FT + ft + 1)
                nc.vector.scalar_tensor_tensor(out=hidden_full[:, ft % FREE, :], in0=ups[ft % 2][:, :], scalar=bT[:, 0, col], in1=sil[:, ft % 2, :],
                                               op0=ALU.add, op1=ALU.mult).then_inc(h_rdy, 1)

            def high(n, k, ft):
                dve.wait_ge(h_rdy, count(n, k, FT, ft + 1))
                nc.vector.tensor_copy(hid[:, 0, ft, :], hidden_full[:, ft % FREE, :]).then_inc(h_high, 1)

            def output(n, k):
                dve.wait_ge(o_done, count(n, k, 1, 1))
                dve.wait_ge(so_free[k], n + 1)
                dve.wait_ge(db_in[k], n * 16 + 16)
                for f in range(2):
                    nc.vector.tensor_tensor(out=tmp[:, f, :], in0=ops[:, f, :], in1=db[k][:, :], op=ALU.add).then_inc(t_rdy, 1)
                dve.wait_ge(t_rdy, count(n, k, 2, 2))
                e = n * 2 + k
                col = bass.ds(e + D, 1) if not isinstance(e, int) else slice(e + D, e + D + 1)
                for f in range(2):
                    nc.vector.tensor_scalar(out=so[:, k, f, :], in0=tmp[:, f, :], scalar1=xg[k][:, f, col], scalar2=h["tg"][:, 1:2],
                                            op0=ALU.mult, op1=ALU.mult)\
                        .then_inc(o_rdy, 1)
                dve.wait_ge(o_rdy, count(n, k, 2, 2))
                nc.vector.tensor_copy(tmp[:, 0, 0:1], tmp[:, 1, 0:1]).then_inc(ou[k], 1)

            def step(n, k, following):
                for ft in range(FT):
                    hidden(n, k, ft)
                    if following:
                        take(*following, ft)
                    high(n, k, ft)
                if following:
                    for q in range(FT, NG):
                        take(*following, q)
                output(n, k)

            dve.sem_inc(tr_low, WG)
            take(0, 0, WG)
            experts(dve, step)


def build(nc, x, ctx_rows, g_xattn, g_ffn, gate_w, up_w, up_b, gw, gb, down_w, down_b, sh_gate_w, sh_up_w, sh_down_w, out):
    dram = lambda name, shape, dt=F32: nc.dram_tensor(name, shape, dt, kind="Internal").ap()
    h = dict(x=x, ctx=ctx_rows, g_xattn=g_xattn, g_ffn=g_ffn, gate_w=gate_w, up_w=up_w, up_b=up_b, gw=gw, gb=gb, down_w=down_w,
             down_b=down_b, sh_gate_w=sh_gate_w, sh_up_w=sh_up_w, sh_down_w=sh_down_w, out=out)
    h["dd"] = dram("distances", (P, DROWS, CELL))
    h["spans"] = dram("spans", (2, P, W), F16)
    h["hx"] = dram("token_rows", (NTOK, HROW))
    ctx = ExitStack()
    with ctx:
        sb = lambda name, shape, dt=F32: ctx.enter_context(nc.sbuf_tensor(name, shape, dt))
        h["X"] = sb("X", [P, NT, D])
        h["ident"] = sb("ident", [P, P])
        h["block_id"] = sb("block_id", [P, 1])
        h["not_first"] = sb("not_first", [P, 1])
        h["first_block"] = sb("first_block", [P, 1])
        h["last_block"] = sb("last_block", [P, 1])
        h["tg"] = sb("tg", [P, 2])
        h["bnst"] = sb("bnstX", [P, NT, 6])
        h["ids"] = sb("ids", [P, 2 * E_], I32)
        right = lambda stack, name, shape, dt=F32: stack.enter_context(nc.sbuf_tensor(name, shape, dt, side="right"))
        left = lambda stack, name, shape: stack.enter_context(nc.sbuf_tensor(name, shape, F32, side="left"))
        h["xg0"], h["bn"] = sb("xg0", [P, 2, HROW]), sb("bn", [P, 2, P])
        with ExitStack() as shared:
            with ExitStack() as attend:
                h["C"] = left(attend, "C", [P, NT, D])
                with ExitStack() as walk:
                    h["dleave"] = left(walk, "dleave", [P, W, RING + STEPS])
                    h["dexit"] = left(walk, "dexit", [P, RING + STEPS])
                    h["steps"] = left(walk, "steps", [P, STEPS])
                    with ExitStack() as distances:
                        for name in ("CT", "XT"):
                            h[name] = right(distances, name, [P, KC, B, S])
                        for name in ("d2", "root", "half_inv"):
                            h[name] = right(distances, name, [P, B, S])[:, :, :]
                        h["laid"] = right(distances, "laid", [P, P, CELL])[:, :, :]
                        h["residual"] = right(distances, "residual", [P, S])[:, :]
                        h["bbrow"], h["ones_row"] = right(distances, "bbrow", [1, B, S]), right(distances, "ones_row", [P, P])
                        h["aa"], h["lnhalf"], h["tiny"] = (right(distances, name, [P, n]) for name, n in (("aa", NT), ("lnhalf", 1), ("tiny", 1)))
                        h["rows"], h["upper"] = left(distances, "rows", [P, RING + 1, CELL]), left(distances, "upper", [P, RING, CELL])
                        h["exit"] = left(distances, "exit", [P, W, RING + 1])
                        h["when"], h["when0"] = (left(distances, name, [P, 2, STEPS]) for name in ("when", "when0"))
                        for name, shape in ("points", [P, W, 2, RING]), ("column", [P, W, 2, RING]), ("leave", [P, W, RING + 1]):
                            h[name] = [left(distances, f"{name}{i}", shape) for i in range(2)]
                        prepare_distances(nc, h)
                        accumulate_costs(nc, h)
                    h["wt0"] = right(ctx, "wt0", [P, 2, 3, KC * F], F32R)
                    h["wn1"] = right(ctx, "wn1", [P, WSIZE])
                    h["swn"] = h["wn1"][:, NT * D:].rearrange("p (v t d) -> p v t d", v=2, d=D)
                    h["sdn"], h["gw_rows"] = right(shared, "sdn", [P, KC, SH]), right(shared, "gw_rows", [E_, D])
                    h["C_parts"] = right(attend, "C_parts", [P, 2, NT, D], F32R)
                    trace_path(nc, h)
                align(nc, h)
            route(nc, h)
        run_experts(nc, h)


_INS = ['x', 'ctx_1024', 'g_xattn', 'g_ffn', 'L0_ffn_gate_w', 'L0_ffn_up_w', 'L0_ffn_up_b', 'L0_ffn_gw', 'L0_ffn_gb',
        'L0_ffn_down_w', 'L0_ffn_down_b', 'L0_ffn_sh_gate_w', 'L0_ffn_sh_up_w', 'L0_ffn_sh_down_w']
_OUT = (B, S, D)


def kernel(**inputs):
    import numpy as np
    import concourse.bacc as bacc
    from concourse.bass_utils import run_bass_kernel_spmd

    nc = bacc.Bacc("TRN2", target_bir_lowering=False, num_devices=1)
    arrays, args = {}, []
    for name in _INS:
        a = np.ascontiguousarray(inputs[name])
        arrays[f"in_{name}"] = a
        args.append(nc.dram_tensor(f"in_{name}", a.shape, mybir.dt.from_np(a.dtype), kind="ExternalInput").ap())
    args.append(nc.dram_tensor("out_x", _OUT, F32, kind="ExternalOutput").ap())
    build(nc, *args)
    r = run_bass_kernel_spmd(nc, [arrays], core_ids=[0])
    return r.results[0]["out_x"]
```
